# Optimizing a Trainium2 kernel written in Bass

```python
import numpy as np
import jax
import jax.numpy as jnp

def _softmax(x, axis=-1):
    return jax.nn.softmax(x, axis=axis)

def _gelu(x):
    return jax.nn.gelu(x, approximate=True)

def _silu(x):
    return jax.nn.silu(x)

def _sigmoid(x):
    return jax.nn.sigmoid(x)

def _layernorm(x, axis=-1, eps=1e-05):
    m = jnp.mean(x, axis=axis, keepdims=True)
    v = jnp.var(x, axis=axis, keepdims=True)
    return (x - m) / jnp.sqrt(v + eps)

def _scatter_add(tgt, idx, src, axis=0):
    return tgt.at[idx].add(src)

def _segment_sum(src, seg, n):
    return jax.ops.segment_sum(src, seg, n)
kernel_name = 'mk_gnn_preln_d4_gnn_r32_fce5d5'

def setup_inputs(seed: int=0):
    np.random.seed(seed)
    _w = jnp.asarray

    def _rec_inputs():
        import jax
        import jax.numpy as jnp
        _gk = jax.random.key(seed)
        x = -0.000202 + 1 * jax.random.normal(jax.random.fold_in(_gk, 1), (3125, 64), jnp.float32)
        _s = jax.random.randint(jax.random.fold_in(_gk, 2), (50000,), 0, 3125, jnp.int32)
        _d = jax.random.randint(jax.random.fold_in(_gk, 3), (50000,), 0, 3125, jnp.int32)
        _loop = jnp.arange(3125, dtype=jnp.int32)
        src = jnp.concatenate([_s, _d, _loop])
        dst = jnp.concatenate([_d, _s, _loop])
        _o = jnp.argsort(dst, stable=True)
        src = src[_o]
        dst = dst[_o]
        edge_attr_64 = 7.68618e-05 + 1.00005 * jax.random.normal(jax.random.fold_in(_gk, 11), (103125, 64), jnp.float32)
        edge_weight = 9.9816e-05 + 0.999782 * jax.random.normal(jax.random.fold_in(_gk, 13), (103125,), jnp.float32)
        return (x, src, dst, edge_attr_64, edge_weight)
    x, src, dst, edge_attr_64, edge_weight = _rec_inputs()

    def _L0_gnn_setup():
        import jax, jax.numpy as jnp
        import numpy as np
        N = 3125
        E = 31250
        D_IN = 64
        H1, C1 = (12, 12)
        H2, C2 = (1, 64)
        NEG_SLOPE = 0.2
        ALPHA = 0.5

        def _add_self_loops(src, dst):
            loop = jnp.arange(N, dtype=src.dtype)
            return (jnp.concatenate([src, loop]), jnp.concatenate([dst, loop]))

        def _ssg_conv(x, src, dst, W, b):
            s, d = _add_self_loops(src, dst)
            deg = jax.ops.segment_sum(jnp.ones_like(s, dtype=x.dtype), d, num_segments=N)
            dinv = jnp.where(deg > 0, jax.lax.rsqrt(deg), 0.0)
            norm = dinv[s] * dinv[d]
            agg = jax.ops.segment_sum(x[s] * norm[:, None], d, num_segments=N)
            h = ALPHA * x + (1.0 - ALPHA) * agg
            return h @ W + b

        def _gatv2_conv(x, src, dst, Wl, bl, Wr, br, att, bias, Hh, Cc):
            s, d = _add_self_loops(src, dst)
            xl = (x @ Wl + bl).reshape(N, Hh, Cc)
            xr = (x @ Wr + br).reshape(N, Hh, Cc)
            e = jax.nn.leaky_relu(xl[s] + xr[d], NEG_SLOPE)
            logits = jnp.einsum('ehc,hc->eh', e, att)
            m = jax.ops.segment_max(logits, d, num_segments=N)
            a = jnp.exp(logits - m[d])
            denom = jax.ops.segment_sum(a, d, num_segments=N)
            a = a / (denom[d] + 1e-16)
            out = jax.ops.segment_sum(xl[s] * a[:, :, None], d, num_segments=N)
            return out.reshape(N, Hh * Cc) + bias
        key = jax.random.key(seed)
        ks = jax.random.split(key, 16)
        features = jax.random.normal(ks[0], (N, D_IN), dtype=jnp.float32)
        src = jax.random.randint(ks[1], (E,), 0, N)
        off = jax.random.randint(ks[2], (E,), 1, N)
        dst = (src + off) % N
        edge_index = jnp.stack([src, dst]).astype(jnp.int64)
        g = lambda k, shape, fan: jax.random.normal(k, shape, jnp.float32) * (1.0 / np.sqrt(fan))
        params = dict(W_ssg=g(ks[3], (D_IN, D_IN), D_IN), b_ssg=jnp.zeros((D_IN,), jnp.float32), W1l=g(ks[4], (D_IN, H1 * C1), D_IN), b1l=jnp.zeros((H1 * C1,), jnp.float32), W1r=g(ks[5], (D_IN, H1 * C1), D_IN), b1r=jnp.zeros((H1 * C1,), jnp.float32), att1=g(ks[6], (H1, C1), C1), bias1=jnp.zeros((H1 * C1,), jnp.float32), W2l=g(ks[7], (H1 * C1, H2 * C2), H1 * C1), b2l=jnp.zeros((H2 * C2,), jnp.float32), W2r=g(ks[8], (H1 * C1, H2 * C2), H1 * C1), b2r=jnp.zeros((H2 * C2,), jnp.float32), att2=g(ks[9], (H2, C2), C2), bias2=jnp.zeros((H2 * C2,), jnp.float32))
        return dict(features=features, edge_index=edge_index, **params)
    _L0_gnn_all = _L0_gnn_setup()
    _L0_gnn_in = {k: v for k, v in _L0_gnn_all.items() if k in ('W_ssg', 'b_ssg', 'W1l', 'b1l', 'W1r', 'b1r', 'att1', 'bias1', 'W2l', 'b2l', 'W2r', 'b2r', 'att2', 'bias2')}
    del _L0_gnn_all

    def _L1_gnn_setup():
        import jax, jax.numpy as jnp
        import numpy as np
        N = 3125
        E = 50000
        D = 64

        def _gcn_conv(x, W, b, src, dst, deg_inv_sqrt, n):
            h = x @ W
            norm = deg_inv_sqrt[src] * deg_inv_sqrt[dst]
            msg = h[src] * norm[:, None]
            out = jax.ops.segment_sum(msg, dst, num_segments=n)
            return out + b
        key = jax.random.key(seed)
        ks = jax.random.split(key, 6)
        x = jax.random.normal(ks[0], (N, D), dtype=jnp.float32)
        edge_index = jax.random.randint(ks[1], (2, E), 0, N, dtype=jnp.int64)
        scale = 1.0 / np.sqrt(D)
        W1 = jax.random.normal(ks[2], (D, D), dtype=jnp.float32) * scale
        W2 = jax.random.normal(ks[3], (D, D), dtype=jnp.float32) * scale
        W3 = jax.random.normal(ks[4], (D, D), dtype=jnp.float32) * scale
        b1 = jnp.zeros((D,), jnp.float32)
        b2 = jnp.zeros((D,), jnp.float32)
        b3 = jnp.zeros((D,), jnp.float32)
        return {'x': x, 'edge_index': edge_index, 'W1': W1, 'b1': b1, 'W2': W2, 'b2': b2, 'W3': W3, 'b3': b3}
    _L1_gnn_all = _L1_gnn_setup()
    _L1_gnn_in = {k: v for k, v in _L1_gnn_all.items() if k in ('W1', 'b1', 'W2', 'b2', 'W3', 'b3')}
    del _L1_gnn_all

    def _L2_gnn_setup():
        import jax, jax.numpy as jnp
        import numpy as np
        N_NODES = 3125
        N_EDGES = 1250000
        D_FEAT = 64

        def _segment_softmax(vals, idx, num_segments):
            seg_max = jax.ops.segment_max(vals, idx, num_segments=num_segments)
            e = jnp.exp(vals - seg_max[idx])
            seg_sum = jax.ops.segment_sum(e, idx, num_segments=num_segments)
            return e / seg_sum[idx]
        key = jax.random.key(seed)
        k1, k2, k3 = jax.random.split(key, 3)
        x = jax.random.normal(k1, (N_NODES, D_FEAT), dtype=jnp.float32)
        edge_index = jax.random.randint(k2, (2, N_EDGES), 0, N_NODES, dtype=jnp.int32)
        edge_attrs = jax.random.normal(k3, (N_EDGES,), dtype=jnp.float32)
        return {'x': x, 'edge_index': edge_index, 'edge_attrs': edge_attrs}
    _L2_gnn_all = _L2_gnn_setup()
    _L2_gnn_in = {k: v for k, v in _L2_gnn_all.items() if k in ()}
    del _L2_gnn_all

    def _L3_gnn_setup():
        import jax, jax.numpy as jnp
        import numpy as np
        N_NODES = 3125
        N_EDGES = 31250
        D_IN = 64
        D_OUT = 64
        key = jax.random.key(seed)
        k_x, k_ei, k_ea, k_w, k_b = jax.random.split(key, 5)
        x = jax.random.normal(k_x, (N_NODES, D_IN), dtype=jnp.float32)
        edge_index = jax.random.randint(k_ei, (2, N_EDGES), 0, N_NODES, dtype=jnp.int64)
        edge_attr = jax.random.normal(k_ea, (N_EDGES, D_IN), dtype=jnp.float32)
        bound = 1.0 / np.sqrt(D_IN)
        W = jax.random.uniform(k_w, (D_OUT, D_IN), dtype=jnp.float32, minval=-bound, maxval=bound)
        b = jax.random.uniform(k_b, (D_OUT,), dtype=jnp.float32, minval=-bound, maxval=bound)
        eps = jnp.zeros((), dtype=jnp.float32)
        return {'x': x, 'edge_index': edge_index, 'edge_attr': edge_attr, 'W': W, 'b': b, 'eps': eps}
    _L3_gnn_all = _L3_gnn_setup()
    _L3_gnn_in = {k: v for k, v in _L3_gnn_all.items() if k in ('W', 'b', 'eps')}
    del _L3_gnn_all
    return {'x': x, 'src': src, 'dst': dst, 'edge_attr_64': edge_attr_64, 'edge_weight': edge_weight, 'L0_gnn_W_ssg': _L0_gnn_in['W_ssg'], 'L0_gnn_b_ssg': _L0_gnn_in['b_ssg'], 'L0_gnn_W1l': _L0_gnn_in['W1l'], 'L0_gnn_b1l': _L0_gnn_in['b1l'], 'L0_gnn_W1r': _L0_gnn_in['W1r'], 'L0_gnn_b1r': _L0_gnn_in['b1r'], 'L0_gnn_att1': _L0_gnn_in['att1'], 'L0_gnn_bias1': _L0_gnn_in['bias1'], 'L0_gnn_W2l': _L0_gnn_in['W2l'], 'L0_gnn_b2l': _L0_gnn_in['b2l'], 'L0_gnn_W2r': _L0_gnn_in['W2r'], 'L0_gnn_b2r': _L0_gnn_in['b2r'], 'L0_gnn_att2': _L0_gnn_in['att2'], 'L0_gnn_bias2': _L0_gnn_in['bias2'], 'L1_gnn_W1': _L1_gnn_in['W1'], 'L1_gnn_b1': _L1_gnn_in['b1'], 'L1_gnn_W2': _L1_gnn_in['W2'], 'L1_gnn_b2': _L1_gnn_in['b2'], 'L1_gnn_W3': _L1_gnn_in['W3'], 'L1_gnn_b3': _L1_gnn_in['b3'], 'L3_gnn_W': _L3_gnn_in['W'], 'L3_gnn_b': _L3_gnn_in['b'], 'L3_gnn_eps': _L3_gnn_in['eps']}

def reference(x, src, dst, edge_attr_64, edge_weight, L0_gnn_W_ssg, L0_gnn_b_ssg, L0_gnn_W1l, L0_gnn_b1l, L0_gnn_W1r, L0_gnn_b1r, L0_gnn_att1, L0_gnn_bias1, L0_gnn_W2l, L0_gnn_b2l, L0_gnn_W2r, L0_gnn_b2r, L0_gnn_att2, L0_gnn_bias2, L1_gnn_W1, L1_gnn_b1, L1_gnn_W2, L1_gnn_b2, L1_gnn_W3, L1_gnn_b3, L3_gnn_W, L3_gnn_b, L3_gnn_eps):
    import jax
    import jax.numpy as jnp

    def _L0_gnn_ref(features, edge_index, W_ssg, b_ssg, W1l, b1l, W1r, b1r, att1, bias1, W2l, b2l, W2r, b2r, att2, bias2):
        import jax, jax.numpy as jnp
        import numpy as np
        N = 3125
        E = 31250
        D_IN = 64
        H1, C1 = (12, 12)
        H2, C2 = (1, 64)
        NEG_SLOPE = 0.2
        ALPHA = 0.5

        def _add_self_loops(src, dst):
            loop = jnp.arange(N, dtype=src.dtype)
            return (jnp.concatenate([src, loop]), jnp.concatenate([dst, loop]))

        def _ssg_conv(x, src, dst, W, b):
            s, d = _add_self_loops(src, dst)
            deg = jax.ops.segment_sum(jnp.ones_like(s, dtype=x.dtype), d, num_segments=N)
            dinv = jnp.where(deg > 0, jax.lax.rsqrt(deg), 0.0)
            norm = dinv[s] * dinv[d]
            agg = jax.ops.segment_sum(x[s] * norm[:, None], d, num_segments=N)
            h = ALPHA * x + (1.0 - ALPHA) * agg
            return h @ W + b

        def _gatv2_conv(x, src, dst, Wl, bl, Wr, br, att, bias, Hh, Cc):
            s, d = _add_self_loops(src, dst)
            xl = (x @ Wl + bl).reshape(N, Hh, Cc)
            xr = (x @ Wr + br).reshape(N, Hh, Cc)
            e = jax.nn.leaky_relu(xl[s] + xr[d], NEG_SLOPE)
            logits = jnp.einsum('ehc,hc->eh', e, att)
            m = jax.ops.segment_max(logits, d, num_segments=N)
            a = jnp.exp(logits - m[d])
            denom = jax.ops.segment_sum(a, d, num_segments=N)
            a = a / (denom[d] + 1e-16)
            out = jax.ops.segment_sum(xl[s] * a[:, :, None], d, num_segments=N)
            return out.reshape(N, Hh * Cc) + bias
        src, dst = (edge_index[0], edge_index[1])
        x = _ssg_conv(features, src, dst, W_ssg, b_ssg)
        x = _gatv2_conv(x, src, dst, W1l, b1l, W1r, b1r, att1, bias1, H1, C1)
        x = _gatv2_conv(x, src, dst, W2l, b2l, W2r, b2r, att2, bias2, H2, C2)
        return x

    def _L1_gnn_ref(x, edge_index, W1, b1, W2, b2, W3, b3):
        import jax, jax.numpy as jnp
        import numpy as np
        N = 3125
        E = 50000
        D = 64

        def _gcn_conv(x, W, b, src, dst, deg_inv_sqrt, n):
            h = x @ W
            norm = deg_inv_sqrt[src] * deg_inv_sqrt[dst]
            msg = h[src] * norm[:, None]
            out = jax.ops.segment_sum(msg, dst, num_segments=n)
            return out + b
        n = x.shape[0]
        loops = jnp.arange(n, dtype=edge_index.dtype)
        src = jnp.concatenate([edge_index[0], loops])
        dst = jnp.concatenate([edge_index[1], loops])
        deg = jax.ops.segment_sum(jnp.ones(src.shape[0], x.dtype), dst, num_segments=n)
        deg_inv_sqrt = jnp.where(deg > 0, jax.lax.rsqrt(jnp.maximum(deg, 1.0)), 0.0)
        h = jax.nn.relu(_gcn_conv(x, W1, b1, src, dst, deg_inv_sqrt, n))
        h = jax.nn.relu(_gcn_conv(h, W2, b2, src, dst, deg_inv_sqrt, n))
        h = _gcn_conv(h, W3, b3, src, dst, deg_inv_sqrt, n)
        return h

    def _L2_gnn_ref(x, edge_index, edge_attrs):
        import jax, jax.numpy as jnp
        import numpy as np
        N_NODES = 3125
        N_EDGES = 1250000
        D_FEAT = 64

        def _segment_softmax(vals, idx, num_segments):
            seg_max = jax.ops.segment_max(vals, idx, num_segments=num_segments)
            e = jnp.exp(vals - seg_max[idx])
            seg_sum = jax.ops.segment_sum(e, idx, num_segments=num_segments)
            return e / seg_sum[idx]
        n = x.shape[0]
        from_, to_ = (edge_index[0], edge_index[1])
        incoming_norm = _segment_softmax(edge_attrs, to_, n)
        outgoing_norm = _segment_softmax(edge_attrs, from_, n)
        norm = jnp.sqrt(incoming_norm * outgoing_norm)
        messages = norm[:, None] * x[from_]
        return jax.ops.segment_sum(messages, to_, num_segments=n)

    def _L3_gnn_ref(x, edge_index, edge_attr, W, b, eps):
        import jax, jax.numpy as jnp
        import numpy as np
        N_NODES = 3125
        N_EDGES = 31250
        D_IN = 64
        D_OUT = 64
        src = edge_index[0]
        dst = edge_index[1]
        msg = jax.nn.relu(x[src] + edge_attr)
        agg = jax.ops.segment_sum(msg, dst, num_segments=x.shape[0])
        h = (1.0 + eps) * x + agg
        out = h @ W.T + b
        return jax.nn.relu(out)
    edge_index = jnp.stack([src, dst])
    h = jnp.maximum(_layernorm(x, axis=-1), 0.0)
    x = x + _L0_gnn_ref(h, edge_index, L0_gnn_W_ssg, L0_gnn_b_ssg, L0_gnn_W1l, L0_gnn_b1l, L0_gnn_W1r, L0_gnn_b1r, L0_gnn_att1, L0_gnn_bias1, L0_gnn_W2l, L0_gnn_b2l, L0_gnn_W2r, L0_gnn_b2r, L0_gnn_att2, L0_gnn_bias2)
    h = jnp.maximum(_layernorm(x, axis=-1), 0.0)
    x = x + _L1_gnn_ref(h, edge_index, L1_gnn_W1, L1_gnn_b1, L1_gnn_W2, L1_gnn_b2, L1_gnn_W3, L1_gnn_b3)
    h = jnp.maximum(_layernorm(x, axis=-1), 0.0)
    x = x + _L2_gnn_ref(h, edge_index, edge_weight)
    h = jnp.maximum(_layernorm(x, axis=-1), 0.0)
    x = x + _L3_gnn_ref(h, edge_index, edge_attr_64, L3_gnn_W, L3_gnn_b, L3_gnn_eps)
    return x

_drawn_inputs = setup_inputs


def setup_inputs(seed=0):
    import zlib

    import numpy as np

    out = dict(_drawn_inputs(seed))
    spreads = {'L0_gnn_b_ssg': (0.0, 0.1),
     'L0_gnn_b1l': (0.0, 0.1),
     'L0_gnn_b1r': (0.0, 2.0),
     'L0_gnn_bias1': (0.0, 0.1),
     'L0_gnn_b2l': (0.0, 0.1),
     'L0_gnn_b2r': (0.0, 2.0),
     'L0_gnn_bias2': (0.0, 0.1),
     'L1_gnn_b1': (0.0, 0.282),
     'L1_gnn_b2': (0.0, 0.1),
     'L1_gnn_b3': (0.0, 0.1)}
    factors = {'edge_weight': 2.845,
     'L0_gnn_W1r': 8.0,
     'L0_gnn_att1': 3.25,
     'L0_gnn_W2r': 64.0,
     'L0_gnn_att2': 64.0,
     'L3_gnn_b': 8.0}
    for name, (base, spread) in spreads.items():
        noise = np.random.default_rng([zlib.crc32(name.encode()), seed]).standard_normal(out[name].shape)
        drawn = base * np.exp(spread * noise) if base else spread * noise
        out[name] = jnp.asarray(drawn.astype(out[name].dtype))
    for name, factor in factors.items():
        out[name] = (out[name] * factor).astype(out[name].dtype)
    return out
```

```python
import math
from contextlib import ExitStack

import concourse.bass as bass
from concourse import mybir

F32 = mybir.dt.float32
BF16 = mybir.dt.bfloat16
I32 = mybir.dt.int32
ALU = mybir.AluOpType
ACT = mybir.ActivationFunctionType
AX = mybir.AxisListType

P = 128
N = 3125
E = 103125
D = 64
H1, C1 = 12, 12
HC = H1 * C1
T = -(-N // P)
NP = T * P
EC = -(-E // P)
EP = EC * P
ER = EP + P
NO_NODE = 4095
S = 32
B = 8
SB = S // B
U = E // S + T + E // (P * S) + 4
OFF = NP * NP
BIG = 1.0e30
HG = 13
KEY_DEG = 4000


class Steps:

    def __init__(self, eng, sem, base=0):
        self.eng, self.sem, self.base, self.n = eng, sem, base, 0

    def mark(self, ins):
        ins.then_inc(self.sem, 1)
        self.n += 1

    def wait(self):
        self.eng.wait_ge(self.sem, self.base + self.n)

    def after(self, ins):
        self.mark(ins)
        self.wait()


def wait_count(eng, sem, count, turns):
    eng.wait_ge(sem, count)
    eng.sem_inc(turns, 1)


def free_bcast(ap, before, after):
    a = ap
    if before:
        a = a.unsqueeze(1)
        a = a.to_broadcast([a.shape[0], before] + list(a.shape[2:]))
    if after:
        a = a.unsqueeze(len(a.shape))
        a = a.to_broadcast(list(a.shape[:-1]) + [after])
    return a


class Scope:

    def __init__(self, nc, ctx):
        self.nc, self.ctx, self.id = nc, ctx, nc.next_id()
        self.sems = []
        ctx.callback(self.release)

    def release(self):
        if self.sems:
            self.nc.clear_and_free_semaphores(self.sems)
            self.nc.all_engine_barrier()

    def sb(self, name, shape, dt=F32):
        return self.ctx.enter_context(self.nc.sbuf_tensor(f"{name}_{self.id}", list(shape), dt))

    def sem(self, name):
        self.sems.append(self.nc.alloc_semaphore(f"{name}_{self.id}"))
        return self.sems[-1]

    def dram(self, name, shape, dt=F32):
        return self.nc.dram_tensor(name, list(shape), dt, kind="Internal").ap()


def bank(g, i):
    return g["banks"][:, i, :]


def persistent(nc, ctx, io):
    s = Scope(nc, ctx)
    g = dict(io)
    g["banks"] = ctx.enter_context(nc.psum_tensor("banks", [P, 8, 512], F32))
    g["X"] = s.sb("X", [P, T, D])
    g["iota_f"] = s.sb("iota_f", [P, P])
    g["iota_b"] = s.sb("iota_b", [P, P], BF16)
    g["pcol"] = s.sb("pcol", [P, 1])
    g["ident"] = s.sb("ident", [P, P])
    g["ident_b"] = s.sb("ident_b", [P, P], BF16)
    g["ones"] = s.sb("ones", [P, P])
    g["deg"] = s.sb("deg", [P, T])
    g["ni"] = s.sb("ni", [P, T, 4])
    g["nid_i"] = s.sb("nid_i", [P, T], I32)
    g["info"] = s.sb("info", [1, 5, T], I32)
    g["PAIR"] = s.dram("PAIR", [NP * NP, 2])
    g["MS"] = s.dram("MS", [NP, 2])
    g["NI"] = s.dram("NI", [NP, 4])
    g["SLOT"] = s.dram("SLOT", [P, (U + T) * 3 * S])
    g["GIDX"] = s.dram("GIDX", [P, (U + T) * S], I32)
    g["H"] = s.sb("H", [P, T, D])
    g["dinv"] = s.sb("dinv", [P, T])
    g["mout"] = s.sb("mout", [P, T])
    g["rank_i"] = s.sb("rank_i", [P, T], I32)
    g["sout"] = s.sb("sout", [P, T])
    g["cmax"] = s.sb("cmax_all", [P, 1])
    g["pool_turns"] = s.sem("pool_turns")
    g["pe_turns"] = s.sem("pe_turns")
    g["v_turns"] = s.sem("v_turns")
    g["sp_turns"] = s.sem("sp_turns")
    g["pair_fill"] = s.sem("pair_fill")
    return g


def prepare(nc, g):
    with ExitStack() as ctx:
        s = Scope(nc, ctx)
        fill = s.sb("fill", [P, NP, 2])
        dst_i = s.sb("dst_i", [P, EC], I32)
        part_i = s.sb("part_i", [P, 2, EC], I32)
        lo_b = s.sb("lo_b", [P, EC], BF16)
        hi_b = s.sb("hi_b", [P, EC], BF16)
        oh_lo = s.sb("oh_lo", [P, 2, HG, P], BF16)
        oh_hi = s.sb("oh_hi", [P, 2, HG, T], BF16)
        zero_b = s.sb("zero_b", [P, P], BF16)
        iota_i = s.sb("iota_i", [P, P], I32)
        pcol_i = s.sb("pcol_i", [P, 1], I32)
        node_i = s.sb("node_i", [P, T], I32)
        tri = s.sb("tri", [P, P])
        key = s.sb("key", [P, T])
        keyrow = s.sb("keyrow", [P, NP])
        dump_v = s.sb("dump_v", [P, NP], BF16)
        dump_a = s.sb("dump_a", [P, NP], BF16)
        greater = s.sb("greater", [P, T])
        sign_sum = s.sb("sign_sum", [P, T])
        rank_i = g["rank_i"]
        niw = s.sb("niw", [P, T, 4])
        small = s.sb("small", [P, 4, T])
        degs_c = s.sb("degs_c", [P, T])
        kcol = s.sb("kcol", [T, 1])
        krow = s.sb("krow", [1, T])
        krow_i = s.sb("krow_i", [1, 2, T], I32)
        row_f = s.sb("row_f", [1, 4, T])
        hist = bank(g, 0)
        pref = bank(g, 1)[:, 0:2 * T].rearrange("p (a t) -> p a t", a=2)
        kps = g["banks"][:, 2:4, :]
        kt = bank(g, 4)[:, 0:P]

        in_dst, in_x = s.sem("in_dst"), s.sem("in_x")
        fill_set = s.sem("fill_set")
        iotas = s.sem("iotas")
        v_steps = s.sem("v_steps")
        onehots_ready = [s.sem(f"onehots_ready{i}") for i in range(2)]
        oh_free = [s.sem(f"oh_free{i}") for i in range(2)]
        hist_done = s.sem("hist_done")
        consts_ready = s.sem("consts_ready")
        deg_ready, pref_done = s.sem("deg_ready"), s.sem("pref_done")
        key_ready, key_turned, key_copied = s.sem("key_ready"), s.sem("key_turned"), s.sem("key_copied")
        signs_done = s.sem("signs_done")
        ranks_ready, ni_written, ni_read = s.sem("ranks_ready"), s.sem("ni_written"), s.sem("ni_read")
        k_ready, k_turned = s.sem("k_ready"), s.sem("k_turned")
        block = ctx.enter_context(nc.Block())
        half_v = T // 2

        @block.sync
        def _(sp):
            sp.dma_start(dst_i[:, :], g["dst"][0:EP].rearrange("(p c) -> p c", p=P)).then_inc(in_dst, 16)
            sp.dma_start(g["X"][:, :, :], g["x"].rearrange("(t p) f -> p t f", p=P)).then_inc(in_x, 16)
            sp.wait_ge(fill_set, 2)
            pair = g["PAIR"].rearrange("(t p d) c -> t p (d c)", t=T, p=P)
            for t in range(T):
                sp.dma_start(pair[t], fill[:, :, :].rearrange("p d c -> p (d c)"),
                             max_dma_last_dim=8192).then_inc(g["pair_fill"], 16)
            sp.wait_ge(ni_written, 16 * T)
            sp.dma_start(g["ni"][:, :, :], g["NI"].rearrange("(t p) c -> p t c", p=P)).then_inc(ni_read, 16)
            sp.wait_ge(in_x, 16)
            sp.wait_ge(g["pair_fill"], 16 * T)

        @block.gpsimd
        def _(pool):
            pool.iota(iota_i[:, :], [[1, P]], base=0, channel_multiplier=0).then_inc(iotas, 1)
            pool.iota(pcol_i[:, :], [[0, 1]], base=0, channel_multiplier=1).then_inc(iotas, 1)
            pool.iota(node_i[:, :], [[P, T]], base=0, channel_multiplier=1).then_inc(iotas, 1)
            pool.memset(fill[:, :, 0], 0.0).then_inc(fill_set, 1)
            pool.memset(fill[:, :, 1], -BIG).then_inc(fill_set, 1)
            pool.wait_ge(ranks_ready, 1)
            for t in range(T):
                pool.indirect_dma_start(g["NI"], bass.IndirectOffsetOnAxis(ap=rank_i[:, t:t + 1], axis=0),
                                        niw[:, t, :], None).then_inc(ni_written, 16)

        @block.tensor
        def _(pe):
            pe.wait_ge(consts_ready, 1)
            pe.matmul(hist[:, 0:T], zero_b[:, :], zero_b[:, 0:T], start=True, stop=False, skip_group_check=True)
            with pe.Fori(0, EC // (2 * HG)) as b:
                for i in range(2):
                    pe.wait_ge(onehots_ready[i], 2 * b + 2)
                    for c in range(HG):
                        mm = pe.matmul(hist[:, 0:T], oh_lo[:, i, c, :], oh_hi[:, i, c, :], start=False, stop=False,
                                       skip_group_check=True)
                    mm.then_inc(oh_free[i], 1)
            pe.matmul(hist[:, 0:T], zero_b[:, :], zero_b[:, 0:T], start=False, stop=True,
                      skip_group_check=True).then_inc(hist_done, 1)
            pe.wait_ge(deg_ready, 1)
            pe.matmul(pref[:, 0, :], tri[:, :], g["deg"][:, :], start=True, stop=True)
            pe.matmul(pref[:, 1, :], g["ones"][:, :], g["deg"][:, :], start=True, stop=True).then_inc(pref_done, 1)
            pe.wait_ge(key_ready, 1)
            for t in range(T):
                if t >= 8 and t % 4 == 0:
                    pe.wait_ge(key_copied, t // 4 - 1)
                mm = pe.transpose(kps[:, (t // 4) % 2, (t % 4) * P:(t % 4 + 1) * P],
                                  key[:, t:t + 1].to_broadcast([P, P]), g["ident"][:, :])
                if t % 4 == 3 or t == T - 1:
                    mm.then_inc(key_turned, 1)
            pe.wait_ge(k_ready, 1)
            pe.transpose(kt[0:T, :], degs_c[:, :], g["ident"][:, :]).then_inc(k_turned, 1)
            pe.wait_ge(k_ready, 2)
            pe.transpose(pref[0:1, 0, :], kcol[:, :], g["ident"][0:T, 0:T]).then_inc(k_turned, 1)

        @block.scalar
        def _(act):
            for j in range(-(-T // 4)):
                act.wait_ge(key_turned, j + 1)
                w = min(4, T - 4 * j) * P
                act.copy(keyrow[:, 4 * j * P:4 * j * P + w], kps[:, j % 2, 0:w]).then_inc(key_copied, 1)
            act.wait_ge(key_copied, -(-T // 4))
            for t in range(half_v, T):
                act.activation(dump_a[:, :], keyrow[:, :], ACT.Sign, bias=key[:, t:t + 1], scale=-1.0,
                               accum_out=sign_sum[:, t:t + 1]).then_inc(signs_done, 1)
                act.wait_ge(signs_done, t - half_v + 1)

        @block.vector
        def _(dve):
            st = Steps(dve, v_steps)
            dve.wait_ge(iotas, 3)
            st.mark(dve.memset(zero_b[:, :], 0.0))
            st.mark(dve.memset(g["ones"][:, :], 1.0))
            st.mark(dve.tensor_copy(g["iota_f"][:, :], iota_i[:, :]))
            st.mark(dve.tensor_copy(g["iota_b"][:, :], iota_i[:, :]))
            st.after(dve.tensor_copy(g["pcol"][:, :], pcol_i[:, :]))
            st.mark(dve.tensor_scalar(tri[:, :], g["iota_f"][:, :], g["pcol"][:, 0:1], None, ALU.is_gt))
            st.mark(dve.tensor_scalar(g["ident"][:, :], g["iota_f"][:, :], g["pcol"][:, 0:1], None, ALU.is_equal))
            st.after(dve.tensor_scalar(g["ident_b"][:, :], g["iota_f"][:, :], g["pcol"][:, 0:1], None, ALU.is_equal))
            dve.sem_inc(consts_ready, 1)
            dve.wait_ge(in_dst, 16)
            st.mark(dve.tensor_scalar(part_i[:, 0, :], dst_i[:, :], P - 1, None, ALU.bitwise_and))
            st.after(dve.tensor_scalar(part_i[:, 1, :], dst_i[:, :], int(math.log2(P)), None, ALU.logical_shift_right))
            st.mark(dve.tensor_copy(lo_b[:, :], part_i[:, 0, :]))
            st.after(dve.tensor_copy(hi_b[:, :], part_i[:, 1, :]))
            for i in range(2):
                dve.sem_inc(oh_free[i], 1)
            with dve.Fori(0, EC // (2 * HG)) as b:
                for i in range(2):
                    dve.wait_ge(oh_free[i], b + 1)
                    dve.tensor_tensor(oh_lo[:, i], free_bcast(lo_b[:, bass.ds(b * 2 * HG + i * HG, HG)], 0, P),
                                      free_bcast(g["iota_b"][:, :], HG, 0), ALU.is_equal).then_inc(onehots_ready[i], 1)
                    dve.tensor_tensor(oh_hi[:, i], free_bcast(hi_b[:, bass.ds(b * 2 * HG + i * HG, HG)], 0, T),
                                      free_bcast(g["iota_b"][:, 0:T], HG, 0), ALU.is_equal).then_inc(onehots_ready[i], 1)
            dve.wait_ge(hist_done, 1)
            st.mark(dve.tensor_copy(g["deg"][:, :], hist[:, 0:T]))
            st.after(dve.tensor_copy(small[:, 3, :], node_i[:, :]))
            dve.sem_inc(deg_ready, 1)
            st.mark(dve.tensor_scalar(key[:, :], g["deg"][:, :], float(KEY_DEG), 4096.0, ALU.min, ALU.mult))
            st.after(dve.tensor_scalar(small[:, 0, :], small[:, 3, :], -1.0, 4095.0, ALU.mult, ALU.add))
            st.after(dve.tensor_tensor(key[:, :], key[:, :], small[:, 0, :], ALU.add))
            dve.sem_inc(key_ready, 1)
            dve.wait_ge(pref_done, 1)
            st.mark(dve.tensor_copy(niw[:, :, 0], small[:, 3, :]))
            st.mark(dve.tensor_copy(niw[:, :, 2], g["deg"][:, :]))
            st.mark(dve.memset(niw[:, :, 3], 0.0))
            st.after(dve.tensor_copy(small[:, 1, :], pref[:, 1, :]))
            st.after(dve.tensor_tensor_scan(small[:, 2, :], g["ones"][:, 0:T], small[:, 1, :], 0.0, ALU.mult, ALU.add))
            st.after(dve.tensor_tensor(small[:, 2, :], small[:, 2, :], small[:, 1, :], ALU.subtract))
            st.after(dve.tensor_tensor(niw[:, :, 1], small[:, 2, :], pref[:, 0, :], ALU.add))
            dve.wait_ge(key_copied, -(-T // 4))
            for t in range(half_v):
                st.after(dve.tensor_scalar(dump_v[:, :], keyrow[:, :], key[:, t:t + 1], 0.0, ALU.is_gt, ALU.add,
                                           accum_out=greater[:, t:t + 1]))
            dve.wait_ge(signs_done, T - half_v)
            st.after(dve.tensor_scalar(greater[:, half_v:T], sign_sum[:, half_v:T], -0.5, 0.5 * (NP - 1),
                                       ALU.mult, ALU.add))
            st.after(dve.tensor_copy(rank_i[:, :], greater[:, :]))
            dve.sem_inc(ranks_ready, 1)
            dve.wait_ge(ni_read, 16)
            st.mark(dve.tensor_copy(g["nid_i"][:, :], g["ni"][:, :, 0]))
            st.after(dve.tensor_copy(degs_c[:, :], g["ni"][:, :, 2]))
            dve.sem_inc(k_ready, 1)
            dve.wait_ge(k_turned, 1)
            st.after(dve.tensor_reduce(kcol[:, :], kt[0:T, :], AX.X, ALU.max))
            dve.sem_inc(k_ready, 1)
            dve.wait_ge(k_turned, 2)
            st.after(dve.tensor_copy(krow[:, :], pref[0:1, 0, :]))
            for i, size in enumerate((B, S)):
                st.after(dve.tensor_scalar(row_f[:, i, :], krow[:, :], 1.0, float(size - 1), ALU.max, ALU.add))
                st.after(dve.tensor_copy(krow_i[:, i, :], row_f[:, i, :]))
                st.after(dve.tensor_scalar(g["info"][:, i, :], krow_i[:, i, :], int(math.log2(size)), None,
                                           ALU.logical_shift_right))
                st.after(dve.tensor_copy(row_f[:, i, :], g["info"][:, i, :]))
                st.after(dve.tensor_tensor_scan(row_f[:, 2 + i, :], g["ones"][0:1, 0:T], row_f[:, i, :], 0.0,
                                                ALU.mult, ALU.add))
                st.after(dve.tensor_tensor(row_f[:, 2 + i, :], row_f[:, 2 + i, :], row_f[:, i, :], ALU.subtract))
                st.after(dve.tensor_copy(g["info"][:, 2 + i, :], row_f[:, 2 + i, :]))
            st.after(dve.tensor_reduce(krow[:, 0:1], row_f[:, 1, :], AX.X, ALU.max))
            st.after(dve.memset(g["info"][:, 4, :], 0))
            st.after(dve.tensor_copy(g["info"][:, 4, 0:1], krow[:, 0:1]))


def fill_slots(nc, g):
    with ExitStack() as ctx:
        s = Scope(nc, ctx)
        start_f = s.sb("start_f", [P, T])
        rem = s.sb("rem", [P, T])
        start_i = s.sb("start_i", [P, T], I32)
        srun = s.sb("srun", [P, T, S], I32)
        wrun = s.sb("wrun", [P, T, S])
        slot = s.sb("slot", [P, T, 3, S])
        place = s.sb("place", [P, S])
        gidx = s.sb("gidx", [P, T, S], I32)
        valid = s.sb("valid", [P, T, S])
        inval = s.sb("inval", [P, T, S])
        tmp = s.sb("tmp", [P, T, S])
        ubase = s.sb("ubase", [1, 6, T])
        u_i = s.sb("u_i", [1, T], I32)
        soft = s.sb("soft", [P, 4, T])
        expd = s.sb("expd", [P, T * S + T])
        msw = s.sb("msw", [P, T, 2])
        v_steps = s.sem("v2_steps")
        exp_in, exp_out = s.sem("exp_in"), s.sem("exp_out")
        ms_ready, ms_out = s.sem("ms_ready"), s.sem("ms_out")
        starts_ready, runs_in = s.sem("starts_ready"), s.sem("runs_in")
        slots_ready, slots_out = s.sem("slots_ready"), s.sem("slots_out")
        block = ctx.enter_context(nc.Block())
        NSTEP = 29

        @block.gpsimd
        def _(pool):
            rounds = pool.value_load(g["info"][0:1, 4, 0:1], min_val=1, max_val=U)
            with pool.Fori(0, rounds) as r:
                wait_count(pool, starts_ready, r + 1, g["pool_turns"])
                for t in range(T):
                    at = bass.IndirectOffsetOnAxis(ap=start_i[:, t:t + 1], axis=0)
                    pool.indirect_dma_start(srun[:, t, :], None, g["src"].unsqueeze(1), at).then_inc(runs_in, 16)
                    pool.indirect_dma_start(wrun[:, t, :], None, g["edge_weight"].unsqueeze(1), at).then_inc(runs_in, 16)
            pool.wait_ge(ms_ready, 2)
            for t in range(T):
                pool.indirect_dma_start(g["MS"], bass.IndirectOffsetOnAxis(ap=g["nid_i"][:, t:t + 1], axis=0),
                                        msw[:, t, :], None).then_inc(ms_out, 16)
            pool.wait_ge(ms_out, 16 * T)

        @block.scalar
        def _(act):
            rounds = act.value_load(g["info"][0:1, 4, 0:1], min_val=1, max_val=U)
            with act.Fori(0, rounds) as r:
                act.wait_ge(exp_in, r + 1)
                act.activation(expd[:, :], expd[:, :], ACT.Exp).then_inc(exp_out, 1)

        @block.vector
        def _(dve):
            st = Steps(dve, v_steps)
            rounds = dve.value_load(g["info"][0:1, 4, 0:1], min_val=1, max_val=U)
            st.mark(dve.tensor_copy(start_f[:, :], g["ni"][:, :, 1]))
            st.mark(dve.tensor_copy(rem[:, :], g["ni"][:, :, 2]))
            st.mark(dve.tensor_copy(ubase[:, 0:2, :], g["info"][:, 1:4:2, :]))
            st.mark(dve.memset(ubase[:, 2, :], 0.0))
            st.mark(dve.tensor_scalar(ubase[:, 5, :], g["iota_f"][0:1, 0:T], float(U), None, ALU.add))
            st.after(dve.tensor_scalar(place[:, :], g["iota_f"][:, 0:S], 1.0, None, ALU.add))
            st.mark(dve.memset(soft[:, 0, :], -BIG))
            st.after(dve.memset(soft[:, 1, :], 0.0))
            first = st.n
            dve.sem_inc(slots_out, 1)
            with dve.Fori(0, rounds) as r:
                st = Steps(dve, v_steps, r * NSTEP + first)
                dve.wait_ge(slots_out, r * (2 * T * 16) + 1)
                st.after(dve.tensor_scalar(start_i[:, :], start_f[:, :], float(E), None, ALU.min))
                st.after(dve.tensor_tensor(ubase[:, 3, :], ubase[:, 2, :], ubase[:, 0, :], ALU.is_lt))
                st.after(dve.tensor_scalar(ubase[:, 4, :], ubase[:, 3, :], -1.0, 1.0, ALU.mult, ALU.add))
                st.after(dve.tensor_tensor(ubase[:, 4, :], ubase[:, 4, :], ubase[:, 5, :], ALU.mult))
                dve.sem_inc(starts_ready, 1)
                st.after(dve.tensor_tensor(ubase[:, 3, :], ubase[:, 3, :], ubase[:, 1, :], ALU.mult))
                st.after(dve.tensor_tensor(u_i[:, :], ubase[:, 3, :], ubase[:, 4, :], ALU.add))
                st.mark(dve.tensor_tensor(valid[:, :, :], free_bcast(rem[:, :], 0, S),
                                          free_bcast(g["iota_f"][:, 0:S], T, 0), ALU.is_gt))
                st.mark(dve.tensor_copy(slot[:, :, 2, :], free_bcast(place[:, :], T, 0)))
                dve.wait_ge(runs_in, (r + 1) * (2 * T * 16))
                st.after(dve.tensor_copy(tmp[:, :, :], srun[:, :, :]))
                st.mark(dve.tensor_scalar(inval[:, :, :], valid[:, :, :], -1.0, None, ALU.add))
                st.after(dve.tensor_tensor(tmp[:, :, :], tmp[:, :, :], valid[:, :, :], ALU.mult))
                st.after(dve.tensor_tensor(slot[:, :, 0, :], tmp[:, :, :], inval[:, :, :], ALU.add))
                st.after(dve.tensor_tensor(tmp[:, :, :], inval[:, :, :], free_bcast(g["ni"][:, :, 0], 0, S), ALU.mult))
                st.after(dve.tensor_tensor(tmp[:, :, :], slot[:, :, 0, :], tmp[:, :, :], ALU.subtract))
                st.after(dve.tensor_tensor(gidx[:, :, :], tmp[:, :, :], inval[:, :, :], ALU.subtract))
                st.after(dve.tensor_tensor(tmp[:, :, :], wrun[:, :, :], valid[:, :, :], ALU.mult))
                st.after(dve.scalar_tensor_tensor(out=slot[:, :, 1, :], in0=inval[:, :, :], scalar=BIG,
                                                  in1=tmp[:, :, :], op0=ALU.mult, op1=ALU.add))
                dve.sem_inc(slots_ready, 1)
                st.mark(dve.tensor_scalar(start_f[:, :], start_f[:, :], float(S), None, ALU.add))
                st.mark(dve.tensor_scalar(rem[:, :], rem[:, :], -float(S), None, ALU.add))
                st.mark(dve.tensor_scalar(place[:, :], place[:, :], float(S), None, ALU.add))
                st.mark(dve.tensor_scalar(ubase[:, 1:3, :], ubase[:, 1:3, :], 1.0, None, ALU.add))
                weights = slot[:, :, 1, :]
                sums = expd[:, 0:T * S].rearrange("p (t k) -> p t k", k=S)
                st.after(dve.tensor_reduce(soft[:, 2, :], weights, AX.X, ALU.max))
                st.after(dve.tensor_tensor(soft[:, 2, :], soft[:, 2, :], soft[:, 0, :], ALU.max))
                st.mark(dve.tensor_tensor(expd[:, T * S:], soft[:, 0, :], soft[:, 2, :], ALU.subtract))
                st.after(dve.tensor_tensor(sums, weights, free_bcast(soft[:, 2, :], 0, S), ALU.subtract))
                dve.sem_inc(exp_in, 1)
                dve.wait_ge(exp_out, r + 1)
                st.mark(dve.tensor_copy(soft[:, 0, :], soft[:, 2, :]))
                st.mark(dve.tensor_reduce(soft[:, 3, :], sums, AX.X, ALU.add))
                st.after(dve.tensor_tensor(soft[:, 1, :], soft[:, 1, :], expd[:, T * S:], ALU.mult))
                st.after(dve.tensor_tensor(soft[:, 1, :], soft[:, 1, :], soft[:, 3, :], ALU.add))
                assert st.n == NSTEP, st.n
            dve.tensor_copy(msw[:, :, 0], soft[:, 0, :]).then_inc(ms_ready, 1)
            dve.tensor_copy(msw[:, :, 1], soft[:, 1, :]).then_inc(ms_ready, 1)

        @block.sync
        def _(sp):
            rounds = sp.value_load(g["info"][0:1, 4, 0:1], min_val=1, max_val=U)
            with sp.Fori(0, rounds) as r:
                wait_count(sp, slots_ready, r + 1, g["sp_turns"])
                for t in range(T):
                    u = sp.value_load(u_i[0:1, t:t + 1], min_val=0, max_val=U + T - 1)
                    sp.dma_start(g["SLOT"][:, bass.ds(u * (3 * S), 3 * S)],
                                 slot[:, t].rearrange("p c k -> p (c k)")).then_inc(slots_out, 16)
                    sp.dma_start(g["GIDX"][:, bass.ds(u * S, S)], gidx[:, t, :]).then_inc(slots_out, 16)
            wait_count(sp, slots_out, rounds * (2 * T * 16) + 1, g["sp_turns"])


def scatter_pairs(nc, g):
    with ExitStack() as ctx:
        s = Scope(nc, ctx)
        a = s.sb("sa", [P, 3, S])
        b = s.sb("sbb", [P, 3, S])
        eq = s.sb("eq", [P, S, S])
        eqp = s.sb("eqp", [P, S, S])
        ex = s.sb("ex", [P, S * S + S])
        acc = s.sb("acc", [P, 4, S])
        new = s.sb("new", [P, 4, S])
        fin = s.sb("fin", [P, 4, S])
        dcol = s.sb("dcol", [P, 1])
        lns = s.sb("lns", [P, S])
        pair = s.sb("pair", [P, S, 2])
        pair_at = s.sb("pair_at", [P, S], I32)
        cmax = s.sb("cmax", [P, S])
        a_in, b_in, a_free, b_free = s.sem("a_in"), s.sem("b_in"), s.sem("a_free"), s.sem("b_free")
        tile_steps, sup_steps, pair_steps = s.sem("tile_steps"), s.sem("sup_steps"), s.sem("pair_steps")
        ex_in, ex_out, ln_in, ln_out = s.sem("ex_in"), s.sem("ex_out"), s.sem("ln_in"), s.sem("ln_out")
        entries_ready, entries_out = s.sem("entries_ready"), s.sem("entries_out")
        block = ctx.enter_context(nc.Block())
        T_STEPS, U_STEPS, Q_STEPS = 1, 12, 16

        def sizes(eng, t):
            return (eng.value_load(g["info"][0:1, 1, bass.ds(t, 1)], min_val=1, max_val=U),
                    eng.value_load(g["info"][0:1, 3, bass.ds(t, 1)], min_val=0, max_val=U))

        @block.sync
        def _(sp):
            pairs = sp.alloc_register("sp_pairs")
            sp.reg_mov(pairs, 0)
            with sp.Fori(0, T) as t:
                rounds, base = sizes(sp, t)
                with sp.Fori(0, rounds) as r:
                    wait_count(sp, a_free, base + r + 1, g["sp_turns"])
                    sp.dma_start(a[:, :, :].rearrange("p c k -> p (c k)"),
                                 g["SLOT"][:, bass.ds(nc.s_assert_within(base + r, 0, U, skip_runtime_bounds_check_because="the tables are sized for it") * (3 * S), 3 * S)]).then_inc(a_in, 16)
                    with sp.Fori(0, rounds) as q:
                        n = sp.snap(pairs, min_val=0, max_val=1 << 23)
                        wait_count(sp, b_free, n + 1, g["sp_turns"])
                        sp.dma_start(b[:, :, :].rearrange("p c k -> p (c k)"),
                                     g["SLOT"][:, bass.ds(nc.s_assert_within(base + q, 0, U, skip_runtime_bounds_check_because="the tables are sized for it") * (3 * S), 3 * S)]).then_inc(b_in, 16)
                        sp.reg_add(pairs, pairs, 1)

        @block.vector
        def _(dve):
            pairs = dve.alloc_register("v_pairs")
            dve.reg_mov(pairs, 0)
            dve.sem_inc(a_free, 1)
            dve.sem_inc(b_free, 1)
            dve.memset(cmax[:, :], 0.0).then_inc(tile_steps, 1)
            with dve.Fori(0, T) as t:
                rounds, base = sizes(dve, t)
                before = dve.value_load(g["info"][0:1, 2, bass.ds(t, 1)], min_val=0, max_val=SB * U)
                st = Steps(dve, tile_steps, t * T_STEPS + 1)
                st.after(dve.tensor_copy(dcol[:, :], g["ni"][:, bass.ds(t, 1), 0]))
                assert st.n == T_STEPS
                dve.sem_inc(g["v_turns"], 1)
                with dve.Fori(0, rounds) as r:
                    st = Steps(dve, sup_steps, (base + r) * U_STEPS)
                    st.mark(dve.memset(acc[:, 0:2, :], 0.0))
                    st.mark(dve.memset(acc[:, 2, :], -BIG))
                    st.after(dve.memset(acc[:, 3, :], 0.0))
                    wait_count(dve, a_in, (base + r) * 16 + 16, g["v_turns"])
                    with dve.Fori(0, rounds) as q:
                        n = dve.snap(pairs, min_val=0, max_val=1 << 23)
                        sq = Steps(dve, pair_steps, n * Q_STEPS)
                        t_ex = ex[:, 0:S * S].rearrange("p (j k) -> p j k", k=S)
                        dve.wait_ge(b_in, n * 16 + 16)
                        sq.after(dve.tensor_tensor(eq[:, :, :], free_bcast(a[:, 0, :], 0, S),
                                                   free_bcast(b[:, 0, :], S, 0), ALU.is_equal))
                        sq.mark(dve.tensor_reduce(new[:, 0, :], eq[:, :, :], AX.X, ALU.add))
                        sq.mark(dve.tensor_tensor(eqp[:, :, :], eq[:, :, :], free_bcast(b[:, 2, :], S, 0), ALU.mult))
                        sq.after(dve.tensor_scalar(t_ex, eq[:, :, :], 2 * BIG, -BIG, ALU.mult, ALU.add))
                        sq.after(dve.tensor_tensor(t_ex, t_ex, free_bcast(b[:, 1, :], S, 0), ALU.min))
                        dve.sem_inc(b_free, 1)
                        sq.mark(dve.tensor_reduce(new[:, 1, :], eqp[:, :, :], AX.X, ALU.max))
                        sq.after(dve.tensor_reduce(new[:, 2, :], t_ex, AX.X, ALU.max))
                        sq.mark(dve.tensor_tensor(acc[:, 0, :], acc[:, 0, :], new[:, 0, :], ALU.add))
                        sq.mark(dve.tensor_tensor(acc[:, 1, :], acc[:, 1, :], new[:, 1, :], ALU.max))
                        sq.after(dve.tensor_tensor(new[:, 2, :], acc[:, 2, :], new[:, 2, :], ALU.max))
                        sq.mark(dve.tensor_tensor(t_ex, t_ex, free_bcast(new[:, 2, :], 0, S), ALU.subtract))
                        sq.after(dve.tensor_tensor(ex[:, S * S:], acc[:, 2, :], new[:, 2, :], ALU.subtract))
                        dve.sem_inc(ex_in, 1)
                        sq.after(dve.tensor_copy(acc[:, 2, :], new[:, 2, :]))
                        dve.wait_ge(ex_out, n + 1)
                        sq.mark(dve.tensor_reduce(new[:, 3, :], t_ex, AX.X, ALU.add))
                        sq.after(dve.tensor_tensor(acc[:, 3, :], acc[:, 3, :], ex[:, S * S:], ALU.mult))
                        sq.after(dve.tensor_tensor(acc[:, 3, :], acc[:, 3, :], new[:, 3, :], ALU.add))
                        assert sq.n == Q_STEPS, sq.n
                        dve.reg_add(pairs, pairs, 1)
                    dve.sem_inc(ln_in, 1)
                    st.mark(dve.tensor_tensor(fin[:, 0, :], acc[:, 1, :], a[:, 2, :], ALU.is_equal))
                    st.mark(dve.tensor_scalar(fin[:, 1, :], a[:, 0, :], 0.0, None, ALU.is_ge))
                    st.mark(dve.tensor_scalar(fin[:, 2, :], a[:, 0, :], float(NP), dcol[:, 0:1], ALU.mult, ALU.add))
                    st.after(dve.tensor_tensor(cmax[:, :], cmax[:, :], acc[:, 0, :], ALU.max))
                    dve.sem_inc(a_free, 1)
                    st.after(dve.tensor_tensor(fin[:, 0, :], fin[:, 0, :], fin[:, 1, :], ALU.mult))
                    st.after(dve.scalar_tensor_tensor(out=fin[:, 2, :], in0=fin[:, 2, :], scalar=-float(OFF),
                                                      in1=fin[:, 0, :], op0=ALU.add, op1=ALU.mult))
                    dve.sem_inc(g["v_turns"], 1)
                    with dve.If(base + r > 0):
                        wait_count(dve, entries_out, (before + r * SB) * (B * 16), g["v_turns"])
                    with dve.Else():
                        dve.sem_inc(g["v_turns"], 1)
                    st.mark(dve.tensor_scalar(pair_at[:, :], fin[:, 2, :], float(OFF), None, ALU.add))
                    st.mark(dve.tensor_copy(pair[:, :, 0], acc[:, 0, :]))
                    dve.wait_ge(ln_out, base + r + 1)
                    st.after(dve.tensor_tensor(pair[:, :, 1], acc[:, 2, :], lns[:, :], ALU.add))
                    dve.sem_inc(entries_ready, 1)
                    assert st.n == U_STEPS, st.n
            st = Steps(dve, tile_steps, T * T_STEPS + 1)
            st.after(dve.tensor_reduce(g["cmax"][:, :], cmax[:, :], AX.X, ALU.max))

        @block.scalar
        def _(act):
            pairs = act.alloc_register("a_pairs")
            act.reg_mov(pairs, 0)
            with act.Fori(0, T) as t:
                rounds, base = sizes(act, t)
                with act.Fori(0, rounds) as r:
                    with act.Fori(0, rounds) as q:
                        n = act.snap(pairs, min_val=0, max_val=1 << 23)
                        act.wait_ge(ex_in, n + 1)
                        act.activation(ex[:, :], ex[:, :], ACT.Exp).then_inc(ex_out, 1)
                        act.reg_add(pairs, pairs, 1)
                    act.wait_ge(ln_in, base + r + 1)
                    act.activation(lns[:, :], acc[:, 3, :], ACT.Ln).then_inc(ln_out, 1)

        @block.gpsimd
        def _(pool):
            with pool.Fori(0, T) as t:
                rounds, base = sizes(pool, t)
                blocks = pool.value_load(g["info"][0:1, 0, bass.ds(t, 1)], min_val=1, max_val=SB * U)
                with pool.Fori(0, rounds) as r:
                    wait_count(pool, entries_ready, base + r + 1, g["pool_turns"])
                    for j in range(SB):
                        with pool.If(blocks > r * SB + j):
                            for k in range(B * j, B * j + B):
                                at = bass.IndirectOffsetOnAxis(ap=pair_at[:, k:k + 1], axis=0)
                                pool.indirect_dma_start(g["PAIR"], at, pair[:, k, :], None, bounds_check=OFF - 1,
                                                        oob_is_err=False).then_inc(entries_out, 16)
            before = pool.value_load(g["info"][0:1, 2, T - 1:T], min_val=0, max_val=SB * U)
            blocks = pool.value_load(g["info"][0:1, 0, T - 1:T], min_val=1, max_val=SB * U)
            wait_count(pool, entries_out, (before + blocks) * (B * 16), g["pool_turns"])


CH = 3
NCH = (T - 1) // CH
assert T == NCH * CH + 1


def read_pairs(nc, g):
    with ExitStack() as ctx:
        s = Scope(nc, ctx)
        half = NP // 2
        rows = [s.sb(f"rows{h}", [P, half, 2]) for h in range(2)]
        top = [s.sb(f"top{h}", [P, 2]) for h in range(2)]
        part = [s.sb(f"part{h}", [P, 1]) for h in range(2)]
        tops = s.sb("tops", [P, 2, T])
        sums = s.sb("sums", [P, 2, T])
        spread = s.sb("spread", [P, 2, T])
        dump = s.sb("dump", [P, half], BF16)
        rows_in = [s.sem(f"rows_in{h}") for h in range(2)]
        rows_free = [s.sem(f"rows_free{h}") for h in range(2)]
        top_ready = [s.sem(f"top_ready{h}") for h in range(2)]
        part_ready = [s.sem(f"part_ready{h}") for h in range(2)]
        v_steps = s.sem("v4_steps")
        spread_in, spread_out = s.sem("spread_in"), s.sem("spread_out")
        block = ctx.enter_context(nc.Block())
        pairs = g["PAIR"].rearrange("(t p d) c -> t p (d c)", t=T, p=P)

        @block.sync
        def _(sp):
            with sp.Fori(0, T) as t:
                for h in range(2):
                    wait_count(sp, rows_free[h], 2 * t + 2, g["sp_turns"])
                    sp.dma_start(rows[h][:, :, :].rearrange("p d c -> p (d c)"),
                                 pairs[bass.ds(t, 1), :, 2 * half * h:2 * half * (h + 1)].squeeze(0),
                                 max_dma_last_dim=8192).then_inc(rows_in[h], 16)

        @block.scalar
        def _(act):
            for h in range(2):
                act.sem_inc(rows_free[h], 1)
            with act.Fori(0, T) as t:
                for h in range(2):
                    act.wait_ge(rows_in[h], 16 * t + 16)
                    act.copy(g["A"][:, bass.ds(t, 1), half * h:half * (h + 1)].squeeze(1), rows[h][:, :, 0])
                    act.wait_ge(top_ready[h], t + 1)
                    act.activation(dump[:, :], rows[h][:, :, 1], ACT.Exp, bias=top[h][:, 1:2],
                                   accum_out=part[h][:, :]).then_inc(part_ready[h], 1)
                    act.wait_ge(part_ready[h], t + 1)
                    act.sem_inc(rows_free[h], 1)
            act.wait_ge(spread_in, 1)
            act.activation(spread[:, :, :], spread[:, :, :], ACT.Exp).then_inc(spread_out, 1)

        @block.vector
        def _(dve):
            for h in range(2):
                dve.sem_inc(rows_free[h], 1)
            with dve.Fori(0, T) as t:
                st = Steps(dve, v_steps, t * 8)
                for h in range(2):
                    dve.wait_ge(rows_in[h], 16 * t + 16)
                    st.after(dve.tensor_reduce(top[h][:, 0:1], rows[h][:, :, 1], AX.X, ALU.max))
                    st.after(dve.tensor_scalar(top[h][:, 1:2], top[h][:, 0:1], -1.0, None, ALU.mult))
                    dve.sem_inc(rows_free[h], 1)
                    dve.sem_inc(top_ready[h], 1)
                    st.after(dve.tensor_copy(tops[:, h, bass.ds(t, 1)], top[h][:, 0:1]))
                    dve.wait_ge(part_ready[h], t + 1)
                    st.after(dve.tensor_copy(sums[:, h, bass.ds(t, 1)], part[h][:, :]))
            st = Steps(dve, v_steps, T * 8)
            st.after(dve.tensor_tensor(g["mout"][:, :], tops[:, 0, :], tops[:, 1, :], ALU.max))
            st.after(dve.tensor_tensor(spread[:, :, :], tops[:, :, :], free_bcast(g["mout"][:, :], 2, 0), ALU.subtract))
            dve.sem_inc(spread_in, 1)
            dve.wait_ge(spread_out, 1)
            st.after(dve.tensor_tensor(sums[:, :, :], sums[:, :, :], spread[:, :, :], ALU.mult))
            st.after(dve.tensor_tensor(g["sout"][:, :], sums[:, 0, :], sums[:, 1, :], ALU.add))


def normalise(nc, g, first=False):
    with ExitStack() as ctx:
        s = Scope(nc, ctx)
        tmp = s.sb("ln_tmp", [P, T, D])
        st4 = s.sb("ln_st", [P, 4, 2 * T])
        v_steps, root_in, root_out = s.sem("ln_steps"), s.sem("root_in"), s.sem("root_out")
        block = ctx.enter_context(nc.Block())
        X, H = g["X"], g["H"]
        w = 2 * T if first else T

        @block.scalar
        def _(act):
            act.wait_ge(root_in, 1)
            act.activation(st4[:, 2, 0:w], st4[:, 1, 0:w], ACT.Sqrt).then_inc(root_out, 1)

        @block.vector
        def _(dve):
            st = Steps(dve, v_steps)
            st.after(dve.tensor_reduce(st4[:, 0, 0:T], X[:, :, :], AX.X, ALU.add))
            st.after(dve.tensor_scalar(st4[:, 0, 0:T], st4[:, 0, 0:T], 1.0 / D, None, ALU.mult))
            st.after(dve.tensor_tensor(H[:, :, :], X[:, :, :], free_bcast(st4[:, 0, 0:T], 0, D), ALU.subtract))
            st.after(dve.tensor_tensor(tmp[:, :, :], H[:, :, :], H[:, :, :], ALU.mult))
            st.after(dve.tensor_reduce(st4[:, 1, 0:T], tmp[:, :, :], AX.X, ALU.add))
            st.after(dve.tensor_scalar(st4[:, 1, 0:T], st4[:, 1, 0:T], 1.0 / D, 1e-5, ALU.mult, ALU.add))
            if first:
                st.after(dve.tensor_scalar(st4[:, 1, T:w], g["deg"][:, :], 1.0, None, ALU.add))
            dve.sem_inc(root_in, 1)
            dve.wait_ge(root_out, 1)
            st.after(dve.reciprocal(st4[:, 3, 0:w], st4[:, 2, 0:w]))
            st.after(dve.tensor_tensor(st4[:, 2, 0:w], st4[:, 3, 0:w], st4[:, 3, 0:w], ALU.mult))
            st.after(dve.tensor_tensor(st4[:, 2, 0:w], st4[:, 2, 0:w], st4[:, 1, 0:w], ALU.mult))
            st.after(dve.tensor_scalar(st4[:, 2, 0:w], st4[:, 2, 0:w], -0.5, 1.5, ALU.mult, ALU.add))
            st.after(dve.tensor_tensor(st4[:, 3, 0:w], st4[:, 3, 0:w], st4[:, 2, 0:w], ALU.mult))
            if first:
                st.after(dve.tensor_copy(g["dinv"][:, :], st4[:, 3, T:w]))
            st.after(dve.tensor_tensor(H[:, :, :], H[:, :, :], free_bcast(st4[:, 3, 0:T], 0, D), ALU.mult))
            st.after(dve.tensor_scalar(H[:, :, :], H[:, :, :], 0.0, None, ALU.max))


def aggregate(nc, g, weight, bias, own_degree=False, scale=1.0, relu=False, add_to_x=False):
    with ExitStack() as ctx:
        s = Scope(nc, ctx)
        tmp = s.sb("ag_tmp", [P, T, D])
        parts = s.sb("ag_parts", [P, T, 3, D], BF16)
        w2 = s.sb("ag_w", [P, D])
        brow = s.sb("ag_b", [P, D])
        o1 = s.sb("ag_o1", [P, CH * P])
        o2 = s.sb("ag_o2", [D, CH * P])
        sv = s.sb("ag_sv", [P, 4, T])
        dparts = s.sb("ag_dparts", [P, 3, T], BF16)
        diag = s.sb("ag_diag", [P, CH, 3, P], BF16)
        c1 = [bank(g, i) for i in range(2)]
        c2 = [bank(g, 2 + i) for i in range(2)]
        pj = bank(g, 4)
        w_in, v_steps = s.sem("w_in"), s.sem("ag_steps")
        parts_ready, diag_ready, diag_free = s.sem("parts_ready"), s.sem("diag_ready"), s.sem("diag_free")
        chunk_done, o1_ready, o2_ready = s.sem("chunk_done"), s.sem("o1_ready"), s.sem("o2_ready")
        pj_done, pj_free = s.sem("pj_done"), s.sem("pj_free")
        loop_steps = s.sem("ag_loop_steps")
        a_part = s.sem("a_part")
        block = ctx.enter_context(nc.Block())
        H = g["H"]
        nself = 3 if own_degree else 1

        @block.sync
        def _(sp):
            for i in range(2):
                sp.dma_start(w2[i * D:(i + 1) * D, :], weight).then_inc(w_in, 16)
            sp.dma_start(brow[:, :], bias.partition_broadcast(P)).then_inc(w_in, 16)

        @block.vector
        def _(dve):
            st = Steps(dve, v_steps)
            dv = free_bcast(g["dinv"][:, :], 0, D)
            st.after(dve.tensor_tensor(H[:, :, :], H[:, :, :], dv, ALU.mult))
            st.after(dve.tensor_copy(parts[:, :, 0, :], H[:, :, :]))
            st.after(dve.tensor_tensor(tmp[:, :, :], H[:, :, :], parts[:, :, 0, :], ALU.subtract))
            st.after(dve.tensor_copy(parts[:, :, 1, :], tmp[:, :, :]))
            st.after(dve.tensor_tensor(parts[:, :, 2, :], tmp[:, :, :], parts[:, :, 1, :], ALU.subtract))
            st.after(dve.tensor_scalar(sv[:, 0, :], g["dinv"][:, :], scale, None, ALU.mult))
            if own_degree:
                st.after(dve.tensor_scalar(sv[:, 1, :], g["deg"][:, :], 2.0, None, ALU.add))
                st.after(dve.tensor_copy(dparts[:, 0, :], sv[:, 1, :]))
                st.after(dve.tensor_tensor(sv[:, 2, :], sv[:, 1, :], dparts[:, 0, :], ALU.subtract))
                st.after(dve.tensor_copy(dparts[:, 1, :], sv[:, 2, :]))
                st.after(dve.tensor_tensor(dparts[:, 2, :], sv[:, 2, :], dparts[:, 1, :], ALU.subtract))
            else:
                st.after(dve.memset(dparts[:, 0, :], 1.0))
            dve.sem_inc(parts_ready, 1)
            dve.sem_inc(diag_free, 1)

            def chunk(c, tiles, t0, steps):
                dve.wait_ge(diag_free, c + 1)
                for j in range(tiles):
                    for i in range(nself):
                        steps.mark(dve.tensor_tensor(diag[:, j, i, :], g["ident_b"][:, :],
                                                     dparts[:, i, bass.ds(t0 + j, 1)].to_broadcast([P, P]),
                                                     ALU.mult))
                steps.wait()
                dve.sem_inc(diag_ready, 1)
                dve.wait_ge(chunk_done, c + 1)
                steps.after(dve.tensor_copy(o2[:, 0:tiles * P], c2[0][0:D, 0:tiles * P]))
                dve.sem_inc(o2_ready, 1)
                dve.wait_ge(pj_done, c + 1)
                steps.after(dve.tensor_tensor(H[:, bass.ds(t0, tiles), :],
                                              pj[:, 0:tiles * D].rearrange("p (t f) -> p t f", f=D),
                                              free_bcast(sv[:, 0, bass.ds(t0, tiles)], 0, D), ALU.mult))
                dve.sem_inc(pj_free, 1)

            n = CH * nself + 2
            with dve.Fori(0, NCH) as c:
                chunk(c, CH, c * CH, Steps(dve, loop_steps, c * n))
            chunk(NCH, 1, NCH * CH, Steps(dve, loop_steps, NCH * n))
            dve.wait_ge(w_in, 48)
            st.after(dve.tensor_tensor(H[:, :, :], H[:, :, :], free_bcast(brow[:, :], T, 0), ALU.add))
            if relu:
                st.after(dve.tensor_scalar(H[:, :, :], H[:, :, :], 0.0, None, ALU.max))
            if add_to_x:
                st.after(dve.tensor_tensor(g["X"][:, :, :], g["X"][:, :, :], H[:, :, :], ALU.add))

        @block.scalar
        def _(act):
            with act.Fori(0, NCH) as c:
                act.wait_ge(chunk_done, c + 1)
                act.copy(o1[:, :], c1[0][:, 0:CH * P]).then_inc(o1_ready, 1)
            act.wait_ge(chunk_done, NCH + 1)
            act.copy(o1[:, 0:P], c1[0][:, 0:P]).then_inc(o1_ready, 1)

        @block.tensor
        def _(pe):
            pe.wait_ge(parts_ready, 1)
            pe.wait_ge(w_in, 48)

            def chunk(c, tiles, t0):
                w = tiles * P
                for src in range(T):
                    moving = g["A"][:, src, bass.ds(t0 * P, w)]
                    pe.matmul(c1[0][:, 0:w], parts[:, src, 0:2, :].rearrange("p a f -> p (a f)"), moving,
                              start=(src == 0), stop=False, skip_group_check=True)
                    pe.matmul(c2[0][0:D, 0:w], parts[:, src, 2, :], moving, start=(src == 0), stop=False,
                              skip_group_check=True)
                pe.wait_ge(diag_ready, c + 1)
                for j in range(tiles):
                    for i in range(nself):
                        last = i == nself - 1
                        own = parts[:, bass.ds(t0 + j, 1), :, :].rearrange("p t a f -> p (t a f)")
                        pe.matmul(c1[0][:, j * P:(j + 1) * P], own[:, 0:2 * D], diag[:, j, i, :], start=False,
                                  stop=last, skip_group_check=True)
                        mm = pe.matmul(c2[0][0:D, j * P:(j + 1) * P], own[:, 2 * D:3 * D], diag[:, j, i, :],
                                       start=False, stop=last, skip_group_check=True)
                mm.then_inc(chunk_done, 1)
                pe.sem_inc(diag_free, 1)
                pe.wait_ge(o1_ready, c + 1)
                pe.wait_ge(o2_ready, c + 1)
                for j in range(tiles):
                    pe.matmul(pj[:, j * D:(j + 1) * D], o1[:, j * P:(j + 1) * P], w2[:, :], start=True, stop=False)
                    mm = pe.matmul(pj[:, j * D:(j + 1) * D], o2[:, j * P:(j + 1) * P], w2[0:D, :], start=False,
                                   stop=True)
                mm.then_inc(pj_done, 1)
                pe.wait_ge(pj_free, c + 1)

            with pe.Fori(0, NCH) as c:
                chunk(c, CH, c * CH)
            chunk(NCH, 1, NCH * CH)


def bring_rows(nc, g, table, rows, width):
    with ExitStack() as ctx:
        s = Scope(nc, ctx)
        rows_in = s.sem("brought")
        block = ctx.enter_context(nc.Block())

        @block.gpsimd
        def _(pool):
            for t in range(T):
                at = bass.IndirectOffsetOnAxis(ap=g["rank_i"][:, t:t + 1], axis=0)
                pool.indirect_dma_start(rows[:, t, 0:width], None, table, at).then_inc(rows_in, 16)
            pool.wait_ge(rows_in, 16 * T)


def attention_tables(nc, g, rows, k_dim, heads, chans, wl, bl, wr, br, att, left, right):
    hc = heads * chans
    chunks = [(k, min(P, k_dim - k)) for k in range(0, k_dim, P)]
    with ExitStack() as ctx:
        s = Scope(nc, ctx)
        w = s.sb("at_w", [P, len(chunks), 2, hc])
        b = s.sb("at_b", [P, 2, hc])
        a = s.sb("at_a", [P, 2, hc])
        xt = s.sb("at_xt", [P, k_dim])
        xT = s.sb("at_xT", [P, len(chunks), P])
        out = s.sb("at_out", [P, 2, hc + heads])
        prod = s.sb("at_prod", [P, 2, hc])
        tp = bank(g, 0)[:, 0:len(chunks) * P].rearrange("p (k n) -> p k n", n=P)
        mp = bank(g, 1)
        w_in, x_ready, x_turned, xT_ready = s.sem("aw_in"), s.sem("x_ready"), s.sem("x_turned"), s.sem("xT_ready")
        projected, rows_out, v_steps = s.sem("projected"), s.sem("rows_out"), s.sem("at_steps")
        rows_ready, mp_free = s.sem("rows_ready"), s.sem("mp_free")
        block = ctx.enter_context(nc.Block())
        att_row = att.rearrange("h c -> (h c)")

        @block.sync
        def _(sp):
            for i, (wd, bd) in enumerate(((wl, bl), (wr, br))):
                for j, (k, n) in enumerate(chunks):
                    sp.dma_start(w[0:n, j, i, :], wd[k:k + n, :]).then_inc(w_in, 16)
                sp.dma_start(b[:, i, :], bd.partition_broadcast(P)).then_inc(w_in, 16)
                sp.dma_start(a[:, i, :], att_row.partition_broadcast(P)).then_inc(w_in, 16)
            with sp.Fori(0, T) as t:
                wait_count(sp, rows_ready, t + 1, g["sp_turns"])
                for i, table in enumerate((left, right)):
                    sp.dma_start(table[bass.ds(t * P, P), :], out[:, i, :]).then_inc(rows_out, 16)
            sp.wait_ge(rows_out, 32 * T + 1)
        n_w = 16 * 2 * (len(chunks) + 2)

        @block.scalar
        def _(act):
            with act.Fori(0, T) as t:
                act.copy(xt[:, :], rows[:, bass.ds(t, 1), 0:k_dim].squeeze(1)).then_inc(x_ready, 1)
                act.wait_ge(x_turned, t + 1)
                for j, (k, n) in enumerate(chunks):
                    act.copy(xT[0:n, j, :], tp[0:n, j, :]).then_inc(xT_ready, 1)

        @block.tensor
        def _(pe):
            pe.wait_ge(w_in, n_w)
            with pe.Fori(0, T) as t:
                wait_count(pe, x_ready, t + 1, g["pe_turns"])
                for j, (k, n) in enumerate(chunks):
                    mm = pe.transpose(tp[0:n, j, :], xt[:, k:k + n], g["ident"][:, :])
                mm.then_inc(x_turned, 1)
                pe.wait_ge(xT_ready, (t + 1) * len(chunks))
                pe.wait_ge(mp_free, t + 1)
                for j, (k, n) in enumerate(chunks):
                    mm = pe.matmul(mp[:, 0:2 * hc], xT[0:n, j, :], w[0:n, j].rearrange("p i c -> p (i c)"),
                                   start=(j == 0), stop=(j == len(chunks) - 1))
                mm.then_inc(projected, 1)

        @block.vector
        def _(dve):
            dve.wait_ge(w_in, n_w)
            st = Steps(dve, v_steps)
            st.after(dve.tensor_scalar(a[:, :, :], a[:, :, :], 0.2, None, ALU.mult))
            first = st.n
            dve.sem_inc(rows_out, 1)
            dve.sem_inc(mp_free, 1)
            with dve.Fori(0, T) as t:
                st = Steps(dve, v_steps, first + t * 3)
                dve.wait_ge(projected, t + 1)
                dve.wait_ge(rows_out, 32 * t + 1)
                st.after(dve.tensor_tensor(out[:, :, 0:hc], mp[:, 0:2 * hc].rearrange("p (i c) -> p i c", i=2),
                                           b[:, :, :], ALU.add))
                dve.sem_inc(mp_free, 1)
                st.after(dve.tensor_tensor(prod[:, :, :], out[:, :, 0:hc], a[:, :, :], ALU.mult))
                st.after(dve.tensor_reduce(out[:, :, hc:], prod[:, :, :].rearrange("p i (h c) -> p i h c", c=chans),
                                           AX.X, ALU.add))
                dve.sem_inc(rows_ready, 1)


def attend(nc, g, heads, chans, att, bias, left, right, result):
    hc, wd = heads * chans, heads * chans + heads
    with ExitStack() as ctx:
        s = Scope(nc, ctx)
        G = s.sb("gathered", [P, 2, B, wd])
        gi = [s.sb(f"gat_idx{i}", [P, B], I32) for i in range(2)]
        nidc = [s.sb(f"nidc{i}", [P, 1], I32) for i in range(2)]
        own_l = [s.sb(f"own_l{i}", [P, wd]) for i in range(2)]
        own_r = [s.sb(f"own_r{i}", [P, wd]) for i in range(2)]
        res = [s.sb(f"res{i}", [P, hc]) for i in range(2)]
        z = s.sb("z", [P, B, hc])
        zo = s.sb("zo", [P, hc])
        wgt = s.sb("wgt", [P, B, hc])
        arow = s.sb("arow", [P, hc])
        brow = s.sb("gbrow", [P, hc])
        num = s.sb("num", [P, hc])
        wsum = s.sb("wsum", [P, hc])
        sm = s.sb("sm", [P, 6, heads])
        lg = s.sb("lg", [P, 2, B, heads])
        ex = s.sb("gat_ex", [P, (B + 1) * heads])
        rem = s.sb("gat_rem", [P, 1])
        maskneg = s.sb("maskneg", [P, B])
        consts_in = s.sem("gc_in")
        nid_ready, own_in, own_free = [[s.sem(f"{n}{i}") for i in range(2)] for n in ("nid_ready", "own_in", "own_free")]
        res_ready, res_out = [[s.sem(f"{n}{i}") for i in range(2)] for n in ("res_ready", "res_out")]
        idx_in, idx_free = [[s.sem(f"{n}{i}") for i in range(2)] for n in ("idx_in", "idx_free")]
        g_in, g_free = [[s.sem(f"{n}{i}") for i in range(2)] for n in ("g_in", "g_free")]
        tile_steps, block_steps, c_steps = s.sem("gt_steps"), s.sem("gb_steps"), s.sem("gc_steps")
        zo_ready, zo_done, z_ready, z_done = s.sem("zo_ready"), s.sem("zo_done"), s.sem("z_ready"), s.sem("z_done")
        ex_ready, ex_done = s.sem("gex_ready"), s.sem("gex_done")
        block = ctx.enter_context(nc.Block())
        T_STEPS, B_STEPS = 11, 20
        info = g["info"]

        def size(eng, t):
            return (eng.value_load(info[0:1, 0, bass.ds(t, 1)], min_val=1, max_val=SB * U),
                    eng.value_load(info[0:1, 2, bass.ds(t, 1)], min_val=0, max_val=SB * U))

        def tiles(eng, tile):
            with eng.Fori(0, T // 2) as i:
                tile(2 * i, 0, i)
                tile(2 * i + 1, 1, i)
            tile(T - 1, 0, T // 2)

        @block.sync
        def _(sp):
            sp.dma_start(arow[:, :], att.rearrange("h c -> (h c)").partition_broadcast(P)).then_inc(consts_in, 16)
            sp.dma_start(brow[:, :], bias.partition_broadcast(P)).then_inc(consts_in, 16)

            def tile(t, b, i):
                blocks, before = size(sp, t)
                base = sp.value_load(info[0:1, 3, bass.ds(t, 1)], min_val=0, max_val=U)
                with sp.Fori(0, blocks) as j:
                    n = before + j
                    col = nc.s_assert_within(base * S + j * B, 0, (U + T - 1) * S,
                                             skip_runtime_bounds_check_because="the tables are sized for it")

                    def load(k):
                        wait_count(sp, idx_free[k], (n >> 1) + 1, g["sp_turns"])
                        sp.dma_start(gi[k][:, :], g["GIDX"][:, bass.ds(col, B)]).then_inc(idx_in[k], 16)
                    with sp.If((n & 1) < 1):
                        load(0)
                    with sp.Else():
                        load(1)
                wait_count(sp, res_ready[b], i + 1, g["sp_turns"])
                sp.dma_start(result[bass.ds(t * P, P), :], res[b][:, :]).then_inc(res_out[b], 16)
            tiles(sp, tile)
            for b in range(2):
                sp.wait_ge(res_out[b], 16 * ((T + 1 - b) // 2) + 1)

        @block.gpsimd
        def _(pool):
            for k in range(2):
                pool.sem_inc(idx_free[k], 1)

            def own(b, i):
                wait_count(pool, nid_ready[b], i + 1, g["pool_turns"])
                at = bass.IndirectOffsetOnAxis(ap=nidc[b][:, 0:1], axis=0)
                pool.indirect_dma_start(own_l[b][:, :], None, left, at).then_inc(own_in[b], 16)
                pool.indirect_dma_start(own_r[b][:, :], None, right, at).then_inc(own_in[b], 16)

            def tile(t, b, i):
                if b == 0 and not isinstance(i, int):
                    own(1, i)
                elif b == 1:
                    own(0, i + 1)
                blocks, before = size(pool, t)
                with pool.Fori(0, blocks) as j:
                    n = before + j

                    def gather(k):
                        wait_count(pool, idx_in[k], (n >> 1) * 16 + 16, g["pool_turns"])
                        wait_count(pool, g_free[k], (n >> 1) + 1, g["pool_turns"])
                        for c in range(B):
                            at = bass.IndirectOffsetOnAxis(ap=gi[k][:, c:c + 1], axis=0)
                            pool.indirect_dma_start(G[:, k, c, :], None, left, at).then_inc(g_in[k], 16)
                    with pool.If((n & 1) < 1):
                        gather(0)
                    with pool.Else():
                        gather(1)
            own(0, 0)
            tiles(pool, tile)

        @block.vector
        def _(dve):
            for k in range(2):
                dve.sem_inc(g_free[k], 1)
                dve.sem_inc(res_out[k], 1)
            dve.wait_ge(consts_in, 32)
            st = Steps(dve, c_steps)
            st.after(dve.tensor_scalar(arow[:, :], arow[:, :], 0.8, None, ALU.mult))
            dve.tensor_copy(nidc[0][:, :], g["nid_i"][:, 0:1]).then_inc(nid_ready[0], 1)
            m, den, mn, bm, bd, rd = (sm[:, i, :] for i in range(6))

            def tile(t, b, i):
                st = Steps(dve, tile_steps, t * T_STEPS)
                dve.wait_ge(own_in[b], i * 32 + 32)
                if not (b == 0 and isinstance(i, int)):
                    dve.tensor_copy(nidc[1 - b][:, :], g["nid_i"][:, bass.ds(t + 1, 1)]).then_inc(nid_ready[1 - b], 1)
                st.mark(dve.tensor_copy(rem[:, :], g["ni"][:, bass.ds(t, 1), 2]))
                st.after(dve.tensor_tensor(zo[:, :], own_l[b][:, 0:hc], own_r[b][:, 0:hc], ALU.add))
                dve.sem_inc(zo_ready, 1)
                st.mark(dve.tensor_copy(num[:, :], own_l[b][:, 0:hc]))
                st.mark(dve.memset(den, 1.0))
                st.mark(dve.tensor_tensor(lg[:, 0, 0, :], own_l[b][:, hc:], own_r[b][:, hc:], ALU.add))
                dve.wait_ge(zo_done, t + 1)
                st.after(dve.tensor_tensor(wsum[:, :], zo[:, :], arow[:, :], ALU.mult))
                st.after(dve.tensor_reduce(m, wsum[:, :].rearrange("p (h c) -> p h c", c=chans), AX.X, ALU.add))
                st.after(dve.tensor_tensor(m, m, lg[:, 0, 0, :], ALU.add))
                blocks, before = size(dve, t)
                dve.sem_inc(g["v_turns"], 1)
                with dve.Fori(0, blocks) as j:
                    n = before + j
                    sb = Steps(dve, block_steps, n * B_STEPS)
                    Gn = G[:, bass.ds(n & 1, 1)].rearrange("p a k w -> p (a k) w")
                    sb.mark(dve.tensor_scalar(maskneg[:, :], g["iota_f"][:, 0:B], rem[:, 0:1], -BIG, ALU.is_ge,
                                              ALU.mult))
                    with dve.If((n & 1) < 1):
                        wait_count(dve, g_in[0], (n >> 1) * (16 * B) + 16 * B, idx_free[0])
                    with dve.Else():
                        wait_count(dve, g_in[1], (n >> 1) * (16 * B) + 16 * B, idx_free[1])
                    sb.after(dve.tensor_tensor(z[:, :, :], Gn[:, :, 0:hc], free_bcast(own_r[b][:, 0:hc], B, 0),
                                               ALU.add))
                    dve.sem_inc(z_ready, 1)
                    sb.after(dve.tensor_tensor(lg[:, 0], Gn[:, :, hc:], free_bcast(own_r[b][:, hc:], B, 0), ALU.add))
                    sb.mark(dve.tensor_tensor(lg[:, 0], lg[:, 0], free_bcast(maskneg[:, :], 0, heads), ALU.add))
                    dve.wait_ge(z_done, n + 1)
                    sb.after(dve.tensor_tensor(z[:, :, :], z[:, :, :], free_bcast(arow[:, :], B, 0), ALU.mult))
                    sb.after(dve.tensor_reduce(lg[:, 1], z[:, :, :].rearrange("p k (h c) -> p k h c", c=chans), AX.X,
                                               ALU.add))
                    sb.after(dve.tensor_tensor(lg[:, 1], lg[:, 1], lg[:, 0], ALU.add))
                    sb.after(dve.tensor_reduce(bm, lg[:, 1].rearrange("p k h -> p h k"), AX.X, ALU.max))
                    sb.after(dve.tensor_tensor(mn, m, bm, ALU.max))
                    a = ex[:, 0:B * heads].rearrange("p (k h) -> p k h", h=heads)
                    sc = ex[:, B * heads:]
                    sb.mark(dve.tensor_tensor(a, lg[:, 1], free_bcast(mn, B, 0), ALU.subtract))
                    sb.after(dve.tensor_tensor(sc, m, mn, ALU.subtract))
                    dve.sem_inc(ex_ready, 1)
                    sb.mark(dve.tensor_copy(m, mn))
                    sb.after(dve.tensor_scalar(rem[:, :], rem[:, :], -float(B), None, ALU.add))
                    dve.wait_ge(ex_done, n + 1)
                    sb.mark(dve.tensor_tensor(wgt[:, :, :].rearrange("p k (h c) -> p k h c", c=chans),
                                              Gn[:, :, 0:hc].rearrange("p k (h c) -> p k h c", c=chans),
                                              free_bcast(ex[:, 0:B * heads], 0, chans)
                                              .rearrange("p (k h) c -> p k h c", h=heads), ALU.mult))
                    sb.mark(dve.tensor_reduce(bd, a.rearrange("p k h -> p h k"), AX.X, ALU.add))
                    sb.mark(dve.tensor_tensor(den, den, sc, ALU.mult))
                    sb.after(dve.tensor_tensor(num[:, :].rearrange("p (h c) -> p h c", c=chans),
                                               num[:, :].rearrange("p (h c) -> p h c", c=chans),
                                               free_bcast(sc, 0, chans), ALU.mult))
                    dve.sem_inc(g["v_turns"], 1)
                    with dve.If((n & 1) < 1):
                        dve.sem_inc(g_free[0], 1)
                    with dve.Else():
                        dve.sem_inc(g_free[1], 1)
                    sb.mark(dve.tensor_tensor(den, den, bd, ALU.add))
                    sb.after(dve.tensor_reduce(wsum[:, :], wgt[:, :, :].rearrange("p k w -> p w k"), AX.X, ALU.add))
                    sb.after(dve.tensor_tensor(num[:, :], num[:, :], wsum[:, :], ALU.add))
                    assert sb.n == B_STEPS, sb.n
                st.after(dve.reciprocal(rd, den))
                dve.wait_ge(res_out[b], i * 16 + 1)
                st.after(dve.tensor_tensor(res[b][:, :].rearrange("p (h c) -> p h c", c=chans),
                                           num[:, :].rearrange("p (h c) -> p h c", c=chans),
                                           free_bcast(rd, 0, chans), ALU.mult))
                st.after(dve.tensor_tensor(res[b][:, :], res[b][:, :], brow[:, :], ALU.add))
                dve.sem_inc(res_ready[b], 1)
                assert st.n == T_STEPS, st.n
            tiles(dve, tile)

        @block.scalar
        def _(act):
            def tile(t, b, i):
                act.wait_ge(zo_ready, t + 1)
                act.activation(zo[:, :], zo[:, :], ACT.Relu).then_inc(zo_done, 1)
                blocks, before = size(act, t)
                with act.Fori(0, blocks) as j:
                    n = before + j
                    act.wait_ge(z_ready, n + 1)
                    act.activation(z[:, :, :], z[:, :, :], ACT.Relu).then_inc(z_done, 1)
                    act.wait_ge(ex_ready, n + 1)
                    act.activation(ex[:, :], ex[:, :], ACT.Exp).then_inc(ex_done, 1)
            tiles(act, tile)


def add_rows(nc, g, rows):
    with ExitStack() as ctx:
        s = Scope(nc, ctx)
        added = s.sem("added")
        block = ctx.enter_context(nc.Block())

        @block.vector
        def _(dve):
            dve.tensor_tensor(g["X"][:, :, :], g["X"][:, :, :], rows[:, :, :], ALU.add).then_inc(added, 1)


def pair_softmax(nc, g):
    with ExitStack() as outer:
        so = Scope(nc, outer)
        rin = so.sb("rin", [P, T])
        outT = so.sb("outT", [D, NP])
        with ExitStack() as ctx:
            s = Scope(nc, ctx)
            rows = [s.sb(f"prow{b}", [P, NP, 2]) for b in range(2)]
            wt = [s.sb(f"pwt{b}", [P, NP]) for b in range(2)]
            hs = [s.sb(f"phs{b}", [P, D]) for b in range(2)]
            minrow = s.sb("minrow", [P, NP])
            ms = s.sb("ms", [P, T, 2])
            hmin = s.sb("hmin", [P, T])
            hout = s.sb("hout", [P, T])
            bias_c = [s.sb(f"bias_c{b}", [P, 1]) for b in range(2)]
            st4 = s.sb("ps_st", [P, 3, 2 * T])
            zero_b = s.sb("pz", [P, 512], BF16)
            pt = [bank(g, c) for c in range(7)]
            turn = bank(g, 7)
            ms_in, root_in, root_out, v_steps = s.sem("ms_in"), s.sem("pr_in"), s.sem("pr_out"), s.sem("ps_steps")
            turned, copied, ready = s.sem("turned"), s.sem("copied"), s.sem("ready")
            rows_in, wt_ready, wt_exp, wt_free = [[s.sem(f"{n}{i}") for i in range(2)] for n in
                                                  ("prow_in", "wt_ready", "wt_exp", "wt_free")]
            tile_steps = s.sem("pt_steps")
            all_done = s.sem("all_done")
            block = ctx.enter_context(nc.Block())
            pairs = g["PAIR"].rearrange("(t p d) c -> t p (d c)", t=T, p=P)
            widths = [512] * (NP // 512) + [NP % 512]

            def tiles(eng, tile):
                with eng.Fori(0, T // 2) as i:
                    tile(2 * i, 0, i)
                    tile(2 * i + 1, 1, i)
                tile(T - 1, 0, T // 2)

            @block.sync
            def _(sp):
                sp.dma_start(ms[:, :, :], g["MS"].rearrange("(t p) c -> p t c", p=P)).then_inc(ms_in, 16)

                def tile(t, b, i):
                    wait_count(sp, wt_ready[b], i + 1, g["sp_turns"])
                    sp.dma_start(rows[b][:, :, :].rearrange("p d c -> p (d c)"), pairs[bass.ds(t, 1)].squeeze(0),
                                 max_dma_last_dim=8192).then_inc(rows_in[b], 16)
                tiles(sp, tile)

            @block.vector
            def _(dve):
                st = Steps(dve, v_steps)
                for b in range(2):
                    dve.sem_inc(wt_ready[b], 1)
                dve.wait_ge(ms_in, 16)
                st.after(dve.tensor_scalar(hmin[:, :], ms[:, :, 0], -0.1 * BIG, 0.5, ALU.max, ALU.mult))
                dve.sem_inc(ready, 1)
                st.mark(dve.memset(zero_b[:, :], 0.0))
                st.mark(dve.tensor_scalar(hout[:, :], g["mout"][:, :], -0.5, None, ALU.mult))
                st.mark(dve.tensor_copy(st4[:, 0, 0:T], ms[:, :, 1]))
                st.after(dve.tensor_copy(st4[:, 0, T:], g["sout"][:, :]))
                dve.sem_inc(root_in, 1)
                dve.wait_ge(root_out, 1)
                st.after(dve.reciprocal(st4[:, 2, :], st4[:, 1, :]))
                st.after(dve.tensor_tensor(st4[:, 1, :], st4[:, 2, :], st4[:, 2, :], ALU.mult))
                st.after(dve.tensor_tensor(st4[:, 1, :], st4[:, 1, :], st4[:, 0, :], ALU.mult))
                st.after(dve.tensor_scalar(st4[:, 1, :], st4[:, 1, :], -0.5, 1.5, ALU.mult, ALU.add))
                st.after(dve.tensor_tensor(st4[:, 2, :], st4[:, 2, :], st4[:, 1, :], ALU.mult))
                st.mark(dve.tensor_copy(rin[:, :], st4[:, 2, 0:T]))
                st.after(dve.tensor_tensor(g["H"][:, :, :], g["H"][:, :, :], free_bcast(st4[:, 2, T:], 0, D), ALU.mult))
                dve.sem_inc(ready, 1)
                dve.wait_ge(copied, -(-T // 4))

                def tile(t, b, i):
                    st = Steps(dve, tile_steps, t * 3)
                    dve.wait_ge(rows_in[b], i * 16 + 16)
                    dve.wait_ge(wt_free[b], i + 1)
                    st.mark(dve.tensor_copy(hs[b][:, :], g["H"][:, bass.ds(t, 1), :].squeeze(1)))
                    st.mark(dve.tensor_copy(bias_c[b][:, :], hout[:, bass.ds(t, 1)]))
                    st.after(dve.tensor_tensor(wt[b][:, :], rows[b][:, :, 1], minrow[:, :], ALU.subtract))
                    dve.sem_inc(wt_ready[b], 1)
                tiles(dve, tile)
                dve.wait_ge(all_done, 1)
                off = 0
                for c, w in enumerate(widths):
                    dve.tensor_copy(outT[:, off:off + w], pt[c][0:D, 0:w]).then_inc(v_steps, 1)
                    off += w

            @block.scalar
            def _(act):
                act.wait_ge(root_in, 1)
                act.activation(st4[:, 1, :], st4[:, 0, :], ACT.Sqrt).then_inc(root_out, 1)
                for j in range(-(-T // 4)):
                    act.wait_ge(turned, j + 1)
                    w = min(4, T - 4 * j) * P
                    act.copy(minrow[:, 4 * j * P:4 * j * P + w], turn[:, 0:w]).then_inc(copied, 1)

                def tile(t, b, i):
                    act.wait_ge(wt_ready[b], i + 2)
                    act.activation(wt[b][:, :], wt[b][:, :], ACT.Exp, bias=bias_c[b][:, 0:1]).then_inc(wt_exp[b], 1)
                tiles(act, tile)

            @block.tensor
            def _(pe):
                pe.wait_ge(ready, 1)
                for t in range(T):
                    if t and t % 4 == 0:
                        pe.wait_ge(copied, t // 4)
                    mm = pe.transpose(turn[:, (t % 4) * P:(t % 4 + 1) * P], hmin[:, t:t + 1].to_broadcast([P, P]),
                                      g["ident"][:, :])
                    if t % 4 == 3 or t == T - 1:
                        mm.then_inc(turned, 1)
                pe.wait_ge(ready, 2)
                for b in range(2):
                    pe.sem_inc(wt_free[b], 1)
                for c, w in enumerate(widths):
                    pe.matmul(pt[c][0:D, 0:w], zero_b[:, 0:D], zero_b[:, 0:w], start=True, stop=False,
                              skip_group_check=True)

                def tile(t, b, i):
                    pe.wait_ge(wt_exp[b], i + 1)
                    off = 0
                    for c, w in enumerate(widths):
                        mm = pe.matmul(pt[c][0:D, 0:w], hs[b][:, :], wt[b][:, off:off + w], start=False, stop=False,
                                       skip_group_check=True)
                        off += w
                    mm.then_inc(wt_free[b], 1)
                tiles(pe, tile)
                for c, w in enumerate(widths):
                    mm = pe.matmul(pt[c][0:D, 0:w], zero_b[:, 0:D], zero_b[:, 0:w], start=False, stop=True,
                                   skip_group_check=True)
                mm.then_inc(all_done, 1)

        with ExitStack() as ctx:
            s = Scope(nc, ctx)
            back = [bank(g, i).rearrange("p (t f) -> p t f", f=D) for i in range(4)]
            tmp = s.sb("ps_tmp", [P, T, D])
            turned, v_steps = s.sem("turned_back"), s.sem("psb_steps")
            block = ctx.enter_context(nc.Block())

            @block.tensor
            def _(pe):
                for t in range(T):
                    pe.transpose(back[t // 8][:, t % 8, :], outT[:, t * P:(t + 1) * P],
                                 g["ident"][0:D, 0:D]).then_inc(turned, 1)

            @block.vector
            def _(dve):
                st = Steps(dve, v_steps)
                for j in range(4):
                    a, b = 8 * j, min(8 * j + 8, T)
                    dve.wait_ge(turned, b)
                    st.after(dve.tensor_tensor(tmp[:, a:b, :], back[j][:, 0:b - a, :],
                                               free_bcast(rin[:, a:b], 0, D), ALU.mult))
                st.after(dve.tensor_tensor(g["X"][:, :, :], g["X"][:, :, :], tmp[:, :, :], ALU.add))


def store_rows(nc, g, table):
    with ExitStack() as ctx:
        s = Scope(nc, ctx)
        out = s.sem("stored")
        block = ctx.enter_context(nc.Block())

        @block.sync
        def _(sp):
            sp.dma_start(table.rearrange("(t p) f -> p t f", p=P), g["H"][:, :, :]).then_inc(out, 16)
            sp.wait_ge(out, 16)


def edge_sums(nc, g, table, result):
    with ExitStack() as ctx:
        s = Scope(nc, ctx)
        G = s.sb("e_rows", [P, 2, B, D])
        AT = s.sb("e_attr", [P, 2, B, D])
        gi = [s.sb(f"e_idx{i}", [P, B], I32) for i in range(2)]
        start_f = s.sb("e_start", [P, 1])
        start_i = [s.sb(f"e_start_i{i}", [P, 1], I32) for i in range(2)]
        z = s.sb("e_z", [P, B, D])
        valid = s.sb("e_valid", [P, B])
        rem = s.sb("e_rem", [P, 1])
        acc = s.sb("e_acc", [P, D])
        part = s.sb("e_part", [P, D])
        res = [s.sb(f"e_res{i}", [P, D]) for i in range(2)]
        res_ready, res_out = [[s.sem(f"{n}{i}") for i in range(2)] for n in ("er_ready", "er_out")]
        idx_in, idx_free, g_in, g_free = [[s.sem(f"{n}{i}") for i in range(2)] for n in
                                          ("e_idx_in", "e_idx_free", "e_g_in", "e_g_free")]
        pool_steps, tile_steps, block_steps = s.sem("ep_steps"), s.sem("et_steps"), s.sem("eb_steps")
        pt_steps = s.sem("ept_steps")
        block = ctx.enter_context(nc.Block())
        T_STEPS, B_STEPS = 3, 6
        info = g["info"]

        def size(eng, t):
            return (eng.value_load(info[0:1, 0, bass.ds(t, 1)], min_val=1, max_val=SB * U),
                    eng.value_load(info[0:1, 2, bass.ds(t, 1)], min_val=0, max_val=SB * U))

        def tiles(eng, tile):
            with eng.Fori(0, T // 2) as i:
                tile(2 * i, 0, i)
                tile(2 * i + 1, 1, i)
            tile(T - 1, 0, T // 2)

        @block.sync
        def _(sp):
            def tile(t, b, i):
                blocks, before = size(sp, t)
                base = sp.value_load(info[0:1, 3, bass.ds(t, 1)], min_val=0, max_val=U)
                with sp.Fori(0, blocks) as j:
                    n = before + j
                    col = nc.s_assert_within(base * S + j * B, 0, (U + T - 1) * S,
                                             skip_runtime_bounds_check_because="the tables are sized for it")

                    def load(k):
                        wait_count(sp, idx_free[k], (n >> 1) + 1, g["sp_turns"])
                        sp.dma_start(gi[k][:, :], g["GIDX"][:, bass.ds(col, B)]).then_inc(idx_in[k], 16)
                    with sp.If((n & 1) < 1):
                        load(0)
                    with sp.Else():
                        load(1)
                wait_count(sp, res_ready[b], i + 1, g["sp_turns"])
                sp.dma_start(result[bass.ds(t * P, P), :], res[b][:, :]).then_inc(res_out[b], 16)
            tiles(sp, tile)
            for b in range(2):
                sp.wait_ge(res_out[b], 16 * ((T + 1 - b) // 2) + 1)

        @block.gpsimd
        def _(pool):
            for k in range(2):
                pool.sem_inc(idx_free[k], 1)

            def tile(t, b, i):
                blocks, before = size(pool, t)
                pool.tensor_copy(start_f[:, :], g["ni"][:, bass.ds(t, 1), 1]).then_inc(pt_steps, 1)
                wait_count(pool, pt_steps, t + 1, g["pool_turns"])
                with pool.Fori(0, blocks) as j:
                    n = before + j

                    def gather(k):
                        wait_count(pool, idx_in[k], (n >> 1) * 16 + 16, g["pool_turns"])
                        wait_count(pool, g_free[k], (n >> 1) + 1, g["pool_turns"])
                        pool.tensor_scalar(start_i[k][:, :], start_f[:, :], float(E), None, ALU.min)\
                            .then_inc(pool_steps, 1)
                        wait_count(pool, pool_steps, 2 * n + 1, g["pool_turns"])
                        at = bass.IndirectOffsetOnAxis(ap=start_i[k][:, 0:1], axis=0)
                        pool.indirect_dma_start(AT[:, k].rearrange("p k f -> p (k f)"), None, g["edge_attr_64"],
                                                at).then_inc(g_in[k], 16)
                        for c in range(B):
                            at = bass.IndirectOffsetOnAxis(ap=gi[k][:, c:c + 1], axis=0)
                            pool.indirect_dma_start(G[:, k, c, :], None, table, at).then_inc(g_in[k], 16)
                        pool.tensor_scalar(start_f[:, :], start_f[:, :], float(B), None, ALU.add)\
                            .then_inc(pool_steps, 1)
                        wait_count(pool, pool_steps, 2 * n + 2, g["pool_turns"])
                    with pool.If((n & 1) < 1):
                        gather(0)
                    with pool.Else():
                        gather(1)
            tiles(pool, tile)

        @block.vector
        def _(dve):
            for k in range(2):
                dve.sem_inc(g_free[k], 1)
                dve.sem_inc(res_out[k], 1)

            def tile(t, b, i):
                st = Steps(dve, tile_steps, t * T_STEPS)
                st.mark(dve.memset(acc[:, :], 0.0))
                st.after(dve.tensor_copy(rem[:, :], g["ni"][:, bass.ds(t, 1), 2]))
                blocks, before = size(dve, t)
                dve.sem_inc(g["v_turns"], 1)
                with dve.Fori(0, blocks) as j:
                    n = before + j
                    sb = Steps(dve, block_steps, n * B_STEPS)
                    Gn = G[:, bass.ds(n & 1, 1)].rearrange("p a k w -> p (a k) w")
                    An = AT[:, bass.ds(n & 1, 1)].rearrange("p a k w -> p (a k) w")
                    sb.after(dve.tensor_scalar(valid[:, :], g["iota_f"][:, 0:B], rem[:, 0:1], None, ALU.is_lt))
                    sb.mark(dve.tensor_scalar(rem[:, :], rem[:, :], -float(B), None, ALU.add))
                    rows = 16 * (B + 1)
                    with dve.If((n & 1) < 1):
                        wait_count(dve, g_in[0], (n >> 1) * rows + rows, idx_free[0])
                    with dve.Else():
                        wait_count(dve, g_in[1], (n >> 1) * rows + rows, idx_free[1])
                    sb.after(dve.tensor_tensor(z[:, :, :], Gn, An, ALU.add))
                    dve.sem_inc(g["v_turns"], 1)
                    with dve.If((n & 1) < 1):
                        dve.sem_inc(g_free[0], 1)
                    with dve.Else():
                        dve.sem_inc(g_free[1], 1)
                    sb.after(dve.scalar_tensor_tensor(out=z[:, :, :], in0=z[:, :, :], scalar=0.0,
                                                      in1=free_bcast(valid[:, :], 0, D), op0=ALU.max, op1=ALU.mult))
                    sb.after(dve.tensor_reduce(part[:, :], z[:, :, :].rearrange("p k w -> p w k"), AX.X, ALU.add))
                    sb.after(dve.tensor_tensor(acc[:, :], acc[:, :], part[:, :], ALU.add))
                    assert sb.n == B_STEPS, sb.n
                dve.wait_ge(res_out[b], i * 16 + 1)
                st.after(dve.tensor_copy(res[b][:, :], acc[:, :]))
                dve.sem_inc(res_ready[b], 1)
                assert st.n == T_STEPS, st.n
            tiles(dve, tile)


def output_layer(nc, g, rows):
    with ExitStack() as ctx:
        s = Scope(nc, ctx)
        w = s.sb("ow", [D, D])
        brow = s.sb("obrow", [P, D])
        eps = s.sb("oeps", [P, 1])
        xt = s.sb("oxt", [P, D])
        xT = s.sb("oxT", [D, P])
        y = s.sb("oy", [P, D])
        tp = bank(g, 0)[:, 0:P]
        mp = bank(g, 1)
        w_in, comb_ready, x_ready, x_turned = s.sem("ow_in"), s.sem("comb_ready"), s.sem("ox_ready"), s.sem("ox_turned")
        xT_ready, projected, mp_free, v_steps = s.sem("oxT_ready"), s.sem("oprojected"), s.sem("omp_free"), s.sem("o_steps")
        out_done, x_done = s.sem("out_done"), s.sem("x_done")
        block = ctx.enter_context(nc.Block())
        full = N // P

        @block.sync
        def _(sp):
            sp.dma_start(w[:, :], g["L3_gnn_W_T"]).then_inc(w_in, 16)
            sp.dma_start(brow[:, :], g["L3_gnn_b"].partition_broadcast(P)).then_inc(w_in, 16)
            sp.dma_start(eps[:, :], g["L3_gnn_eps"].partition_broadcast(P)).then_inc(w_in, 16)
            sp.wait_ge(x_done, 1)
            sp.dma_start(g["out"][0:full * P, :].rearrange("(t p) f -> p t f", p=P),
                         g["X"][:, 0:full, :]).then_inc(out_done, 16)
            sp.dma_start(g["out"][full * P:N, :], g["X"][0:N - full * P, full, :]).then_inc(out_done, 16)
            sp.wait_ge(out_done, 32)

        @block.scalar
        def _(act):
            act.wait_ge(comb_ready, 1)
            with act.Fori(0, T) as t:
                act.copy(xt[:, :], g["H"][:, bass.ds(t, 1), :].squeeze(1)).then_inc(x_ready, 1)
                act.wait_ge(x_turned, t + 1)
                act.copy(xT[:, :], tp[0:D, :]).then_inc(xT_ready, 1)

        @block.tensor
        def _(pe):
            pe.wait_ge(w_in, 48)
            with pe.Fori(0, T) as t:
                wait_count(pe, x_ready, t + 1, g["pe_turns"])
                pe.transpose(tp[0:D, :], xt[:, :], g["ident"][:, :]).then_inc(x_turned, 1)
                pe.wait_ge(mp_free, t + 1)
                pe.wait_ge(xT_ready, t + 1)
                pe.matmul(mp[:, 0:D], xT[:, :], w[:, :], start=True, stop=True).then_inc(projected, 1)

        @block.vector
        def _(dve):
            st = Steps(dve, v_steps)
            dve.wait_ge(w_in, 48)
            st.after(dve.tensor_scalar(eps[:, :], eps[:, :], 1.0, None, ALU.add))
            H = g["H"][:, :, :].rearrange("p t f -> p (t f)")
            st.after(dve.scalar_tensor_tensor(out=H, in0=H, scalar=eps[:, 0:1],
                                              in1=rows[:, :, :].rearrange("p t f -> p (t f)"), op0=ALU.mult,
                                              op1=ALU.add))
            dve.sem_inc(comb_ready, 1)
            dve.sem_inc(mp_free, 1)
            first = st.n
            with dve.Fori(0, T) as t:
                st = Steps(dve, v_steps, first + 3 * t)
                dve.wait_ge(projected, t + 1)
                st.after(dve.tensor_tensor(y[:, :], mp[:, 0:D], brow[:, :], ALU.add))
                dve.sem_inc(mp_free, 1)
                st.after(dve.tensor_scalar(y[:, :], y[:, :], 0.0, None, ALU.max))
                xs = g["X"][:, bass.ds(t, 1), :].squeeze(1)
                st.after(dve.tensor_tensor(xs, xs, y[:, :], ALU.add))
            dve.sem_inc(x_done, 1)


def build(nc, io):
    with ExitStack() as ctx:
        g = persistent(nc, ctx, io)
        s = Scope(nc, ctx)
        prepare(nc, g)
        fill_slots(nc, g)
        scatter_pairs(nc, g)
        with ExitStack() as dense:
            g["A"] = dense.enter_context(nc.sbuf_tensor("A", [P, T, NP], BF16))
            read_pairs(nc, g)
            normalise(nc, g, first=True)
            aggregate(nc, g, g["L0_gnn_W_ssg"], g["L0_gnn_b_ssg"], own_degree=True, scale=0.5)
            tabs = [s.dram(f"TAB{i}", [NP, w]) for i, w in enumerate((HC + H1, HC + H1, D + 1, D + 1))]
            heads1, heads2 = s.dram("HEADS1", [NP, HC]), s.dram("HEADS2", [NP, D])
            attention_tables(nc, g, g["H"], D, H1, C1, *[g[f"L0_gnn_{n}"] for n in ("W1l", "b1l", "W1r", "b1r", "att1")],
                             tabs[0], tabs[1])
            attend(nc, g, H1, C1, g["L0_gnn_att1"], g["L0_gnn_bias1"], tabs[0], tabs[1], heads1)
            with ExitStack() as c2:
                rows = c2.enter_context(nc.sbuf_tensor("heads_rows", [P, T, HC], F32))
                bring_rows(nc, g, heads1, rows, HC)
                attention_tables(nc, g, rows, HC, 1, D, *[g[f"L0_gnn_{n}"] for n in ("W2l", "b2l", "W2r", "b2r", "att2")],
                                 tabs[2], tabs[3])
            attend(nc, g, 1, D, g["L0_gnn_att2"], g["L0_gnn_bias2"], tabs[2], tabs[3], heads2)
            bring_rows(nc, g, heads2, g["H"], D)
            add_rows(nc, g, g["H"])
            normalise(nc, g)
            aggregate(nc, g, g["L1_gnn_W1"], g["L1_gnn_b1"], relu=True)
            aggregate(nc, g, g["L1_gnn_W2"], g["L1_gnn_b2"], relu=True)
            aggregate(nc, g, g["L1_gnn_W3"], g["L1_gnn_b3"], add_to_x=True)
        normalise(nc, g)
        pair_softmax(nc, g)
        normalise(nc, g)
        features, sums = s.dram("FEATURES", [NP, D]), s.dram("SUMS", [NP, D])
        store_rows(nc, g, features)
        edge_sums(nc, g, features, sums)
        with ExitStack() as c3:
            rows = c3.enter_context(nc.sbuf_tensor("sum_rows", [P, T, D], F32))
            bring_rows(nc, g, sums, rows, D)
            output_layer(nc, g, rows)


def kernel(**inputs):
    import numpy as np
    import concourse.bacc as bacc
    from concourse.bass_utils import run_bass_kernel_spmd

    def padded(name, rows, value=0):
        a = np.asarray(inputs[name])
        out = np.full((rows,) + a.shape[1:], value, a.dtype)
        out[:a.shape[0]] = a
        return out

    arrays = {"x": padded("x", NP), "src": padded("src", ER), "dst": padded("dst", ER, NO_NODE),
              "edge_weight": padded("edge_weight", ER), "edge_attr_64": padded("edge_attr_64", ER)}
    for name in inputs:
        if name.startswith("L"):
            arrays[name] = np.ascontiguousarray(np.asarray(inputs[name]))
    arrays["L3_gnn_eps"] = arrays["L3_gnn_eps"].reshape(1)
    arrays["L3_gnn_W_T"] = np.ascontiguousarray(arrays.pop("L3_gnn_W").T)
    nc = bacc.Bacc("TRN2", target_bir_lowering=False, num_devices=1)
    io = {k: nc.dram_tensor(f"in_{k}", a.shape, mybir.dt.from_np(a.dtype), kind="ExternalInput").ap()
          for k, a in arrays.items()}
    io["out"] = nc.dram_tensor("out_x", (N, D), F32, kind="ExternalOutput").ap()
    build(nc, io)
    r = run_bass_kernel_spmd(nc, [{f"in_{k}": a for k, a in arrays.items()}], core_ids=[0])
    return r.results[0]["out_x"]
```

```python
import math
from contextlib import ExitStack

import concourse.bass as bass
from concourse import mybir

F32 = mybir.dt.float32
BF16 = mybir.dt.bfloat16
I32 = mybir.dt.int32
ALU = mybir.AluOpType
ACT = mybir.ActivationFunctionType
AX = mybir.AxisListType

P = 128
N = 3125
E = 103125
D = 64
H1, C1 = 12, 12
HC = H1 * C1
T = -(-N // P)
NP = T * P
EC = -(-E // P)
EP = EC * P
ER = EP + P
NO_NODE = 4095
S = 32
B = 8
SB = S // B
GB = B + 1
Q = 4
BQ = B // Q
GS = SB * GB
NO_ROW = NP
RING = 4
U = E // S + T + E // (P * S) + 4
OFF = NP * NP
BIG = 1.0e30
HG = 13
KEY_DEG = 4000


class Steps:

    def __init__(self, eng, sem, base=0):
        self.eng, self.sem, self.base, self.n = eng, sem, base, 0

    def mark(self, ins):
        ins.then_inc(self.sem, 1)
        self.n += 1

    def wait(self):
        self.eng.wait_ge(self.sem, self.base + self.n)

    def after(self, ins):
        self.mark(ins)
        self.wait()


def wait_count(eng, sem, count, turns):
    eng.wait_ge(sem, count)
    eng.sem_inc(turns, 1)


def free_bcast(ap, before, after):
    a = ap
    if before:
        a = a.unsqueeze(1)
        a = a.to_broadcast([a.shape[0], before] + list(a.shape[2:]))
    if after:
        a = a.unsqueeze(len(a.shape))
        a = a.to_broadcast(list(a.shape[:-1]) + [after])
    return a


class Scope:

    def __init__(self, nc, ctx):
        self.nc, self.ctx, self.id = nc, ctx, nc.next_id()
        self.sems = []
        ctx.callback(self.release)

    def release(self):
        if self.sems:
            self.nc.clear_and_free_semaphores(self.sems)
            self.nc.all_engine_barrier()

    def sb(self, name, shape, dt=F32):
        return self.ctx.enter_context(self.nc.sbuf_tensor(f"{name}_{self.id}", list(shape), dt))

    def sem(self, name):
        self.sems.append(self.nc.alloc_semaphore(f"{name}_{self.id}"))
        return self.sems[-1]

    def dram(self, name, shape, dt=F32):
        return self.nc.dram_tensor(name, list(shape), dt, kind="Internal").ap()


def bank(g, i):
    return g["banks"][:, i, :]


def persistent(nc, ctx, io):
    s = Scope(nc, ctx)
    g = dict(io)
    g["banks"] = ctx.enter_context(nc.psum_tensor("banks", [P, 8, 512], F32))
    g["X"] = s.sb("X", [P, T, D])
    g["iota_f"] = s.sb("iota_f", [P, P])
    g["iota_b"] = s.sb("iota_b", [P, P], BF16)
    g["pcol"] = s.sb("pcol", [P, 1])
    g["ident"] = s.sb("ident", [P, P])
    g["ident_b"] = s.sb("ident_b", [P, P], BF16)
    g["ones"] = s.sb("ones", [P, P])
    g["deg"] = s.sb("deg", [P, T])
    g["ni"] = s.sb("ni", [P, T, 4])
    g["nid_i"] = s.sb("nid_i", [P, T + 1], I32)
    g["info"] = s.sb("info", [1, 5, T], I32)
    g["PAIR"] = s.dram("PAIR", [NP * NP, 2])
    g["MS"] = s.dram("MS", [NP, 2])
    g["NI"] = s.dram("NI", [NP, 4])
    g["SLOT"] = s.dram("SLOT", [P, (U + T) * 3 * S])
    g["GIDX"] = s.dram("GIDX", [P, (U + T) * GS], I32)
    g["H"] = s.sb("H", [P, T, D])
    g["dinv"] = s.sb("dinv", [P, T])
    g["mout"] = s.sb("mout", [P, T])
    g["rank_i"] = s.sb("rank_i", [P, T], I32)
    g["sout"] = s.sb("sout", [P, T])
    g["cmax"] = s.sb("cmax_all", [P, 1])
    g["pool_turns"] = s.sem("pool_turns")
    g["pe_turns"] = s.sem("pe_turns")
    g["act_turns"] = s.sem("act_turns")
    g["v_turns"] = s.sem("v_turns")
    g["sp_turns"] = s.sem("sp_turns")
    g["pair_fill"] = s.sem("pair_fill")
    return g


def prepare(nc, g):
    with ExitStack() as ctx:
        s = Scope(nc, ctx)
        fill = s.sb("fill", [P, NP, 2])
        dst_i = s.sb("dst_i", [P, EC], I32)
        part_i = s.sb("part_i", [P, 2, EC], I32)
        lo_b = s.sb("lo_b", [P, EC], BF16)
        hi_b = s.sb("hi_b", [P, EC], BF16)
        oh_lo = s.sb("oh_lo", [P, 2, HG, P], BF16)
        oh_hi = s.sb("oh_hi", [P, 2, HG, T], BF16)
        zero_b = s.sb("zero_b", [P, P], BF16)
        iota_i = s.sb("iota_i", [P, P], I32)
        pcol_i = s.sb("pcol_i", [P, 1], I32)
        node_i = s.sb("node_i", [P, T], I32)
        tri = s.sb("tri", [P, P])
        key = s.sb("key", [P, T])
        keyrow = s.sb("keyrow", [P, NP])
        dump_v = s.sb("dump_v", [P, NP], BF16)
        dump_a = s.sb("dump_a", [P, NP], BF16)
        greater = s.sb("greater", [P, T])
        sign_sum = s.sb("sign_sum", [P, T])
        rank_i = g["rank_i"]
        niw = s.sb("niw", [P, T, 4])
        small = s.sb("small", [P, 4, T])
        degs_c = s.sb("degs_c", [P, T])
        kcol = s.sb("kcol", [T, 1])
        krow = s.sb("krow", [1, T])
        krow_i = s.sb("krow_i", [1, 2, T], I32)
        row_f = s.sb("row_f", [1, 4, T])
        hist = bank(g, 0)
        pref = bank(g, 1)[:, 0:2 * T].rearrange("p (a t) -> p a t", a=2)
        kps = g["banks"][:, 2:4, :]
        kt = bank(g, 4)[:, 0:P]

        in_dst, in_x = s.sem("in_dst"), s.sem("in_x")
        fill_set = s.sem("fill_set")
        iotas = s.sem("iotas")
        v_steps = s.sem("v_steps")
        onehots_ready = [s.sem(f"onehots_ready{i}") for i in range(2)]
        oh_free = [s.sem(f"oh_free{i}") for i in range(2)]
        hist_done = s.sem("hist_done")
        consts_ready = s.sem("consts_ready")
        deg_ready, pref_done = s.sem("deg_ready"), s.sem("pref_done")
        key_ready, key_turned, key_copied = s.sem("key_ready"), s.sem("key_turned"), s.sem("key_copied")
        signs_done = s.sem("signs_done")
        ranks_ready, ni_written, ni_read = s.sem("ranks_ready"), s.sem("ni_written"), s.sem("ni_read")
        k_ready, k_turned = s.sem("k_ready"), s.sem("k_turned")
        block = ctx.enter_context(nc.Block())
        half_v = T // 2

        @block.sync
        def _(sp):
            sp.dma_start(dst_i[:, :], g["dst"][0:EP].rearrange("(p c) -> p c", p=P)).then_inc(in_dst, 16)
            sp.dma_start(g["X"][:, :, :], g["x"].rearrange("(t p) f -> p t f", p=P)).then_inc(in_x, 16)
            sp.wait_ge(fill_set, 2)
            pair = g["PAIR"].rearrange("(t p d) c -> t p (d c)", t=T, p=P)
            for t in range(T):
                sp.dma_start(pair[t], fill[:, :, :].rearrange("p d c -> p (d c)"),
                             max_dma_last_dim=8192).then_inc(g["pair_fill"], 16)
            sp.wait_ge(ni_written, 16 * T)
            sp.dma_start(g["ni"][:, :, :], g["NI"].rearrange("(t p) c -> p t c", p=P)).then_inc(ni_read, 16)
            sp.wait_ge(in_x, 16)
            sp.wait_ge(g["pair_fill"], 16 * T)

        @block.gpsimd
        def _(pool):
            pool.iota(iota_i[:, :], [[1, P]], base=0, channel_multiplier=0).then_inc(iotas, 1)
            pool.iota(pcol_i[:, :], [[0, 1]], base=0, channel_multiplier=1).then_inc(iotas, 1)
            pool.iota(node_i[:, :], [[P, T]], base=0, channel_multiplier=1).then_inc(iotas, 1)
            pool.memset(fill[:, :, 0], 0.0).then_inc(fill_set, 1)
            pool.memset(fill[:, :, 1], -BIG).then_inc(fill_set, 1)
            pool.wait_ge(ranks_ready, 1)
            for t in range(T):
                pool.indirect_dma_start(g["NI"], bass.IndirectOffsetOnAxis(ap=rank_i[:, t:t + 1], axis=0),
                                        niw[:, t, :], None).then_inc(ni_written, 16)

        @block.tensor
        def _(pe):
            pe.wait_ge(consts_ready, 1)
            pe.matmul(hist[:, 0:T], zero_b[:, :], zero_b[:, 0:T], start=True, stop=False, skip_group_check=True)
            with pe.Fori(0, EC // (2 * HG)) as b:
                for i in range(2):
                    pe.wait_ge(onehots_ready[i], 2 * b + 2)
                    for c in range(HG):
                        mm = pe.matmul(hist[:, 0:T], oh_lo[:, i, c, :], oh_hi[:, i, c, :], start=False, stop=False,
                                       skip_group_check=True)
                    mm.then_inc(oh_free[i], 1)
            pe.matmul(hist[:, 0:T], zero_b[:, :], zero_b[:, 0:T], start=False, stop=True,
                      skip_group_check=True).then_inc(hist_done, 1)
            pe.wait_ge(deg_ready, 1)
            pe.matmul(pref[:, 0, :], tri[:, :], g["deg"][:, :], start=True, stop=True)
            pe.matmul(pref[:, 1, :], g["ones"][:, :], g["deg"][:, :], start=True, stop=True).then_inc(pref_done, 1)
            pe.wait_ge(key_ready, 1)
            for t in range(T):
                if t >= 8 and t % 4 == 0:
                    pe.wait_ge(key_copied, t // 4 - 1)
                mm = pe.transpose(kps[:, (t // 4) % 2, (t % 4) * P:(t % 4 + 1) * P],
                                  key[:, t:t + 1].to_broadcast([P, P]), g["ident"][:, :])
                if t % 4 == 3 or t == T - 1:
                    mm.then_inc(key_turned, 1)
            pe.wait_ge(k_ready, 1)
            pe.transpose(kt[0:T, :], degs_c[:, :], g["ident"][:, :]).then_inc(k_turned, 1)
            pe.wait_ge(k_ready, 2)
            pe.transpose(pref[0:1, 0, :], kcol[:, :], g["ident"][0:T, 0:T]).then_inc(k_turned, 1)

        @block.scalar
        def _(act):
            for j in range(-(-T // 4)):
                act.wait_ge(key_turned, j + 1)
                w = min(4, T - 4 * j) * P
                act.copy(keyrow[:, 4 * j * P:4 * j * P + w], kps[:, j % 2, 0:w]).then_inc(key_copied, 1)
            act.wait_ge(key_copied, -(-T // 4))
            for t in range(half_v, T):
                act.activation(dump_a[:, :], keyrow[:, :], ACT.Sign, bias=key[:, t:t + 1], scale=-1.0,
                               accum_out=sign_sum[:, t:t + 1]).then_inc(signs_done, 1)
                act.wait_ge(signs_done, t - half_v + 1)

        @block.vector
        def _(dve):
            st = Steps(dve, v_steps)
            dve.wait_ge(iotas, 3)
            st.mark(dve.memset(zero_b[:, :], 0.0))
            st.mark(dve.memset(g["ones"][:, :], 1.0))
            st.mark(dve.tensor_copy(g["iota_f"][:, :], iota_i[:, :]))
            st.mark(dve.tensor_copy(g["iota_b"][:, :], iota_i[:, :]))
            st.after(dve.tensor_copy(g["pcol"][:, :], pcol_i[:, :]))
            st.mark(dve.tensor_scalar(tri[:, :], g["iota_f"][:, :], g["pcol"][:, 0:1], None, ALU.is_gt))
            st.mark(dve.tensor_scalar(g["ident"][:, :], g["iota_f"][:, :], g["pcol"][:, 0:1], None, ALU.is_equal))
            st.after(dve.tensor_scalar(g["ident_b"][:, :], g["iota_f"][:, :], g["pcol"][:, 0:1], None, ALU.is_equal))
            dve.sem_inc(consts_ready, 1)
            dve.wait_ge(in_dst, 16)
            st.mark(dve.tensor_scalar(part_i[:, 0, :], dst_i[:, :], P - 1, None, ALU.bitwise_and))
            st.after(dve.tensor_scalar(part_i[:, 1, :], dst_i[:, :], int(math.log2(P)), None, ALU.logical_shift_right))
            st.mark(dve.tensor_copy(lo_b[:, :], part_i[:, 0, :]))
            st.after(dve.tensor_copy(hi_b[:, :], part_i[:, 1, :]))
            for i in range(2):
                dve.sem_inc(oh_free[i], 1)
            with dve.Fori(0, EC // (2 * HG)) as b:
                for i in range(2):
                    dve.wait_ge(oh_free[i], b + 1)
                    dve.tensor_tensor(oh_lo[:, i], free_bcast(lo_b[:, bass.ds(b * 2 * HG + i * HG, HG)], 0, P),
                                      free_bcast(g["iota_b"][:, :], HG, 0), ALU.is_equal).then_inc(onehots_ready[i], 1)
                    dve.tensor_tensor(oh_hi[:, i], free_bcast(hi_b[:, bass.ds(b * 2 * HG + i * HG, HG)], 0, T),
                                      free_bcast(g["iota_b"][:, 0:T], HG, 0), ALU.is_equal).then_inc(onehots_ready[i], 1)
            dve.wait_ge(hist_done, 1)
            st.mark(dve.tensor_copy(g["deg"][:, :], hist[:, 0:T]))
            st.after(dve.tensor_copy(small[:, 3, :], node_i[:, :]))
            dve.sem_inc(deg_ready, 1)
            st.mark(dve.tensor_scalar(key[:, :], g["deg"][:, :], float(KEY_DEG), 4096.0, ALU.min, ALU.mult))
            st.after(dve.tensor_scalar(small[:, 0, :], small[:, 3, :], -1.0, 4095.0, ALU.mult, ALU.add))
            st.after(dve.tensor_tensor(key[:, :], key[:, :], small[:, 0, :], ALU.add))
            dve.sem_inc(key_ready, 1)
            dve.wait_ge(pref_done, 1)
            st.mark(dve.tensor_copy(niw[:, :, 0], small[:, 3, :]))
            st.mark(dve.tensor_copy(niw[:, :, 2], g["deg"][:, :]))
            st.mark(dve.memset(niw[:, :, 3], 0.0))
            st.after(dve.tensor_copy(small[:, 1, :], pref[:, 1, :]))
            st.after(dve.tensor_tensor_scan(small[:, 2, :], g["ones"][:, 0:T], small[:, 1, :], 0.0, ALU.mult, ALU.add))
            st.after(dve.tensor_tensor(small[:, 2, :], small[:, 2, :], small[:, 1, :], ALU.subtract))
            st.after(dve.tensor_tensor(niw[:, :, 1], small[:, 2, :], pref[:, 0, :], ALU.add))
            dve.wait_ge(key_copied, -(-T // 4))
            for t in range(half_v):
                st.after(dve.tensor_scalar(dump_v[:, :], keyrow[:, :], key[:, t:t + 1], 0.0, ALU.is_gt, ALU.add,
                                           accum_out=greater[:, t:t + 1]))
            dve.wait_ge(signs_done, T - half_v)
            st.after(dve.tensor_scalar(greater[:, half_v:T], sign_sum[:, half_v:T], -0.5, 0.5 * (NP - 1),
                                       ALU.mult, ALU.add))
            st.after(dve.tensor_copy(rank_i[:, :], greater[:, :]))
            dve.sem_inc(ranks_ready, 1)
            dve.wait_ge(ni_read, 16)
            st.mark(dve.memset(g["nid_i"][:, T:], 0))
            st.mark(dve.tensor_copy(g["nid_i"][:, 0:T], g["ni"][:, :, 0]))
            st.after(dve.tensor_copy(degs_c[:, :], g["ni"][:, :, 2]))
            dve.sem_inc(k_ready, 1)
            dve.wait_ge(k_turned, 1)
            st.after(dve.tensor_reduce(kcol[:, :], kt[0:T, :], AX.X, ALU.max))
            dve.sem_inc(k_ready, 1)
            dve.wait_ge(k_turned, 2)
            st.after(dve.tensor_copy(krow[:, :], pref[0:1, 0, :]))
            for i, size in enumerate((B, S)):
                st.after(dve.tensor_scalar(row_f[:, i, :], krow[:, :], 1.0, float(size - 1), ALU.max, ALU.add))
                st.after(dve.tensor_copy(krow_i[:, i, :], row_f[:, i, :]))
                st.after(dve.tensor_scalar(g["info"][:, i, :], krow_i[:, i, :], int(math.log2(size)), None,
                                           ALU.logical_shift_right))
                st.after(dve.tensor_copy(row_f[:, i, :], g["info"][:, i, :]))
                st.after(dve.tensor_tensor_scan(row_f[:, 2 + i, :], g["ones"][0:1, 0:T], row_f[:, i, :], 0.0,
                                                ALU.mult, ALU.add))
                st.after(dve.tensor_tensor(row_f[:, 2 + i, :], row_f[:, 2 + i, :], row_f[:, i, :], ALU.subtract))
                st.after(dve.tensor_copy(g["info"][:, 2 + i, :], row_f[:, 2 + i, :]))
            st.after(dve.tensor_reduce(krow[:, 0:1], row_f[:, 1, :], AX.X, ALU.max))
            st.after(dve.memset(g["info"][:, 4, :], 0))
            st.after(dve.tensor_copy(g["info"][:, 4, 0:1], krow[:, 0:1]))


def fill_slots(nc, g):
    with ExitStack() as ctx:
        s = Scope(nc, ctx)
        start_f = s.sb("start_f", [P, T])
        rem = s.sb("rem", [P, T])
        start_i = s.sb("start_i", [P, T], I32)
        srun = s.sb("srun", [P, T, S], I32)
        wrun = s.sb("wrun", [P, T, S])
        slot = s.sb("slot", [P, T, 3, S])
        place = s.sb("place", [P, S])
        gidx = s.sb("gidx", [P, T, SB, GB], I32)
        first_f = s.sb("first_f", [P, T, SB])
        blk = s.sb("blk", [P, SB])
        valid = s.sb("valid", [P, T, S])
        inval = s.sb("inval", [P, T, S])
        tmp = s.sb("tmp", [P, T, S])
        ubase = s.sb("ubase", [1, 6, T])
        u_i = s.sb("u_i", [1, T], I32)
        soft = s.sb("soft", [P, 4, T])
        expd = s.sb("expd", [P, T * S + T])
        msw = s.sb("msw", [P, T, 2])
        v_steps = s.sem("v2_steps")
        exp_in, exp_out = s.sem("exp_in"), s.sem("exp_out")
        ms_ready, ms_out = s.sem("ms_ready"), s.sem("ms_out")
        starts_ready, runs_in = s.sem("starts_ready"), s.sem("runs_in")
        slots_ready, slots_out = s.sem("slots_ready"), s.sem("slots_out")
        block = ctx.enter_context(nc.Block())
        NSTEP = 29

        @block.gpsimd
        def _(pool):
            rounds = pool.value_load(g["info"][0:1, 4, 0:1], min_val=1, max_val=U)
            with pool.Fori(0, rounds) as r:
                wait_count(pool, starts_ready, r + 1, g["pool_turns"])
                for t in range(T):
                    at = bass.IndirectOffsetOnAxis(ap=start_i[:, t:t + 1], axis=0)
                    pool.indirect_dma_start(srun[:, t, :], None, g["src"].unsqueeze(1), at).then_inc(runs_in, 16)
                    pool.indirect_dma_start(wrun[:, t, :], None, g["edge_weight"].unsqueeze(1), at).then_inc(runs_in, 16)
            pool.wait_ge(ms_ready, 2)
            for t in range(T):
                pool.indirect_dma_start(g["MS"], bass.IndirectOffsetOnAxis(ap=g["nid_i"][:, t:t + 1], axis=0),
                                        msw[:, t, :], None).then_inc(ms_out, 16)
            pool.wait_ge(ms_out, 16 * T)

        @block.scalar
        def _(act):
            rounds = act.value_load(g["info"][0:1, 4, 0:1], min_val=1, max_val=U)
            with act.Fori(0, rounds) as r:
                act.wait_ge(exp_in, r + 1)
                act.activation(expd[:, :], expd[:, :], ACT.Exp).then_inc(exp_out, 1)

        @block.vector
        def _(dve):
            st = Steps(dve, v_steps)
            rounds = dve.value_load(g["info"][0:1, 4, 0:1], min_val=1, max_val=U)
            st.mark(dve.tensor_copy(start_f[:, :], g["ni"][:, :, 1]))
            st.mark(dve.tensor_copy(rem[:, :], g["ni"][:, :, 2]))
            st.mark(dve.tensor_copy(ubase[:, 0:2, :], g["info"][:, 1:4:2, :]))
            st.mark(dve.memset(ubase[:, 2, :], 0.0))
            st.mark(dve.tensor_scalar(ubase[:, 5, :], g["iota_f"][0:1, 0:T], float(U), None, ALU.add))
            st.mark(dve.tensor_scalar(blk[:, :], g["iota_f"][:, 0:SB], float(B), None, ALU.mult))
            st.after(dve.tensor_scalar(place[:, :], g["iota_f"][:, 0:S], 1.0, None, ALU.add))
            st.mark(dve.memset(soft[:, 0, :], -BIG))
            st.after(dve.memset(soft[:, 1, :], 0.0))
            first = st.n
            dve.sem_inc(slots_out, 1)
            with dve.Fori(0, rounds) as r:
                st = Steps(dve, v_steps, r * NSTEP + first)
                dve.wait_ge(slots_out, r * (2 * T * 16) + 1)
                st.after(dve.tensor_scalar(start_i[:, :], start_f[:, :], float(E), None, ALU.min))
                st.after(dve.tensor_tensor(ubase[:, 3, :], ubase[:, 2, :], ubase[:, 0, :], ALU.is_lt))
                st.after(dve.tensor_scalar(ubase[:, 4, :], ubase[:, 3, :], -1.0, 1.0, ALU.mult, ALU.add))
                st.after(dve.tensor_tensor(ubase[:, 4, :], ubase[:, 4, :], ubase[:, 5, :], ALU.mult))
                dve.sem_inc(starts_ready, 1)
                st.after(dve.tensor_tensor(ubase[:, 3, :], ubase[:, 3, :], ubase[:, 1, :], ALU.mult))
                st.after(dve.tensor_tensor(u_i[:, :], ubase[:, 3, :], ubase[:, 4, :], ALU.add))
                st.mark(dve.tensor_tensor(valid[:, :, :], free_bcast(rem[:, :], 0, S),
                                          free_bcast(g["iota_f"][:, 0:S], T, 0), ALU.is_gt))
                st.mark(dve.tensor_copy(slot[:, :, 2, :], free_bcast(place[:, :], T, 0)))
                dve.wait_ge(runs_in, (r + 1) * (2 * T * 16))
                st.after(dve.tensor_copy(tmp[:, :, :], srun[:, :, :]))
                st.mark(dve.tensor_scalar(inval[:, :, :], valid[:, :, :], -1.0, None, ALU.add))
                st.after(dve.tensor_tensor(tmp[:, :, :], tmp[:, :, :], valid[:, :, :], ALU.mult))
                st.after(dve.tensor_tensor(slot[:, :, 0, :], tmp[:, :, :], inval[:, :, :], ALU.add))
                by_block = "p t (b k) -> p t b k"
                st.after(dve.scalar_tensor_tensor(out=gidx[:, :, :, 1:GB], in0=inval[:, :, :].rearrange(by_block, k=B),
                                                  scalar=-float(NO_ROW + 1),
                                                  in1=slot[:, :, 0, :].rearrange(by_block, k=B), op0=ALU.mult,
                                                  op1=ALU.add))
                st.after(dve.tensor_tensor(first_f[:, :, :], free_bcast(start_f[:, :], 0, SB), free_bcast(blk[:, :], T, 0),
                                           ALU.add))
                st.after(dve.tensor_scalar(gidx[:, :, :, 0], first_f[:, :, :], float(E), None, ALU.min))
                st.after(dve.tensor_tensor(tmp[:, :, :], wrun[:, :, :], valid[:, :, :], ALU.mult))
                st.after(dve.scalar_tensor_tensor(out=slot[:, :, 1, :], in0=inval[:, :, :], scalar=BIG,
                                                  in1=tmp[:, :, :], op0=ALU.mult, op1=ALU.add))
                dve.sem_inc(slots_ready, 1)
                st.mark(dve.tensor_scalar(start_f[:, :], start_f[:, :], float(S), None, ALU.add))
                st.mark(dve.tensor_scalar(rem[:, :], rem[:, :], -float(S), None, ALU.add))
                st.mark(dve.tensor_scalar(place[:, :], place[:, :], float(S), None, ALU.add))
                st.mark(dve.tensor_scalar(ubase[:, 1:3, :], ubase[:, 1:3, :], 1.0, None, ALU.add))
                weights = slot[:, :, 1, :]
                sums = expd[:, 0:T * S].rearrange("p (t k) -> p t k", k=S)
                st.after(dve.tensor_reduce(soft[:, 2, :], weights, AX.X, ALU.max))
                st.after(dve.tensor_tensor(soft[:, 2, :], soft[:, 2, :], soft[:, 0, :], ALU.max))
                st.mark(dve.tensor_tensor(expd[:, T * S:], soft[:, 0, :], soft[:, 2, :], ALU.subtract))
                st.after(dve.tensor_tensor(sums, weights, free_bcast(soft[:, 2, :], 0, S), ALU.subtract))
                dve.sem_inc(exp_in, 1)
                dve.wait_ge(exp_out, r + 1)
                st.mark(dve.tensor_copy(soft[:, 0, :], soft[:, 2, :]))
                st.mark(dve.tensor_reduce(soft[:, 3, :], sums, AX.X, ALU.add))
                st.after(dve.tensor_tensor(soft[:, 1, :], soft[:, 1, :], expd[:, T * S:], ALU.mult))
                st.after(dve.tensor_tensor(soft[:, 1, :], soft[:, 1, :], soft[:, 3, :], ALU.add))
                assert st.n == NSTEP, st.n
            dve.tensor_copy(msw[:, :, 0], soft[:, 0, :]).then_inc(ms_ready, 1)
            dve.tensor_copy(msw[:, :, 1], soft[:, 1, :]).then_inc(ms_ready, 1)

        @block.sync
        def _(sp):
            rounds = sp.value_load(g["info"][0:1, 4, 0:1], min_val=1, max_val=U)
            with sp.Fori(0, rounds) as r:
                wait_count(sp, slots_ready, r + 1, g["sp_turns"])
                for t in range(T):
                    u = sp.value_load(u_i[0:1, t:t + 1], min_val=0, max_val=U + T - 1)
                    sp.dma_start(g["SLOT"][:, bass.ds(u * (3 * S), 3 * S)],
                                 slot[:, t].rearrange("p c k -> p (c k)")).then_inc(slots_out, 16)
                    sp.dma_start(g["GIDX"][:, bass.ds(u * GS, GS)],
                                 gidx[:, t].rearrange("p b k -> p (b k)")).then_inc(slots_out, 16)
            wait_count(sp, slots_out, rounds * (2 * T * 16) + 1, g["sp_turns"])


def scatter_pairs(nc, g):
    with ExitStack() as ctx:
        s = Scope(nc, ctx)
        a = s.sb("sa", [P, 3, S])
        b = s.sb("sbb", [P, 3, S])
        differs = s.sb("differs", [P, S, S], BF16)
        zero_b = s.sb("sz", [P, P], BF16)
        places = s.sb("places", [P, 1])
        counted, counted_later = bank(g, 0)[:, 0:S], bank(g, 1)[:, 0:S]
        ex = s.sb("ex", [P, S * S + S])
        acc = s.sb("acc", [P, 2, S])
        new = s.sb("new", [P, 2, S])
        edges = s.sb("edges", [P, S])
        fin = s.sb("fin", [P, 4, S])
        dcol = s.sb("dcol", [P, 1])
        lns = s.sb("lns", [P, S])
        pair = s.sb("pair", [P, 2, S, 2])
        pair_at = s.sb("pair_at", [P, 2, S], I32)
        opened = s.sb("opened", [P, 2, 2])
        cmax = s.sb("cmax", [P, S])
        a_in, b_in, a_free, b_free = s.sem("a_in"), s.sem("b_in"), s.sem("a_free"), s.sem("b_free")
        tile_steps, sup_steps, pair_steps = s.sem("tile_steps"), s.sem("sup_steps"), s.sem("pair_steps")
        ex_in, ex_out, ln_in, ln_out = s.sem("ex_in"), s.sem("ex_out"), s.sem("ln_in"), s.sem("ln_out")
        entries_ready, entries_written = s.sem("entries_ready"), s.sem("entries_written")
        differs_ready, differs_free = s.sem("differs_ready"), s.sem("differs_free")
        counts_ready, counts_free, zero_ready = s.sem("counts_ready"), s.sem("counts_free"), s.sem("zero_ready")
        first_out, rest_out = s.sem("first_out"), s.sem("rest_out")
        block = ctx.enter_context(nc.Block())
        T_STEPS, U_STEPS, Q_STEPS = 1, 13, 11

        def sizes(eng, t):
            return (eng.value_load(g["info"][0:1, 1, bass.ds(t, 1)], min_val=1, max_val=U),
                    eng.value_load(g["info"][0:1, 3, bass.ds(t, 1)], min_val=0, max_val=U))

        @block.sync
        def _(sp):
            pairs = sp.alloc_register("sp_pairs")
            sp.reg_mov(pairs, 0)
            with sp.Fori(0, T) as t:
                rounds, base = sizes(sp, t)
                with sp.Fori(0, rounds) as r:
                    wait_count(sp, a_free, base + r + 1, g["sp_turns"])
                    sp.dma_start(a[:, :, :].rearrange("p c k -> p (c k)"),
                                 g["SLOT"][:, bass.ds(nc.s_assert_within(base + r, 0, U, skip_runtime_bounds_check_because="the tables are sized for it") * (3 * S), 3 * S)]).then_inc(a_in, 16)
                    with sp.Fori(0, rounds) as q:
                        n = sp.snap(pairs, min_val=0, max_val=1 << 23)
                        wait_count(sp, b_free, n + 1, g["sp_turns"])
                        sp.dma_start(b[:, :, :].rearrange("p c k -> p (c k)"),
                                     g["SLOT"][:, bass.ds(nc.s_assert_within(base + q, 0, U, skip_runtime_bounds_check_because="the tables are sized for it") * (3 * S), 3 * S)]).then_inc(b_in, 16)
                        sp.reg_add(pairs, pairs, 1)

        @block.vector
        def _(dve):
            pairs = dve.alloc_register("v_pairs")
            dve.reg_mov(pairs, 0)
            dve.sem_inc(a_free, 1)
            dve.sem_inc(b_free, 1)
            dve.sem_inc(entries_written, 1)
            dve.sem_inc(differs_free, 1)
            dve.sem_inc(counts_free, 1)
            dve.memset(zero_b[:, :], 0.0).then_inc(zero_ready, 1)
            dve.memset(cmax[:, :], 0.0).then_inc(tile_steps, 1)
            with dve.Fori(0, T) as t:
                rounds, base = sizes(dve, t)
                st = Steps(dve, tile_steps, t * T_STEPS + 1)
                st.after(dve.tensor_copy(dcol[:, :], g["ni"][:, bass.ds(t, 1), 0]))
                assert st.n == T_STEPS
                dve.sem_inc(g["v_turns"], 1)
                with dve.Fori(0, rounds) as r:
                    st = Steps(dve, sup_steps, (base + r) * U_STEPS)
                    st.mark(dve.memset(acc[:, 0, :], -BIG))
                    st.after(dve.memset(acc[:, 1, :], 0.0))
                    wait_count(dve, a_in, (base + r) * 16 + 16, g["v_turns"])
                    with dve.Fori(0, rounds) as q:
                        n = dve.snap(pairs, min_val=0, max_val=1 << 23)
                        sq = Steps(dve, pair_steps, n * Q_STEPS)
                        t_ex = ex[:, 0:S * S].rearrange("p (j k) -> p j k", k=S)
                        wait_count(dve, b_in, n * 16 + 16, g["v_turns"])
                        dve.wait_ge(differs_free, n + 1)
                        sq.after(dve.tensor_tensor(differs[:, :, :], free_bcast(a[:, 0, :], 0, S),
                                                   free_bcast(b[:, 0, :], S, 0), ALU.not_equal))
                        dve.sem_inc(differs_ready, 1)
                        sq.mark(dve.tensor_copy(places[:, :], b[:, 2, S - 1:S]))
                        sq.after(dve.scalar_tensor_tensor(out=t_ex, in0=differs[:, :, :], scalar=-BIG,
                                                          in1=free_bcast(b[:, 1, :], S, 0), op0=ALU.mult, op1=ALU.add))
                        dve.sem_inc(b_free, 1)
                        sq.after(dve.tensor_reduce(new[:, 0, :], t_ex, AX.X, ALU.max))
                        sq.after(dve.tensor_tensor(new[:, 0, :], acc[:, 0, :], new[:, 0, :], ALU.max))
                        sq.mark(dve.tensor_tensor(t_ex, t_ex, free_bcast(new[:, 0, :], 0, S), ALU.subtract))
                        sq.after(dve.tensor_tensor(ex[:, S * S:], acc[:, 0, :], new[:, 0, :], ALU.subtract))
                        dve.sem_inc(ex_in, 1)
                        sq.mark(dve.tensor_copy(acc[:, 0, :], new[:, 0, :]))
                        dve.wait_ge(ex_out, n + 1)
                        sq.mark(dve.tensor_reduce(new[:, 1, :], t_ex, AX.X, ALU.add))
                        sq.after(dve.tensor_tensor(acc[:, 1, :], acc[:, 1, :], ex[:, S * S:], ALU.mult))
                        sq.after(dve.tensor_tensor(acc[:, 1, :], acc[:, 1, :], new[:, 1, :], ALU.add))
                        assert sq.n == Q_STEPS, sq.n
                        dve.reg_add(pairs, pairs, 1)
                    dve.sem_inc(ln_in, 1)
                    st.mark(dve.tensor_scalar(fin[:, 1, :], a[:, 0, :], 0.0, None, ALU.is_ge))
                    st.mark(dve.tensor_scalar(fin[:, 2, :], a[:, 0, :], float(NP), dcol[:, 0:1], ALU.mult, ALU.add))
                    dve.wait_ge(counts_ready, base + r + 1)
                    st.mark(dve.tensor_scalar(edges[:, :], counted, -1.0, places[:, 0:1], ALU.mult, ALU.add))
                    st.after(dve.tensor_tensor(fin[:, 0, :], counted_later, a[:, 2, :], ALU.add))
                    dve.sem_inc(a_free, 1)
                    dve.sem_inc(counts_free, 1)
                    st.mark(dve.tensor_tensor(cmax[:, :], cmax[:, :], edges[:, :], ALU.max))
                    st.after(dve.tensor_scalar(fin[:, 0, :], fin[:, 0, :], places[:, 0:1], None, ALU.is_equal))
                    st.after(dve.tensor_tensor(fin[:, 0, :], fin[:, 0, :], fin[:, 1, :], ALU.mult))
                    st.after(dve.scalar_tensor_tensor(out=fin[:, 2, :], in0=fin[:, 2, :], scalar=-float(OFF),
                                                      in1=fin[:, 0, :], op0=ALU.add, op1=ALU.mult))
                    n = base + r
                    dve.wait_ge(entries_written, n + 1)
                    st.mark(dve.tensor_scalar(pair_at[:, bass.ds(n & 1, 1), :].squeeze(1), fin[:, 2, :], float(OFF),
                                              None, ALU.add))
                    st.mark(dve.tensor_copy(pair[:, bass.ds(n & 1, 1), :, 0].squeeze(1), edges[:, :]))
                    dve.wait_ge(ln_out, n + 1)
                    st.after(dve.tensor_tensor(pair[:, bass.ds(n & 1, 1), :, 1].squeeze(1), acc[:, 0, :], lns[:, :],
                                               ALU.add))
                    dve.sem_inc(entries_ready, 1)
                    assert st.n == U_STEPS, st.n
            st = Steps(dve, tile_steps, T * T_STEPS + 1)
            st.after(dve.tensor_reduce(g["cmax"][:, :], cmax[:, :], AX.X, ALU.max))

        @block.tensor
        def _(pe):
            pairs = pe.alloc_register("pe_pairs")
            pe.reg_mov(pairs, 0)

            def count(out, upto):
                for k in range(S):
                    if upto(k):
                        pe.matmul(out[:, 0:upto(k)], g["ident_b"][:, :], differs[:, 0:upto(k), k], start=False,
                                  stop=False, skip_group_check=True)

            pe.wait_ge(zero_ready, 1)
            with pe.Fori(0, T) as t:
                rounds, base = sizes(pe, t)
                with pe.Fori(0, rounds) as r:
                    wait_count(pe, counts_free, base + r + 1, g["pe_turns"])
                    for out in (counted, counted_later):
                        pe.matmul(out, zero_b[:, :], zero_b[:, 0:S], start=True, stop=False, skip_group_check=True)
                    with pe.Fori(0, rounds) as q:
                        n = pe.snap(pairs, min_val=0, max_val=1 << 23)
                        wait_count(pe, differs_ready, n + 1, g["pe_turns"])
                        count(counted, lambda k: S)
                        with pe.If(q > r):
                            count(counted_later, lambda k: S)
                        with pe.Else():
                            with pe.If(r > q):
                                pe.sem_inc(g["pe_turns"], 1)
                            with pe.Else():
                                count(counted_later, lambda k: k)
                            pe.sem_inc(g["pe_turns"], 1)
                        pe.matmul(counted, zero_b[:, :], zero_b[:, 0:S], start=False, stop=False,
                                  skip_group_check=True).then_inc(differs_free, 1)
                        pe.reg_add(pairs, pairs, 1)
                    for out in (counted, counted_later):
                        mm = pe.matmul(out, zero_b[:, :], zero_b[:, 0:S], start=False, stop=True, skip_group_check=True)
                    mm.then_inc(counts_ready, 1)

        @block.scalar
        def _(act):
            pairs = act.alloc_register("a_pairs")
            act.reg_mov(pairs, 0)
            with act.Fori(0, T) as t:
                rounds, base = sizes(act, t)
                with act.Fori(0, rounds) as r:
                    with act.Fori(0, rounds) as q:
                        n = act.snap(pairs, min_val=0, max_val=1 << 23)
                        act.wait_ge(ex_in, n + 1)
                        act.activation(ex[:, :], ex[:, :], ACT.Exp).then_inc(ex_out, 1)
                        act.reg_add(pairs, pairs, 1)
                    act.wait_ge(ln_in, base + r + 1)
                    act.activation(lns[:, :], acc[:, 1, :], ACT.Ln).then_inc(ln_out, 1)

        @block.gpsimd
        def _(pool):
            rest = pool.alloc_register("rest_count")
            pool.reg_mov(rest, 16)

            def scatter(n, k, blocks, r):
                wait_count(pool, first_out, n * (B * 16) + 16, g["pool_turns"])
                for j in range(SB):
                    with pool.If(blocks > r * SB + j):
                        for c in range(B * j, B * j + B):
                            at = bass.IndirectOffsetOnAxis(ap=pair_at[:, k, c:c + 1], axis=0)
                            pool.indirect_dma_start(g["PAIR"], at, pair[:, k, c, :], None, bounds_check=OFF - 1,
                                                    oob_is_err=False).then_inc(rest_out if j else first_out, 16)
                        if j:
                            pool.reg_add(rest, rest, B * 16)
                    if j == 0:
                        wait_count(pool, rest_out, pool.snap(rest, min_val=16, max_val=1 << 30), g["pool_turns"])
                        pool.sem_inc(entries_written, 1)

            for i, sem in enumerate((first_out, rest_out)):
                at = bass.IndirectOffsetOnAxis(ap=g["nid_i"][:, 0:1], axis=0)
                pool.indirect_dma_start(opened[:, i, :], None, g["MS"], at).then_inc(sem, 16)
            with pool.Fori(0, T) as t:
                rounds, base = sizes(pool, t)
                blocks = pool.value_load(g["info"][0:1, 0, bass.ds(t, 1)], min_val=1, max_val=SB * U)
                with pool.Fori(0, rounds) as r:
                    n = base + r
                    wait_count(pool, entries_ready, n + 1, g["pool_turns"])
                    with pool.If((n & 1) < 1):
                        scatter(n, 0, blocks, r)
                    with pool.Else():
                        scatter(n, 1, blocks, r)
            rounds, base = sizes(pool, T - 1)
            wait_count(pool, first_out, (base + rounds) * (B * 16) + 16, g["pool_turns"])
            wait_count(pool, rest_out, pool.snap(rest, min_val=16, max_val=1 << 30), g["pool_turns"])


CH = 3
NCH = (T - 1) // CH
assert T == NCH * CH + 1


def read_pairs(nc, g):
    with ExitStack() as ctx:
        s = Scope(nc, ctx)
        half = NP // 2
        rows = [s.sb(f"rows{h}", [P, half, 2]) for h in range(2)]
        top = [s.sb(f"top{h}", [P, 2]) for h in range(2)]
        part = [s.sb(f"part{h}", [P, 1]) for h in range(2)]
        tops = s.sb("tops", [P, 2, T])
        sums = s.sb("sums", [P, 2, T])
        spread = s.sb("spread", [P, 2, T])
        dump = s.sb("dump", [P, half], BF16)
        rows_in = [s.sem(f"rows_in{h}") for h in range(2)]
        rows_free = [s.sem(f"rows_free{h}") for h in range(2)]
        top_ready = [s.sem(f"top_ready{h}") for h in range(2)]
        part_ready = [s.sem(f"part_ready{h}") for h in range(2)]
        v_steps = s.sem("v4_steps")
        spread_in, spread_out = s.sem("spread_in"), s.sem("spread_out")
        block = ctx.enter_context(nc.Block())
        pairs = g["PAIR"].rearrange("(t p d) c -> t p (d c)", t=T, p=P)

        @block.sync
        def _(sp):
            with sp.Fori(0, T) as t:
                for h in range(2):
                    wait_count(sp, rows_free[h], 2 * t + 2, g["sp_turns"])
                    sp.dma_start(rows[h][:, :, :].rearrange("p d c -> p (d c)"),
                                 pairs[bass.ds(t, 1), :, 2 * half * h:2 * half * (h + 1)].squeeze(0),
                                 max_dma_last_dim=8192).then_inc(rows_in[h], 16)

        @block.scalar
        def _(act):
            for h in range(2):
                act.sem_inc(rows_free[h], 1)
            with act.Fori(0, T) as t:
                for h in range(2):
                    act.wait_ge(rows_in[h], 16 * t + 16)
                    act.copy(g["A"][:, bass.ds(t, 1), half * h:half * (h + 1)].squeeze(1), rows[h][:, :, 0])
                    act.wait_ge(top_ready[h], t + 1)
                    act.activation(dump[:, :], rows[h][:, :, 1], ACT.Exp, bias=top[h][:, 1:2],
                                   accum_out=part[h][:, :]).then_inc(part_ready[h], 1)
                    act.wait_ge(part_ready[h], t + 1)
                    act.sem_inc(rows_free[h], 1)
            act.wait_ge(spread_in, 1)
            act.activation(spread[:, :, :], spread[:, :, :], ACT.Exp).then_inc(spread_out, 1)

        @block.vector
        def _(dve):
            for h in range(2):
                dve.sem_inc(rows_free[h], 1)
            with dve.Fori(0, T) as t:
                st = Steps(dve, v_steps, t * 8)
                for h in range(2):
                    dve.wait_ge(rows_in[h], 16 * t + 16)
                    st.after(dve.tensor_reduce(top[h][:, 0:1], rows[h][:, :, 1], AX.X, ALU.max))
                    st.after(dve.tensor_scalar(top[h][:, 1:2], top[h][:, 0:1], -1.0, None, ALU.mult))
                    dve.sem_inc(rows_free[h], 1)
                    dve.sem_inc(top_ready[h], 1)
                    st.after(dve.tensor_copy(tops[:, h, bass.ds(t, 1)], top[h][:, 0:1]))
                    dve.wait_ge(part_ready[h], t + 1)
                    st.after(dve.tensor_copy(sums[:, h, bass.ds(t, 1)], part[h][:, :]))
            st = Steps(dve, v_steps, T * 8)
            st.after(dve.tensor_tensor(g["mout"][:, :], tops[:, 0, :], tops[:, 1, :], ALU.max))
            st.after(dve.tensor_tensor(spread[:, :, :], tops[:, :, :], free_bcast(g["mout"][:, :], 2, 0), ALU.subtract))
            dve.sem_inc(spread_in, 1)
            dve.wait_ge(spread_out, 1)
            st.after(dve.tensor_tensor(sums[:, :, :], sums[:, :, :], spread[:, :, :], ALU.mult))
            st.after(dve.tensor_tensor(g["sout"][:, :], sums[:, 0, :], sums[:, 1, :], ALU.add))


def normalise(nc, g, first=False):
    with ExitStack() as ctx:
        s = Scope(nc, ctx)
        tmp = s.sb("ln_tmp", [P, T, D])
        st4 = s.sb("ln_st", [P, 4, 2 * T])
        v_steps, root_in, root_out = s.sem("ln_steps"), s.sem("root_in"), s.sem("root_out")
        block = ctx.enter_context(nc.Block())
        X, H = g["X"], g["H"]
        w = 2 * T if first else T

        @block.scalar
        def _(act):
            act.wait_ge(root_in, 1)
            act.activation(st4[:, 2, 0:w], st4[:, 1, 0:w], ACT.Sqrt).then_inc(root_out, 1)

        @block.vector
        def _(dve):
            st = Steps(dve, v_steps)
            st.after(dve.tensor_reduce(st4[:, 0, 0:T], X[:, :, :], AX.X, ALU.add))
            st.after(dve.tensor_scalar(st4[:, 0, 0:T], st4[:, 0, 0:T], 1.0 / D, None, ALU.mult))
            st.after(dve.tensor_tensor(H[:, :, :], X[:, :, :], free_bcast(st4[:, 0, 0:T], 0, D), ALU.subtract))
            st.after(dve.tensor_tensor(tmp[:, :, :], H[:, :, :], H[:, :, :], ALU.mult))
            st.after(dve.tensor_reduce(st4[:, 1, 0:T], tmp[:, :, :], AX.X, ALU.add))
            st.after(dve.tensor_scalar(st4[:, 1, 0:T], st4[:, 1, 0:T], 1.0 / D, 1e-5, ALU.mult, ALU.add))
            if first:
                st.after(dve.tensor_scalar(st4[:, 1, T:w], g["deg"][:, :], 1.0, None, ALU.add))
            dve.sem_inc(root_in, 1)
            dve.wait_ge(root_out, 1)
            st.after(dve.reciprocal(st4[:, 3, 0:w], st4[:, 2, 0:w]))
            st.after(dve.tensor_tensor(st4[:, 2, 0:w], st4[:, 3, 0:w], st4[:, 3, 0:w], ALU.mult))
            st.after(dve.tensor_tensor(st4[:, 2, 0:w], st4[:, 2, 0:w], st4[:, 1, 0:w], ALU.mult))
            st.after(dve.tensor_scalar(st4[:, 2, 0:w], st4[:, 2, 0:w], -0.5, 1.5, ALU.mult, ALU.add))
            st.after(dve.tensor_tensor(st4[:, 3, 0:w], st4[:, 3, 0:w], st4[:, 2, 0:w], ALU.mult))
            if first:
                st.after(dve.tensor_copy(g["dinv"][:, :], st4[:, 3, T:w]))
            st.after(dve.tensor_tensor(H[:, :, :], H[:, :, :], free_bcast(st4[:, 3, 0:T], 0, D), ALU.mult))
            st.after(dve.tensor_scalar(H[:, :, :], H[:, :, :], 0.0, None, ALU.max))


def aggregate(nc, g, weight, bias, own_degree=False, scale=1.0, relu=False, add_to_x=False):
    with ExitStack() as ctx:
        s = Scope(nc, ctx)
        tmp = s.sb("ag_tmp", [P, T, D])
        parts = s.sb("ag_parts", [P, T, 3, D], BF16)
        w2 = s.sb("ag_w", [P, D])
        brow = s.sb("ag_b", [P, D])
        o1 = s.sb("ag_o1", [P, CH * P])
        o2 = s.sb("ag_o2", [D, CH * P])
        sv = s.sb("ag_sv", [P, 4, T])
        dparts = s.sb("ag_dparts", [P, 3, T], BF16)
        diag = s.sb("ag_diag", [P, CH, 3, P], BF16)
        pj = bank(g, 4)
        w_in, v_steps = s.sem("w_in"), s.sem("ag_steps")
        parts_ready, diag_ready = s.sem("parts_ready"), s.sem("diag_ready")
        chunk_done, o1_ready, o2_ready = s.sem("chunk_done"), s.sem("o1_ready"), s.sem("o2_ready")
        pj_done, pj_free = s.sem("pj_done"), s.sem("pj_free")
        loop_steps = s.sem("ag_loop_steps")
        a_part = s.sem("a_part")
        block = ctx.enter_context(nc.Block())
        H = g["H"]
        nself = 3 if own_degree else 1

        def sums(c, third):
            return g["banks"][:, bass.ds((c & 1) + 2 * third, 1), :].squeeze(1)

        @block.sync
        def _(sp):
            for i in range(2):
                sp.dma_start(w2[i * D:(i + 1) * D, :], weight).then_inc(w_in, 16)
            sp.dma_start(brow[:, :], bias.partition_broadcast(P)).then_inc(w_in, 16)

        @block.vector
        def _(dve):
            st = Steps(dve, v_steps)
            dv = free_bcast(g["dinv"][:, :], 0, D)
            st.after(dve.tensor_tensor(H[:, :, :], H[:, :, :], dv, ALU.mult))
            st.after(dve.tensor_copy(parts[:, :, 0, :], H[:, :, :]))
            st.after(dve.tensor_tensor(tmp[:, :, :], H[:, :, :], parts[:, :, 0, :], ALU.subtract))
            st.after(dve.tensor_copy(parts[:, :, 1, :], tmp[:, :, :]))
            st.after(dve.tensor_tensor(parts[:, :, 2, :], tmp[:, :, :], parts[:, :, 1, :], ALU.subtract))
            st.after(dve.tensor_scalar(sv[:, 0, :], g["dinv"][:, :], scale, None, ALU.mult))
            if own_degree:
                st.after(dve.tensor_scalar(sv[:, 1, :], g["deg"][:, :], 2.0, None, ALU.add))
                st.after(dve.tensor_copy(dparts[:, 0, :], sv[:, 1, :]))
                st.after(dve.tensor_tensor(sv[:, 2, :], sv[:, 1, :], dparts[:, 0, :], ALU.subtract))
                st.after(dve.tensor_copy(dparts[:, 1, :], sv[:, 2, :]))
                st.after(dve.tensor_tensor(dparts[:, 2, :], sv[:, 2, :], dparts[:, 1, :], ALU.subtract))
            else:
                st.after(dve.memset(dparts[:, 0, :], 1.0))
            dve.sem_inc(parts_ready, 1)
            for sem in (pj_free, pj_done):
                dve.sem_inc(sem, 1)

            def diagonals(c, tiles, t0, steps):
                if not isinstance(c, int) or c:
                    dve.wait_ge(chunk_done, c)
                for j in range(tiles):
                    for i in range(nself):
                        steps.mark(dve.tensor_tensor(diag[:, j, i, :], g["ident_b"][:, :],
                                                     dparts[:, i, bass.ds(t0 + j, 1)].to_broadcast([P, P]),
                                                     ALU.mult))
                steps.wait()
                dve.sem_inc(diag_ready, 1)

            def finish(c, tiles, t0, steps):
                dve.wait_ge(chunk_done, c + 1)
                steps.after(dve.tensor_copy(o2[:, 0:tiles * P], sums(c, 1)[0:D, 0:tiles * P]))
                dve.sem_inc(o2_ready, 1)
                dve.wait_ge(pj_done, c + 2)
                steps.after(dve.tensor_tensor(H[:, bass.ds(t0, tiles), :],
                                              pj[:, 0:tiles * D].rearrange("p (t f) -> p t f", f=D),
                                              free_bcast(sv[:, 0, bass.ds(t0, tiles)], 0, D), ALU.mult))
                dve.sem_inc(pj_free, 1)

            n = CH * nself + 2
            diagonals(0, CH, 0, st)
            with dve.Fori(0, NCH - 1) as c:
                loop = Steps(dve, loop_steps, c * n)
                diagonals(c + 1, CH, (c + 1) * CH, loop)
                finish(c, CH, c * CH, loop)
            diagonals(NCH, 1, NCH * CH, st)
            finish(NCH - 1, CH, (NCH - 1) * CH, st)
            finish(NCH, 1, NCH * CH, st)
            dve.wait_ge(w_in, 48)
            st.after(dve.tensor_tensor(H[:, :, :], H[:, :, :], free_bcast(brow[:, :], T, 0), ALU.add))
            if relu:
                st.after(dve.tensor_scalar(H[:, :, :], H[:, :, :], 0.0, None, ALU.max))
            if add_to_x:
                st.after(dve.tensor_tensor(g["X"][:, :, :], g["X"][:, :, :], H[:, :, :], ALU.add))

        @block.scalar
        def _(act):
            with act.Fori(0, NCH) as c:
                act.wait_ge(chunk_done, c + 1)
                act.wait_ge(pj_done, c + 1)
                act.copy(o1[:, :], sums(c, 0)[:, 0:CH * P]).then_inc(o1_ready, 1)
            act.wait_ge(chunk_done, NCH + 1)
            act.wait_ge(pj_done, NCH + 1)
            act.copy(o1[:, 0:P], sums(NCH, 0)[:, 0:P]).then_inc(o1_ready, 1)

        @block.tensor
        def _(pe):
            pe.wait_ge(parts_ready, 1)
            pe.wait_ge(w_in, 48)

            def add_up(c, tiles, t0):
                w = tiles * P
                c1, c2 = sums(c, 0), sums(c, 1)
                for src in range(T):
                    moving = g["A"][:, src, bass.ds(t0 * P, w)]
                    pe.matmul(c1[:, 0:w], parts[:, src, 0:2, :].rearrange("p a f -> p (a f)"), moving,
                              start=(src == 0), stop=False, skip_group_check=True)
                    pe.matmul(c2[0:D, 0:w], parts[:, src, 2, :], moving, start=(src == 0), stop=False,
                              skip_group_check=True)
                wait_count(pe, diag_ready, c + 1, g["pe_turns"])
                for j in range(tiles):
                    for i in range(nself):
                        last = i == nself - 1
                        own = parts[:, bass.ds(t0 + j, 1), :, :].rearrange("p t a f -> p (t a f)")
                        pe.matmul(c1[:, j * P:(j + 1) * P], own[:, 0:2 * D], diag[:, j, i, :], start=False,
                                  stop=last, skip_group_check=True)
                        mm = pe.matmul(c2[0:D, j * P:(j + 1) * P], own[:, 2 * D:3 * D], diag[:, j, i, :],
                                       start=False, stop=last, skip_group_check=True)
                mm.then_inc(chunk_done, 1)

            def project(c, tiles):
                pe.wait_ge(o1_ready, c + 1)
                pe.wait_ge(o2_ready, c + 1)
                pe.wait_ge(pj_free, c + 1)
                for j in range(tiles):
                    pe.matmul(pj[:, j * D:(j + 1) * D], o1[:, j * P:(j + 1) * P], w2[:, :], start=True, stop=False)
                    mm = pe.matmul(pj[:, j * D:(j + 1) * D], o2[:, j * P:(j + 1) * P], w2[0:D, :], start=False,
                                   stop=True)
                mm.then_inc(pj_done, 1)

            add_up(0, CH, 0)
            with pe.Fori(0, NCH - 1) as c:
                add_up(c + 1, CH, (c + 1) * CH)
                project(c, CH)
            add_up(NCH, 1, NCH * CH)
            project(NCH - 1, CH)
            project(NCH, 1)


def bring_rows(nc, g, table, rows, width):
    with ExitStack() as ctx:
        s = Scope(nc, ctx)
        rows_in = s.sem("brought")
        block = ctx.enter_context(nc.Block())

        @block.gpsimd
        def _(pool):
            for t in range(T):
                at = bass.IndirectOffsetOnAxis(ap=g["rank_i"][:, t:t + 1], axis=0)
                pool.indirect_dma_start(rows[:, t, 0:width], None, table, at).then_inc(rows_in, 16)
            pool.wait_ge(rows_in, 16 * T)


def attention_tables(nc, g, rows, k_dim, heads, chans, wl, bl, wr, br, att, left, right):
    hc = heads * chans
    chunks = [(k, min(P, k_dim - k)) for k in range(0, k_dim, P)]
    with ExitStack() as ctx:
        s = Scope(nc, ctx)
        w = s.sb("at_w", [P, len(chunks), 2, hc])
        b = s.sb("at_b", [P, 2, hc])
        a = s.sb("at_a", [P, 2, hc])
        xt = s.sb("at_xt", [P, k_dim])
        xT = s.sb("at_xT", [P, len(chunks), P])
        out = s.sb("at_out", [P, 2, hc + heads])
        prod = s.sb("at_prod", [P, 2, hc])
        none = s.sb("at_none", [1, hc + heads])
        tp = bank(g, 0)[:, 0:len(chunks) * P].rearrange("p (k n) -> p k n", n=P)
        mp = bank(g, 1)
        w_in, x_ready, x_turned, xT_ready = s.sem("aw_in"), s.sem("x_ready"), s.sem("x_turned"), s.sem("xT_ready")
        projected, rows_out, v_steps = s.sem("projected"), s.sem("rows_out"), s.sem("at_steps")
        rows_ready, mp_free = s.sem("rows_ready"), s.sem("mp_free")
        none_ready, none_out = s.sem("none_ready"), s.sem("none_out")
        block = ctx.enter_context(nc.Block())
        att_row = att.rearrange("h c -> (h c)")

        @block.sync
        def _(sp):
            for i, (wd, bd) in enumerate(((wl, bl), (wr, br))):
                for j, (k, n) in enumerate(chunks):
                    sp.dma_start(w[0:n, j, i, :], wd[k:k + n, :]).then_inc(w_in, 16)
                sp.dma_start(b[:, i, :], bd.partition_broadcast(P)).then_inc(w_in, 16)
                sp.dma_start(a[:, i, :], att_row.partition_broadcast(P)).then_inc(w_in, 16)
            sp.wait_ge(none_ready, 1)
            sp.dma_start(left[NO_ROW:NO_ROW + 1, :], none[:, :]).then_inc(none_out, 16)
            sp.dma_start(right[NO_ROW:NO_ROW + 1, :], none[:, :]).then_inc(none_out, 16)
            sp.wait_ge(none_out, 32)
            with sp.Fori(0, T) as t:
                wait_count(sp, rows_ready, t + 1, g["sp_turns"])
                for i, table in enumerate((left, right)):
                    sp.dma_start(table[bass.ds(t * P, P), :], out[:, i, :]).then_inc(rows_out, 16)
            sp.wait_ge(rows_out, 32 * T + 1)
        n_w = 16 * 2 * (len(chunks) + 2)

        @block.scalar
        def _(act):
            with act.Fori(0, T) as t:
                act.copy(xt[:, :], rows[:, bass.ds(t, 1), 0:k_dim].squeeze(1)).then_inc(x_ready, 1)
                act.wait_ge(x_turned, t + 1)
                for j, (k, n) in enumerate(chunks):
                    act.copy(xT[0:n, j, :], tp[0:n, j, :]).then_inc(xT_ready, 1)

        @block.tensor
        def _(pe):
            pe.wait_ge(w_in, n_w)
            with pe.Fori(0, T) as t:
                wait_count(pe, x_ready, t + 1, g["pe_turns"])
                for j, (k, n) in enumerate(chunks):
                    mm = pe.transpose(tp[0:n, j, :], xt[:, k:k + n], g["ident"][:, :])
                mm.then_inc(x_turned, 1)
                pe.wait_ge(xT_ready, (t + 1) * len(chunks))
                pe.wait_ge(mp_free, t + 1)
                for j, (k, n) in enumerate(chunks):
                    mm = pe.matmul(mp[:, 0:2 * hc], xT[0:n, j, :], w[0:n, j].rearrange("p i c -> p (i c)"),
                                   start=(j == 0), stop=(j == len(chunks) - 1))
                mm.then_inc(projected, 1)

        @block.vector
        def _(dve):
            dve.wait_ge(w_in, n_w)
            st = Steps(dve, v_steps)
            st.mark(dve.memset(none[:, 0:hc], 0.0))
            st.mark(dve.memset(none[:, hc:], -BIG))
            st.after(dve.tensor_scalar(a[:, :, :], a[:, :, :], 0.2, None, ALU.mult))
            dve.sem_inc(none_ready, 1)
            first = st.n
            dve.sem_inc(rows_out, 1)
            dve.sem_inc(mp_free, 1)
            with dve.Fori(0, T) as t:
                st = Steps(dve, v_steps, first + t * 3)
                dve.wait_ge(projected, t + 1)
                dve.wait_ge(rows_out, 32 * t + 1)
                st.after(dve.tensor_tensor(out[:, :, 0:hc], mp[:, 0:2 * hc].rearrange("p (i c) -> p i c", i=2),
                                           b[:, :, :], ALU.add))
                dve.sem_inc(mp_free, 1)
                st.after(dve.tensor_tensor(prod[:, :, :], out[:, :, 0:hc], a[:, :, :], ALU.mult))
                st.after(dve.tensor_reduce(out[:, :, hc:], prod[:, :, :].rearrange("p i (h c) -> p i h c", c=chans),
                                           AX.X, ALU.add))
                dve.sem_inc(rows_ready, 1)


def sizes_of(eng, g, t):
    info = g["info"]
    return (eng.value_load(info[0:1, 0, bass.ds(t, 1)], min_val=1, max_val=SB * U),
            eng.value_load(info[0:1, 2, bass.ds(t, 1)], min_val=0, max_val=SB * U))


def block_column(nc, base, j):
    return nc.s_assert_within(base * GS + j * GB, 0, (U + T - 1) * GS,
                              skip_runtime_bounds_check_because="the tables are sized for it")


def attend(nc, g, heads, chans, att, bias, left, right, result):
    hc, wd = heads * chans, heads * (chans + 1)
    gs = 3 if 4 * wd > 512 else 4
    groups = [(k, min(gs, B - k)) for k in range(0, B, gs)]
    nb = len(groups)
    assert gs * wd <= 512 and 2 * nb + 1 <= 8
    with ExitStack() as ctx:
        s = Scope(nc, ctx)
        G = s.sb("gathered", [P, RING, B, wd])
        gi = s.sb("gat_idx", [P, GB], I32)
        nidc = s.sb("nidc", [P, 1], I32)
        own = s.sb("own", [P, 2, 2, wd])
        res = s.sb("res", [P, hc])
        z = g["H"][:, :, :].rearrange("p t f -> p (t f)")[:, 0:B * hc].rearrange("p (k w) -> p k w", w=hc)
        zo = s.sb("zo", [P, wd])
        wgt = s.sb("wgt", [P, B + 1, heads, chans + 1])
        arow = s.sb("arow", [P, hc])
        brow = s.sb("gbrow", [P, hc])
        num = s.sb("num", [P, heads, chans + 1])
        sm = s.sb("sm", [P, 4, heads])
        lg = s.sb("lg", [P, B, heads])
        ex = s.sb("gat_ex", [P, B + 1, heads])
        own_in, res_ready, res_out = s.sem("own_in"), s.sem("res_ready"), s.sem("res_out")
        consts_in, tile_done = s.sem("gc_in"), s.sem("tile_done")
        nid_ready, g_free = s.sem("nid_ready"), s.sem("g_free")
        idx_in, g_in = [[s.sem(f"{n}{q}") for q in range(Q)] for n in ("idx_in", "g_in")]
        tile_steps, block_steps, sum_steps, c_steps = (s.sem(n) for n in ("gt_steps", "gb_steps", "gd_steps", "gc_steps"))
        z_ready, z_free = s.sem("z_ready"), s.sem("z_free")
        wgt_ready, sum_ready = s.sem("wgt_ready"), s.sem("sum_ready")
        ex_ready, ex_done = s.sem("gex_ready"), s.sem("gex_done")
        block = ctx.enter_context(nc.Block())
        runs = [(0, nb, gs)] if B % gs == 0 else [(0, nb - 1, gs), (nb - 1, 1, B % gs)]
        T_STEPS, B_STEPS, D_STEPS = 9, nb + len(runs) + 7, 2
        PART = BQ * 16

        @block.sync
        def _(sp):
            sp.dma_start(arow[:, :], att.rearrange("h c -> (h c)").partition_broadcast(P)).then_inc(consts_in, 16)
            sp.dma_start(brow[:, :], bias.partition_broadcast(P)).then_inc(consts_in, 16)
            with sp.Fori(0, T) as t:
                blocks, before = sizes_of(sp, g, t)
                base = sp.value_load(g["info"][0:1, 3, bass.ds(t, 1)], min_val=0, max_val=U)
                with sp.Fori(0, blocks) as j:
                    n = before + j
                    for q in range(Q):
                        wait_count(sp, g_in[q], n * PART + 16, g["sp_turns"])
                        a, w = (1 + q * BQ, BQ) if q else (0, 1 + BQ)
                        sp.dma_start(gi[:, a:a + w], g["GIDX"][:, bass.ds(block_column(nc, base, j) + a, w)])\
                            .then_inc(idx_in[q], 16)

        @block.gpsimd
        def _(pool):
            def own_rows(k):
                for i, table in enumerate((left, right)):
                    at = bass.IndirectOffsetOnAxis(ap=nidc[:, :], axis=0)
                    pool.indirect_dma_start(own[:, k, i, :], None, table, at).then_inc(own_in, 16)

            def gather(n, k):
                for q in range(Q):
                    wait_count(pool, idx_in[q], n * 16 + 16, g["pool_turns"])
                    for c in range(q * BQ, (q + 1) * BQ):
                        at = bass.IndirectOffsetOnAxis(ap=gi[:, 1 + c:2 + c], axis=0)
                        pool.indirect_dma_start(G[:, k, c, :], None, left, at).then_inc(g_in[q], 16)
            for q in range(Q):
                at = bass.IndirectOffsetOnAxis(ap=g["nid_i"][:, 0:1], axis=0)
                pool.indirect_dma_start(G[:, RING - 1, q, :], None, left, at).then_inc(g_in[q], 16)
            pool.tensor_copy(nidc[:, :], g["nid_i"][:, 0:1]).then_inc(nid_ready, 1)
            pool.wait_ge(nid_ready, 1)
            own_rows(0)
            with pool.Fori(0, T) as t:
                blocks, before = sizes_of(pool, g, t)
                with pool.Fori(0, blocks) as j:
                    n = before + j
                    wait_count(pool, g_free, n + 1, g["pool_turns"])
                    with pool.If((n & 2) < 1):
                        with pool.If((n & 1) < 1):
                            gather(n, 0)
                        with pool.Else():
                            gather(n, 1)
                        pool.sem_inc(g["pool_turns"], 1)
                    with pool.Else():
                        with pool.If((n & 1) < 1):
                            gather(n, 2)
                        with pool.Else():
                            gather(n, 3)
                        pool.sem_inc(g["pool_turns"], 1)
                wait_count(pool, own_in, t * 32 + 32, g["pool_turns"])
                pool.tensor_copy(nidc[:, :], g["nid_i"][:, bass.ds(t + 1, 1)]).then_inc(nid_ready, 1)
                wait_count(pool, tile_done, t + 1, g["pool_turns"])
                wait_count(pool, nid_ready, t + 2, g["pool_turns"])
                with pool.If((t & 1) < 1):
                    own_rows(1)
                with pool.Else():
                    own_rows(0)
            pool.wait_ge(own_in, 32 * (T + 1))

        @block.tensor
        def _(pe):
            def add_pairs(t, n):
                for q in range(Q):
                    wait_count(pe, g_in[q], n * PART + PART + 16, g["pe_turns"])
                wait_count(pe, z_free, n + 1, g["pe_turns"])
                for i, (k, w) in enumerate(groups):
                    out = g["banks"][:, bass.ds((n & 1) * nb + i, 1), 0:w * wd].squeeze(1)
                    pe.matmul(out, g["ident"][:, :], G[:, bass.ds(n & (RING - 1), 1), k:k + w, :]
                              .rearrange("p a k w -> p (a k w)"), start=True, stop=False)
                    row = own[:, bass.ds(t & 1, 1), 1, :].to_broadcast([P, w, wd])
                    pe.matmul(out, g["ident"][:, :], row, start=False, stop=True).then_inc(z_ready, 1)

            def sum_slots(n):
                wait_count(pe, wgt_ready, n + 1, g["pe_turns"])
                for k in range(B):
                    mm = pe.matmul(bank(g, 7)[:, 0:wd], g["ident"][:, :], wgt[:, k].rearrange("p h c -> p (h c)"),
                                   start=(k == 0), stop=(k == B - 1))
                mm.then_inc(sum_ready, 1)

            pe.wait_ge(own_in, 32)
            add_pairs(0, 0)
            with pe.Fori(0, T) as t:
                blocks, before = sizes_of(pe, g, t)
                with pe.Fori(0, blocks - 1) as j:
                    add_pairs(t, before + j + 1)
                    sum_slots(before + j)
                with pe.If(t < T - 1):
                    wait_count(pe, own_in, t * 32 + 64, g["pe_turns"])
                    add_pairs(t + 1, before + blocks)
                with pe.Else():
                    pe.sem_inc(g["pe_turns"], 1)
                sum_slots(before + blocks - 1)

        @block.vector
        def _(dve):
            for _ in range(RING):
                dve.sem_inc(g_free, 1)
            dve.sem_inc(tile_done, 1)
            for _ in range(D_STEPS):
                dve.sem_inc(sum_steps, 1)
            dve.sem_inc(res_out, 1)
            for _ in range(2):
                dve.sem_inc(z_free, 1)
            dve.wait_ge(consts_in, 32)
            st = Steps(dve, c_steps)
            st.after(dve.tensor_scalar(arow[:, :], arow[:, :], 0.8, None, ALU.mult))
            m, mn, bm, rd = (sm[:, i, :] for i in range(4))
            num_rows = num[:, :, 0:chans]

            def zsum(n, i, w):
                return g["banks"][:, bass.ds((n & 1) * nb + i, w), :]

            def add_block(done):
                sd = Steps(dve, sum_steps, done * D_STEPS)
                scale = wgt[:, B, :, chans]
                sd.after(dve.tensor_tensor(num[:, :, :], num[:, :, :], free_bcast(scale, 0, chans + 1), ALU.mult))
                dve.wait_ge(sum_ready, done)
                sd.after(dve.tensor_tensor(num[:, :, :], num[:, :, :],
                                           bank(g, 7)[:, 0:wd].rearrange("p (h c) -> p h c", h=heads), ALU.add))
                assert sd.n == D_STEPS

            def weigh(n, done=None):
                sb = Steps(dve, block_steps, n * B_STEPS)
                for i, (k, w) in enumerate(groups):
                    dve.wait_ge(z_ready, n * nb + i + 1)
                    zs = zsum(n, i, 1)[:, :, 0:w * wd].rearrange("p i (k w) -> p (i k) w", k=w)
                    sb.mark(dve.scalar_tensor_tensor(out=z[:, k:k + w, :], in0=zs[:, :, 0:hc], scalar=0.0,
                                                     in1=free_bcast(arow[:, :], w, 0), op0=ALU.max, op1=ALU.mult))
                sb.wait()
                sb.after(dve.tensor_reduce(lg[:, :, :], z[:, :, :].rearrange("p k (h c) -> p k h c", c=chans), AX.X,
                                           ALU.add))
                for i, w, slots in runs:
                    k0, k1 = i * gs, i * gs + w * slots
                    zs = zsum(n, i, w)[:, :, 0:slots * wd].rearrange("p i (k w) -> p i k w", k=slots)
                    lk = lg[:, k0:k1, :].rearrange("p (i k) h -> p i k h", i=w)
                    sb.mark(dve.tensor_tensor(lk, lk, zs[:, :, :, hc:wd], ALU.add))
                sb.wait()
                dve.sem_inc(z_free, 1)
                sb.after(dve.tensor_reduce(bm, lg[:, :, :].rearrange("p k h -> p h k"), AX.X, ALU.max))
                sb.after(dve.tensor_tensor(mn, m, bm, ALU.max))
                sb.mark(dve.tensor_tensor(ex[:, 0:B, :], lg[:, :, :], free_bcast(mn, B, 0), ALU.subtract))
                sb.after(dve.tensor_tensor(ex[:, B, :], m, mn, ALU.subtract))
                if done is not None:
                    add_block(done)
                dve.sem_inc(ex_ready, 1)
                sb.mark(dve.tensor_copy(m, mn))
                dve.wait_ge(ex_done, n + 1)
                Gn = G[:, bass.ds(n & (RING - 1), 1), :, 0:hc].rearrange("p a k (h c) -> p (a k) h c", h=heads)
                sb.after(dve.tensor_tensor(wgt[:, 0:B, :, 0:chans], Gn, free_bcast(wgt[:, 0:B, :, chans], 0, chans),
                                           ALU.mult))
                dve.sem_inc(g_free, 1)
                dve.sem_inc(wgt_ready, 1)
                assert sb.n == B_STEPS, sb.n

            with dve.Fori(0, T) as t:
                st = Steps(dve, tile_steps, t * T_STEPS)
                blocks, before = sizes_of(dve, g, t)
                dve.wait_ge(own_in, t * 32 + 32)
                own_l, own_r = (own[:, bass.ds(t & 1, 1), i, :].rearrange("p a w -> p (a w)") for i in range(2))
                st.mark(dve.tensor_tensor(zo[:, :], own_l, own_r, ALU.add))
                st.mark(dve.tensor_copy(num_rows, own_l[:, 0:hc].rearrange("p (h c) -> p h c", c=chans)))
                st.after(dve.memset(num[:, :, chans], 1.0))
                st.after(dve.scalar_tensor_tensor(out=z[:, 0, :], in0=zo[:, 0:hc], scalar=0.0, in1=arow[:, :],
                                                  op0=ALU.max, op1=ALU.mult))
                st.after(dve.tensor_reduce(m, z[:, 0, :].rearrange("p (h c) -> p h c", c=chans), AX.X, ALU.add))
                st.after(dve.tensor_tensor(m, m, zo[:, hc:], ALU.add))
                weigh(before)
                dve.sem_inc(g["v_turns"], 1)
                with dve.Fori(0, blocks - 1) as j:
                    weigh(before + j + 1, before + j + 1)
                add_block(before + blocks)
                dve.sem_inc(tile_done, 1)
                st.after(dve.reciprocal(rd, num[:, :, chans]))
                dve.wait_ge(res_out, t * 16 + 1)
                st.after(dve.tensor_tensor(res[:, :].rearrange("p (h c) -> p h c", c=chans), num_rows,
                                           free_bcast(rd, 0, chans), ALU.mult))
                st.after(dve.tensor_tensor(res[:, :], res[:, :], brow[:, :], ALU.add))
                dve.sem_inc(res_ready, 1)
                assert st.n == T_STEPS, st.n

        @block.scalar
        def _(act):
            with act.Fori(0, T) as t:
                blocks, before = sizes_of(act, g, t)
                with act.Fori(0, blocks) as j:
                    act.wait_ge(ex_ready, before + j + 1)
                    act.activation(wgt[:, :, :, chans], ex[:, :, :], ACT.Exp).then_inc(ex_done, 1)
                wait_count(act, res_ready, t + 1, g["act_turns"])
                act.dma_start(result[bass.ds(t * P, P), :], res[:, :]).then_inc(res_out, 16)
            act.wait_ge(res_out, 16 * T + 1)


def add_rows(nc, g, rows):
    with ExitStack() as ctx:
        s = Scope(nc, ctx)
        added = s.sem("added")
        block = ctx.enter_context(nc.Block())

        @block.vector
        def _(dve):
            dve.tensor_tensor(g["X"][:, :, :], g["X"][:, :, :], rows[:, :, :], ALU.add).then_inc(added, 1)


def pair_softmax(nc, g):
    with ExitStack() as outer:
        so = Scope(nc, outer)
        rin = so.sb("rin", [P, T])
        outT = so.sb("outT", [D, NP])
        with ExitStack() as ctx:
            s = Scope(nc, ctx)
            rows = [s.sb(f"prow{b}", [P, NP, 2]) for b in range(2)]
            wt = [s.sb(f"pwt{b}", [P, NP]) for b in range(2)]
            hs = [s.sb(f"phs{b}", [P, D]) for b in range(2)]
            minrow = s.sb("minrow", [P, NP])
            ms = s.sb("ms", [P, T, 2])
            hmin = s.sb("hmin", [P, T])
            hout = s.sb("hout", [P, T])
            bias_c = [s.sb(f"bias_c{b}", [P, 1]) for b in range(2)]
            st4 = s.sb("ps_st", [P, 3, 2 * T])
            zero_b = s.sb("pz", [P, 512], BF16)
            pt = [bank(g, c) for c in range(7)]
            turn = bank(g, 7)
            ms_in, root_in, root_out, v_steps = s.sem("ms_in"), s.sem("pr_in"), s.sem("pr_out"), s.sem("ps_steps")
            turned, copied, ready = s.sem("turned"), s.sem("copied"), s.sem("ready")
            rows_in, wt_ready, wt_exp, wt_free = [[s.sem(f"{n}{i}") for i in range(2)] for n in
                                                  ("prow_in", "wt_ready", "wt_exp", "wt_free")]
            tile_steps = s.sem("pt_steps")
            all_done = s.sem("all_done")
            block = ctx.enter_context(nc.Block())
            pairs = g["PAIR"].rearrange("(t p d) c -> t p (d c)", t=T, p=P)
            widths = [512] * (NP // 512) + [NP % 512]

            def tiles(eng, tile):
                with eng.Fori(0, T // 2) as i:
                    tile(2 * i, 0, i)
                    tile(2 * i + 1, 1, i)
                tile(T - 1, 0, T // 2)

            @block.sync
            def _(sp):
                sp.dma_start(ms[:, :, :], g["MS"].rearrange("(t p) c -> p t c", p=P)).then_inc(ms_in, 16)

                def tile(t, b, i):
                    wait_count(sp, wt_ready[b], i + 1, g["sp_turns"])
                    sp.dma_start(rows[b][:, :, :].rearrange("p d c -> p (d c)"), pairs[bass.ds(t, 1)].squeeze(0),
                                 max_dma_last_dim=8192).then_inc(rows_in[b], 16)
                tiles(sp, tile)

            @block.vector
            def _(dve):
                st = Steps(dve, v_steps)
                for b in range(2):
                    dve.sem_inc(wt_ready[b], 1)
                dve.wait_ge(ms_in, 16)
                st.after(dve.tensor_scalar(hmin[:, :], ms[:, :, 0], -0.1 * BIG, 0.5, ALU.max, ALU.mult))
                dve.sem_inc(ready, 1)
                st.mark(dve.memset(zero_b[:, :], 0.0))
                st.mark(dve.tensor_scalar(hout[:, :], g["mout"][:, :], -0.5, None, ALU.mult))
                st.mark(dve.tensor_copy(st4[:, 0, 0:T], ms[:, :, 1]))
                st.after(dve.tensor_copy(st4[:, 0, T:], g["sout"][:, :]))
                dve.sem_inc(root_in, 1)
                dve.wait_ge(root_out, 1)
                st.after(dve.reciprocal(st4[:, 2, :], st4[:, 1, :]))
                st.after(dve.tensor_tensor(st4[:, 1, :], st4[:, 2, :], st4[:, 2, :], ALU.mult))
                st.after(dve.tensor_tensor(st4[:, 1, :], st4[:, 1, :], st4[:, 0, :], ALU.mult))
                st.after(dve.tensor_scalar(st4[:, 1, :], st4[:, 1, :], -0.5, 1.5, ALU.mult, ALU.add))
                st.after(dve.tensor_tensor(st4[:, 2, :], st4[:, 2, :], st4[:, 1, :], ALU.mult))
                st.mark(dve.tensor_copy(rin[:, :], st4[:, 2, 0:T]))
                st.after(dve.tensor_tensor(g["H"][:, :, :], g["H"][:, :, :], free_bcast(st4[:, 2, T:], 0, D), ALU.mult))
                dve.sem_inc(ready, 1)
                dve.wait_ge(copied, -(-T // 4))

                def tile(t, b, i):
                    st = Steps(dve, tile_steps, t * 3)
                    dve.wait_ge(rows_in[b], i * 16 + 16)
                    dve.wait_ge(wt_free[b], i + 1)
                    st.mark(dve.tensor_copy(hs[b][:, :], g["H"][:, bass.ds(t, 1), :].squeeze(1)))
                    st.mark(dve.tensor_copy(bias_c[b][:, :], hout[:, bass.ds(t, 1)]))
                    st.after(dve.tensor_tensor(wt[b][:, :], rows[b][:, :, 1], minrow[:, :], ALU.subtract))
                    dve.sem_inc(wt_ready[b], 1)
                tiles(dve, tile)
                dve.wait_ge(all_done, 1)
                off = 0
                for c, w in enumerate(widths):
                    dve.tensor_copy(outT[:, off:off + w], pt[c][0:D, 0:w]).then_inc(v_steps, 1)
                    off += w

            @block.scalar
            def _(act):
                act.wait_ge(root_in, 1)
                act.activation(st4[:, 1, :], st4[:, 0, :], ACT.Sqrt).then_inc(root_out, 1)
                for j in range(-(-T // 4)):
                    act.wait_ge(turned, j + 1)
                    w = min(4, T - 4 * j) * P
                    act.copy(minrow[:, 4 * j * P:4 * j * P + w], turn[:, 0:w]).then_inc(copied, 1)

                def tile(t, b, i):
                    act.wait_ge(wt_ready[b], i + 2)
                    act.activation(wt[b][:, :], wt[b][:, :], ACT.Exp, bias=bias_c[b][:, 0:1]).then_inc(wt_exp[b], 1)
                tiles(act, tile)

            @block.tensor
            def _(pe):
                pe.wait_ge(ready, 1)
                for t in range(T):
                    if t and t % 4 == 0:
                        pe.wait_ge(copied, t // 4)
                    mm = pe.transpose(turn[:, (t % 4) * P:(t % 4 + 1) * P], hmin[:, t:t + 1].to_broadcast([P, P]),
                                      g["ident"][:, :])
                    if t % 4 == 3 or t == T - 1:
                        mm.then_inc(turned, 1)
                pe.wait_ge(ready, 2)
                for b in range(2):
                    pe.sem_inc(wt_free[b], 1)
                for c, w in enumerate(widths):
                    pe.matmul(pt[c][0:D, 0:w], zero_b[:, 0:D], zero_b[:, 0:w], start=True, stop=False,
                              skip_group_check=True)

                def tile(t, b, i):
                    pe.wait_ge(wt_exp[b], i + 1)
                    off = 0
                    for c, w in enumerate(widths):
                        mm = pe.matmul(pt[c][0:D, 0:w], hs[b][:, :], wt[b][:, off:off + w], start=False, stop=False,
                                       skip_group_check=True)
                        off += w
                    mm.then_inc(wt_free[b], 1)
                tiles(pe, tile)
                for c, w in enumerate(widths):
                    mm = pe.matmul(pt[c][0:D, 0:w], zero_b[:, 0:D], zero_b[:, 0:w], start=False, stop=True,
                                   skip_group_check=True)
                mm.then_inc(all_done, 1)

        with ExitStack() as ctx:
            s = Scope(nc, ctx)
            back = [bank(g, i).rearrange("p (t f) -> p t f", f=D) for i in range(4)]
            tmp = s.sb("ps_tmp", [P, T, D])
            turned, v_steps = s.sem("turned_back"), s.sem("psb_steps")
            block = ctx.enter_context(nc.Block())

            @block.tensor
            def _(pe):
                for t in range(T):
                    pe.transpose(back[t // 8][:, t % 8, :], outT[:, t * P:(t + 1) * P],
                                 g["ident"][0:D, 0:D]).then_inc(turned, 1)

            @block.vector
            def _(dve):
                st = Steps(dve, v_steps)
                for j in range(4):
                    a, b = 8 * j, min(8 * j + 8, T)
                    dve.wait_ge(turned, b)
                    st.after(dve.tensor_tensor(tmp[:, a:b, :], back[j][:, 0:b - a, :],
                                               free_bcast(rin[:, a:b], 0, D), ALU.mult))
                st.after(dve.tensor_tensor(g["X"][:, :, :], g["X"][:, :, :], tmp[:, :, :], ALU.add))


def store_rows(nc, g, table):
    with ExitStack() as ctx:
        s = Scope(nc, ctx)
        none = s.sb("f_none", [1, D])
        out, none_ready = s.sem("stored"), s.sem("f_none_ready")
        block = ctx.enter_context(nc.Block())

        @block.vector
        def _(dve):
            dve.memset(none[:, :], -BIG).then_inc(none_ready, 1)

        @block.sync
        def _(sp):
            sp.dma_start(table[0:NP, :].rearrange("(t p) f -> p t f", p=P), g["H"][:, :, :]).then_inc(out, 16)
            sp.wait_ge(none_ready, 1)
            sp.dma_start(table[NO_ROW:NO_ROW + 1, :], none[:, :]).then_inc(out, 16)
            sp.wait_ge(out, 32)


def edge_sums(nc, g, table, result):
    with ExitStack() as ctx:
        s = Scope(nc, ctx)
        G = s.sb("e_rows", [P, RING, B, D])
        AT = s.sb("e_attr", [P, RING, B * D])
        gi = s.sb("e_idx", [P, GB], I32)
        z = s.sb("e_z", [P, B, D])
        acc = s.sb("e_acc", [P, D])
        part = s.sb("e_part", [P, D])
        res = s.sb("e_res", [P, D])
        res_ready, res_out = s.sem("er_ready"), s.sem("er_out")
        g_free = s.sem("e_g_free")
        idx_in, g_in = [[s.sem(f"{n}{q}") for q in range(Q)] for n in ("e_idx_in", "e_g_in")]
        tile_steps, block_steps = s.sem("et_steps"), s.sem("eb_steps")
        block = ctx.enter_context(nc.Block())
        T_STEPS, B_STEPS = 2, 4
        PARTS = [(BQ + (q == 0)) * 16 for q in range(Q)]

        @block.sync
        def _(sp):
            with sp.Fori(0, T) as t:
                blocks, before = sizes_of(sp, g, t)
                base = sp.value_load(g["info"][0:1, 3, bass.ds(t, 1)], min_val=0, max_val=U)
                with sp.Fori(0, blocks) as j:
                    n = before + j
                    for q in range(Q):
                        wait_count(sp, g_in[q], n * PARTS[q] + 16, g["sp_turns"])
                        a, w = (1 + q * BQ, BQ) if q else (0, 1 + BQ)
                        sp.dma_start(gi[:, a:a + w], g["GIDX"][:, bass.ds(block_column(nc, base, j) + a, w)])\
                            .then_inc(idx_in[q], 16)

        @block.gpsimd
        def _(pool):
            def gather(n, k):
                for q in range(Q):
                    wait_count(pool, idx_in[q], n * 16 + 16, g["pool_turns"])
                    if q == 0:
                        at = bass.IndirectOffsetOnAxis(ap=gi[:, 0:1], axis=0)
                        pool.indirect_dma_start(AT[:, k, :], None, g["edge_attr_64"], at).then_inc(g_in[q], 16)
                    for c in range(q * BQ, (q + 1) * BQ):
                        at = bass.IndirectOffsetOnAxis(ap=gi[:, 1 + c:2 + c], axis=0)
                        pool.indirect_dma_start(G[:, k, c, :], None, table, at).then_inc(g_in[q], 16)

            for q in range(Q):
                at = bass.IndirectOffsetOnAxis(ap=g["nid_i"][:, 0:1], axis=0)
                pool.indirect_dma_start(G[:, RING - 1, q, :], None, table, at).then_inc(g_in[q], 16)
            with pool.Fori(0, T) as t:
                blocks, before = sizes_of(pool, g, t)
                with pool.Fori(0, blocks) as j:
                    n = before + j
                    wait_count(pool, g_free, n + 1, g["pool_turns"])
                    with pool.If((n & 2) < 1):
                        with pool.If((n & 1) < 1):
                            gather(n, 0)
                        with pool.Else():
                            gather(n, 1)
                        pool.sem_inc(g["pool_turns"], 1)
                    with pool.Else():
                        with pool.If((n & 1) < 1):
                            gather(n, 2)
                        with pool.Else():
                            gather(n, 3)
                        pool.sem_inc(g["pool_turns"], 1)

        @block.vector
        def _(dve):
            for _ in range(RING):
                dve.sem_inc(g_free, 1)
            dve.sem_inc(res_out, 1)
            with dve.Fori(0, T) as t:
                st = Steps(dve, tile_steps, t * T_STEPS)
                st.after(dve.memset(acc[:, :], 0.0))
                blocks, before = sizes_of(dve, g, t)
                with dve.Fori(0, blocks) as j:
                    n = before + j
                    sb = Steps(dve, block_steps, n * B_STEPS)
                    Gn = G[:, bass.ds(n & (RING - 1), 1)].rearrange("p a k w -> p (a k) w")
                    An = AT[:, bass.ds(n & (RING - 1), 1)].rearrange("p a (k w) -> p (a k) w", w=D)
                    for q in range(Q):
                        wait_count(dve, g_in[q], (n + 1) * PARTS[q] + 16, g["v_turns"])
                    sb.after(dve.tensor_tensor(z[:, :, :], Gn, An, ALU.add))
                    dve.sem_inc(g_free, 1)
                    sb.after(dve.tensor_scalar(z[:, :, :], z[:, :, :], 0.0, None, ALU.max))
                    sb.after(dve.tensor_reduce(part[:, :], z[:, :, :].rearrange("p k w -> p w k"), AX.X, ALU.add))
                    sb.after(dve.tensor_tensor(acc[:, :], acc[:, :], part[:, :], ALU.add))
                    assert sb.n == B_STEPS, sb.n
                dve.wait_ge(res_out, t * 16 + 1)
                st.after(dve.tensor_copy(res[:, :], acc[:, :]))
                dve.sem_inc(res_ready, 1)
                assert st.n == T_STEPS, st.n

        @block.scalar
        def _(act):
            with act.Fori(0, T) as t:
                wait_count(act, res_ready, t + 1, g["act_turns"])
                act.dma_start(result[bass.ds(t * P, P), :], res[:, :]).then_inc(res_out, 16)
            act.wait_ge(res_out, 16 * T + 1)


def output_layer(nc, g, rows):
    with ExitStack() as ctx:
        s = Scope(nc, ctx)
        w = s.sb("ow", [D, D])
        brow = s.sb("obrow", [P, D])
        eps = s.sb("oeps", [P, 1])
        xt = s.sb("oxt", [P, D])
        xT = s.sb("oxT", [D, P])
        y = s.sb("oy", [P, D])
        tp = bank(g, 0)[:, 0:P]
        mp = bank(g, 1)
        w_in, comb_ready, x_ready, x_turned = s.sem("ow_in"), s.sem("comb_ready"), s.sem("ox_ready"), s.sem("ox_turned")
        xT_ready, projected, mp_free, v_steps = s.sem("oxT_ready"), s.sem("oprojected"), s.sem("omp_free"), s.sem("o_steps")
        out_done, x_done = s.sem("out_done"), s.sem("x_done")
        block = ctx.enter_context(nc.Block())
        full = N // P

        @block.sync
        def _(sp):
            sp.dma_start(w[:, :], g["L3_gnn_W_T"]).then_inc(w_in, 16)
            sp.dma_start(brow[:, :], g["L3_gnn_b"].partition_broadcast(P)).then_inc(w_in, 16)
            sp.dma_start(eps[:, :], g["L3_gnn_eps"].partition_broadcast(P)).then_inc(w_in, 16)
            sp.wait_ge(x_done, 1)
            sp.dma_start(g["out"][0:full * P, :].rearrange("(t p) f -> p t f", p=P),
                         g["X"][:, 0:full, :]).then_inc(out_done, 16)
            sp.dma_start(g["out"][full * P:N, :], g["X"][0:N - full * P, full, :]).then_inc(out_done, 16)
            sp.wait_ge(out_done, 32)

        @block.scalar
        def _(act):
            act.wait_ge(comb_ready, 1)
            with act.Fori(0, T) as t:
                act.copy(xt[:, :], g["H"][:, bass.ds(t, 1), :].squeeze(1)).then_inc(x_ready, 1)
                act.wait_ge(x_turned, t + 1)
                act.copy(xT[:, :], tp[0:D, :]).then_inc(xT_ready, 1)

        @block.tensor
        def _(pe):
            pe.wait_ge(w_in, 48)
            with pe.Fori(0, T) as t:
                wait_count(pe, x_ready, t + 1, g["pe_turns"])
                pe.transpose(tp[0:D, :], xt[:, :], g["ident"][:, :]).then_inc(x_turned, 1)
                pe.wait_ge(mp_free, t + 1)
                pe.wait_ge(xT_ready, t + 1)
                pe.matmul(mp[:, 0:D], xT[:, :], w[:, :], start=True, stop=True).then_inc(projected, 1)

        @block.vector
        def _(dve):
            st = Steps(dve, v_steps)
            dve.wait_ge(w_in, 48)
            st.after(dve.tensor_scalar(eps[:, :], eps[:, :], 1.0, None, ALU.add))
            H = g["H"][:, :, :].rearrange("p t f -> p (t f)")
            st.after(dve.scalar_tensor_tensor(out=H, in0=H, scalar=eps[:, 0:1],
                                              in1=rows[:, :, :].rearrange("p t f -> p (t f)"), op0=ALU.mult,
                                              op1=ALU.add))
            dve.sem_inc(comb_ready, 1)
            dve.sem_inc(mp_free, 1)
            first = st.n
            with dve.Fori(0, T) as t:
                st = Steps(dve, v_steps, first + 3 * t)
                dve.wait_ge(projected, t + 1)
                st.after(dve.tensor_tensor(y[:, :], mp[:, 0:D], brow[:, :], ALU.add))
                dve.sem_inc(mp_free, 1)
                st.after(dve.tensor_scalar(y[:, :], y[:, :], 0.0, None, ALU.max))
                xs = g["X"][:, bass.ds(t, 1), :].squeeze(1)
                st.after(dve.tensor_tensor(xs, xs, y[:, :], ALU.add))
            dve.sem_inc(x_done, 1)


def build(nc, io):
    with ExitStack() as ctx:
        g = persistent(nc, ctx, io)
        s = Scope(nc, ctx)
        prepare(nc, g)
        fill_slots(nc, g)
        scatter_pairs(nc, g)
        with ExitStack() as dense:
            g["A"] = dense.enter_context(nc.sbuf_tensor("A", [P, T, NP], BF16))
            read_pairs(nc, g)
            normalise(nc, g, first=True)
            aggregate(nc, g, g["L0_gnn_W_ssg"], g["L0_gnn_b_ssg"], own_degree=True, scale=0.5)
            tabs = [s.dram(f"TAB{i}", [NP + 1, w]) for i, w in enumerate((HC + H1, HC + H1, D + 1, D + 1))]
            heads1, heads2 = s.dram("HEADS1", [NP, HC]), s.dram("HEADS2", [NP, D])
            attention_tables(nc, g, g["H"], D, H1, C1, *[g[f"L0_gnn_{n}"] for n in ("W1l", "b1l", "W1r", "b1r", "att1")],
                             tabs[0], tabs[1])
            attend(nc, g, H1, C1, g["L0_gnn_att1"], g["L0_gnn_bias1"], tabs[0], tabs[1], heads1)
            with ExitStack() as c2:
                rows = c2.enter_context(nc.sbuf_tensor("heads_rows", [P, T, HC], F32))
                bring_rows(nc, g, heads1, rows, HC)
                attention_tables(nc, g, rows, HC, 1, D, *[g[f"L0_gnn_{n}"] for n in ("W2l", "b2l", "W2r", "b2r", "att2")],
                                 tabs[2], tabs[3])
            attend(nc, g, 1, D, g["L0_gnn_att2"], g["L0_gnn_bias2"], tabs[2], tabs[3], heads2)
            bring_rows(nc, g, heads2, g["H"], D)
            add_rows(nc, g, g["H"])
            normalise(nc, g)
            aggregate(nc, g, g["L1_gnn_W1"], g["L1_gnn_b1"], relu=True)
            aggregate(nc, g, g["L1_gnn_W2"], g["L1_gnn_b2"], relu=True)
            aggregate(nc, g, g["L1_gnn_W3"], g["L1_gnn_b3"], add_to_x=True)
        normalise(nc, g)
        pair_softmax(nc, g)
        normalise(nc, g)
        features, sums = s.dram("FEATURES", [NP + 1, D]), s.dram("SUMS", [NP, D])
        store_rows(nc, g, features)
        edge_sums(nc, g, features, sums)
        with ExitStack() as c3:
            rows = c3.enter_context(nc.sbuf_tensor("sum_rows", [P, T, D], F32))
            bring_rows(nc, g, sums, rows, D)
            output_layer(nc, g, rows)


def kernel(**inputs):
    import numpy as np
    import concourse.bacc as bacc
    from concourse.bass_utils import run_bass_kernel_spmd

    def padded(name, rows, value=0):
        a = np.asarray(inputs[name])
        out = np.full((rows,) + a.shape[1:], value, a.dtype)
        out[:a.shape[0]] = a
        return out

    arrays = {"x": padded("x", NP), "src": padded("src", ER), "dst": padded("dst", ER, NO_NODE),
              "edge_weight": padded("edge_weight", ER), "edge_attr_64": padded("edge_attr_64", ER)}
    for name in inputs:
        if name.startswith("L"):
            arrays[name] = np.ascontiguousarray(np.asarray(inputs[name]))
    arrays["L3_gnn_eps"] = arrays["L3_gnn_eps"].reshape(1)
    arrays["L3_gnn_W_T"] = np.ascontiguousarray(arrays.pop("L3_gnn_W").T)
    nc = bacc.Bacc("TRN2", target_bir_lowering=False, num_devices=1)
    io = {k: nc.dram_tensor(f"in_{k}", a.shape, mybir.dt.from_np(a.dtype), kind="ExternalInput").ap()
          for k, a in arrays.items()}
    io["out"] = nc.dram_tensor("out_x", (N, D), F32, kind="ExternalOutput").ap()
    build(nc, io)
    r = run_bass_kernel_spmd(nc, [{f"in_{k}": a for k, a in arrays.items()}], core_ids=[0])
    return r.results[0]["out_x"]
```

```python
import math
from contextlib import ExitStack

import concourse.bass as bass
from concourse import mybir

F32 = mybir.dt.float32
BF16 = mybir.dt.bfloat16
I32 = mybir.dt.int32
ALU = mybir.AluOpType
ACT = mybir.ActivationFunctionType
AX = mybir.AxisListType

P = 128
N = 3125
E = 103125
D = 64
H1, C1 = 12, 12
HC = H1 * C1
T = -(-N // P)
NP = T * P
EC = -(-E // P)
EP = EC * P
ER = EP + P
NO_NODE = 4095
S = 32
B = 8
SB = S // B
GB = B + 1
Q = 4
BQ = B // Q
HB = B // 2
GS = SB * GB
NO_ROW = NP
RING = 4
U = E // S + T + E // (P * S) + 4
OFF = NP * NP
BIG = 1.0e30
HG = 13
KEY_DEG = 4000


class Steps:

    def __init__(self, eng, sem, base=0):
        self.eng, self.sem, self.base, self.n = eng, sem, base, 0

    def mark(self, ins):
        ins.then_inc(self.sem, 1)
        self.n += 1

    def wait(self):
        self.eng.wait_ge(self.sem, self.base + self.n)

    def after(self, ins):
        self.mark(ins)
        self.wait()


def wait_count(eng, sem, count, turns):
    eng.wait_ge(sem, count)
    eng.sem_inc(turns, 1)


def free_bcast(ap, before, after):
    a = ap
    if before:
        a = a.unsqueeze(1)
        a = a.to_broadcast([a.shape[0], before] + list(a.shape[2:]))
    if after:
        a = a.unsqueeze(len(a.shape))
        a = a.to_broadcast(list(a.shape[:-1]) + [after])
    return a


class Scope:

    def __init__(self, nc, ctx):
        self.nc, self.ctx, self.id = nc, ctx, nc.next_id()
        self.sems = []
        ctx.callback(self.release)

    def release(self):
        if self.sems:
            self.nc.clear_and_free_semaphores(self.sems)
            self.nc.all_engine_barrier()

    def sb(self, name, shape, dt=F32):
        return self.ctx.enter_context(self.nc.sbuf_tensor(f"{name}_{self.id}", list(shape), dt))

    def sem(self, name):
        self.sems.append(self.nc.alloc_semaphore(f"{name}_{self.id}"))
        return self.sems[-1]

    def dram(self, name, shape, dt=F32):
        return self.nc.dram_tensor(name, list(shape), dt, kind="Internal").ap()


def bank(g, i):
    return g["banks"][:, i, :]


def sizes_of(eng, g, t):
    info = g["info"]
    return (eng.value_load(info[0:1, 0, bass.ds(t, 1)], min_val=1, max_val=SB * U),
            eng.value_load(info[0:1, 2, bass.ds(t, 1)], min_val=0, max_val=SB * U))


def halves_of(eng, g, t):
    return eng.value_load(g["info"][0:1, 5, bass.ds(t, 1)], min_val=1, max_val=2 * SB * U)


def persistent(nc, ctx, io):
    s = Scope(nc, ctx)
    g = dict(io)
    g["banks"] = ctx.enter_context(nc.psum_tensor("banks", [P, 8, 512], F32))
    g["X"] = s.sb("X", [P, T, D])
    g["iota_f"] = s.sb("iota_f", [P, P])
    g["iota_b"] = s.sb("iota_b", [P, P], BF16)
    g["pcol"] = s.sb("pcol", [P, 1])
    g["ident"] = s.sb("ident", [P, P])
    g["ident_b"] = s.sb("ident_b", [P, P], BF16)
    g["ones"] = s.sb("ones", [P, P])
    g["deg"] = s.sb("deg", [P, T])
    g["ni"] = s.sb("ni", [P, T, 4])
    g["nid_i"] = s.sb("nid_i", [P, T + 1], I32)
    g["info"] = s.sb("info", [1, 6, T], I32)
    g["PAIR"] = s.dram("PAIR", [NP * NP, 2])
    g["MS"] = s.dram("MS", [NP, 2])
    g["NI"] = s.dram("NI", [NP, 4])
    g["SLOT"] = s.dram("SLOT", [P, (U + T) * 3 * S])
    g["GIDX"] = s.dram("GIDX", [P, (U + T) * GS], I32)
    g["H"] = s.sb("H", [P, T, D])
    g["dinv"] = s.sb("dinv", [P, T])
    g["mout"] = s.sb("mout", [P, T])
    g["rank_i"] = s.sb("rank_i", [P, T], I32)
    g["sout"] = s.sb("sout", [P, T])
    g["cmax"] = s.sb("cmax_all", [P, 1])
    g["pool_turns"] = s.sem("pool_turns")
    g["pe_turns"] = s.sem("pe_turns")
    g["act_turns"] = s.sem("act_turns")
    g["v_turns"] = s.sem("v_turns")
    g["sp_turns"] = s.sem("sp_turns")
    g["pair_fill"] = s.sem("pair_fill")
    return g


def prepare(nc, g, fill):
    with ExitStack() as ctx:
        s = Scope(nc, ctx)
        dst_i = s.sb("dst_i", [P, EC], I32)
        part_i = s.sb("part_i", [P, 2, EC], I32)
        lo_b = s.sb("lo_b", [P, EC], BF16)
        hi_b = s.sb("hi_b", [P, EC], BF16)
        oh_lo = s.sb("oh_lo", [P, 2, HG, P], BF16)
        oh_hi = s.sb("oh_hi", [P, 2, HG, T], BF16)
        zero_b = s.sb("zero_b", [P, P], BF16)
        iota_i = s.sb("iota_i", [P, P], I32)
        pcol_i = s.sb("pcol_i", [P, 1], I32)
        node_i = s.sb("node_i", [P, T], I32)
        tri = s.sb("tri", [P, P])
        key = s.sb("key", [P, T])
        keyrow = s.sb("keyrow", [P, NP])
        dump_v = s.sb("dump_v", [P, NP], BF16)
        dump_a = s.sb("dump_a", [P, NP], BF16)
        greater = s.sb("greater", [P, T])
        sign_sum = s.sb("sign_sum", [P, T])
        rank_i = g["rank_i"]
        niw = s.sb("niw", [P, T, 4])
        small = s.sb("small", [P, 4, T])
        degs_c = s.sb("degs_c", [P, T])
        kcol = s.sb("kcol", [T, 1])
        krow = s.sb("krow", [1, T])
        krow_i = s.sb("krow_i", [1, 3, T], I32)
        row_f = s.sb("row_f", [1, 4, T])
        hist = bank(g, 0)
        pref = bank(g, 1)[:, 0:2 * T].rearrange("p (a t) -> p a t", a=2)
        kps = g["banks"][:, 2:4, :]
        kt = bank(g, 4)[:, 0:P]

        in_dst, in_x = s.sem("in_dst"), s.sem("in_x")
        fill_set = s.sem("fill_set")
        iotas = s.sem("iotas")
        v_steps = s.sem("v_steps")
        onehots_ready = [s.sem(f"onehots_ready{i}") for i in range(2)]
        oh_free = [s.sem(f"oh_free{i}") for i in range(2)]
        hist_done = s.sem("hist_done")
        consts_ready = s.sem("consts_ready")
        deg_ready, pref_done = s.sem("deg_ready"), s.sem("pref_done")
        key_ready, key_turned, key_copied = s.sem("key_ready"), s.sem("key_turned"), s.sem("key_copied")
        signs_done = s.sem("signs_done")
        ranks_ready, ni_written, ni_read = s.sem("ranks_ready"), s.sem("ni_written"), s.sem("ni_read")
        k_ready, k_turned = s.sem("k_ready"), s.sem("k_turned")
        block = ctx.enter_context(nc.Block())
        half_v = T // 2

        @block.sync
        def _(sp):
            sp.dma_start(dst_i[:, :], g["dst"][0:EP].rearrange("(p c) -> p c", p=P)).then_inc(in_dst, 16)
            sp.dma_start(g["X"][:, :, :], g["x"].rearrange("(t p) f -> p t f", p=P)).then_inc(in_x, 16)
            sp.wait_ge(ni_written, 16 * T)
            sp.dma_start(g["ni"][:, :, :], g["NI"].rearrange("(t p) c -> p t c", p=P)).then_inc(ni_read, 16)
            sp.wait_ge(in_x, 16)

        @block.gpsimd
        def _(pool):
            pool.iota(iota_i[:, :], [[1, P]], base=0, channel_multiplier=0).then_inc(iotas, 1)
            pool.iota(pcol_i[:, :], [[0, 1]], base=0, channel_multiplier=1).then_inc(iotas, 1)
            pool.iota(node_i[:, :], [[P, T]], base=0, channel_multiplier=1).then_inc(iotas, 1)
            pool.memset(fill[:, :, 0], 0.0).then_inc(fill_set, 1)
            pool.memset(fill[:, :, 1], -BIG).then_inc(fill_set, 1)
            pool.wait_ge(ranks_ready, 1)
            for t in range(T):
                pool.indirect_dma_start(g["NI"], bass.IndirectOffsetOnAxis(ap=rank_i[:, t:t + 1], axis=0),
                                        niw[:, t, :], None).then_inc(ni_written, 16)

        @block.tensor
        def _(pe):
            pe.wait_ge(consts_ready, 1)
            pe.matmul(hist[:, 0:T], zero_b[:, :], zero_b[:, 0:T], start=True, stop=False, skip_group_check=True)
            with pe.Fori(0, EC // (2 * HG)) as b:
                for i in range(2):
                    pe.wait_ge(onehots_ready[i], 2 * b + 2)
                    for c in range(HG):
                        mm = pe.matmul(hist[:, 0:T], oh_lo[:, i, c, :], oh_hi[:, i, c, :], start=False, stop=False,
                                       skip_group_check=True)
                    mm.then_inc(oh_free[i], 1)
            pe.matmul(hist[:, 0:T], zero_b[:, :], zero_b[:, 0:T], start=False, stop=True,
                      skip_group_check=True).then_inc(hist_done, 1)
            pe.wait_ge(deg_ready, 1)
            pe.matmul(pref[:, 0, :], tri[:, :], g["deg"][:, :], start=True, stop=True)
            pe.matmul(pref[:, 1, :], g["ones"][:, :], g["deg"][:, :], start=True, stop=True).then_inc(pref_done, 1)
            pe.wait_ge(key_ready, 1)
            for t in range(T):
                if t >= 8 and t % 4 == 0:
                    pe.wait_ge(key_copied, t // 4 - 1)
                mm = pe.transpose(kps[:, (t // 4) % 2, (t % 4) * P:(t % 4 + 1) * P],
                                  key[:, t:t + 1].to_broadcast([P, P]), g["ident"][:, :])
                if t % 4 == 3 or t == T - 1:
                    mm.then_inc(key_turned, 1)
            pe.wait_ge(k_ready, 1)
            pe.transpose(kt[0:T, :], degs_c[:, :], g["ident"][:, :]).then_inc(k_turned, 1)
            pe.wait_ge(k_ready, 2)
            pe.transpose(pref[0:1, 0, :], kcol[:, :], g["ident"][0:T, 0:T]).then_inc(k_turned, 1)

        @block.scalar
        def _(act):
            act.wait_ge(fill_set, 2)
            pair = g["PAIR"].rearrange("(t p d) c -> t p (d c)", t=T, p=P)
            for t in range(T):
                act.dma_start(pair[t], fill[:, :, :].rearrange("p d c -> p (d c)"),
                              max_dma_last_dim=8192).then_inc(g["pair_fill"], 16)
            for j in range(-(-T // 4)):
                act.wait_ge(key_turned, j + 1)
                w = min(4, T - 4 * j) * P
                act.copy(keyrow[:, 4 * j * P:4 * j * P + w], kps[:, j % 2, 0:w]).then_inc(key_copied, 1)
            act.wait_ge(key_copied, -(-T // 4))
            for t in range(half_v, T):
                act.activation(dump_a[:, :], keyrow[:, :], ACT.Sign, bias=key[:, t:t + 1], scale=-1.0,
                               accum_out=sign_sum[:, t:t + 1]).then_inc(signs_done, 1)
                act.wait_ge(signs_done, t - half_v + 1)

        @block.vector
        def _(dve):
            st = Steps(dve, v_steps)
            dve.wait_ge(iotas, 3)
            st.mark(dve.memset(zero_b[:, :], 0.0))
            st.mark(dve.memset(g["ones"][:, :], 1.0))
            st.mark(dve.tensor_copy(g["iota_f"][:, :], iota_i[:, :]))
            st.mark(dve.tensor_copy(g["iota_b"][:, :], iota_i[:, :]))
            st.after(dve.tensor_copy(g["pcol"][:, :], pcol_i[:, :]))
            st.mark(dve.tensor_scalar(tri[:, :], g["iota_f"][:, :], g["pcol"][:, 0:1], None, ALU.is_gt))
            st.mark(dve.tensor_scalar(g["ident"][:, :], g["iota_f"][:, :], g["pcol"][:, 0:1], None, ALU.is_equal))
            st.after(dve.tensor_scalar(g["ident_b"][:, :], g["iota_f"][:, :], g["pcol"][:, 0:1], None, ALU.is_equal))
            dve.sem_inc(consts_ready, 1)
            dve.wait_ge(in_dst, 16)
            st.mark(dve.tensor_scalar(part_i[:, 0, :], dst_i[:, :], P - 1, None, ALU.bitwise_and))
            st.after(dve.tensor_scalar(part_i[:, 1, :], dst_i[:, :], int(math.log2(P)), None, ALU.logical_shift_right))
            st.mark(dve.tensor_copy(lo_b[:, :], part_i[:, 0, :]))
            st.after(dve.tensor_copy(hi_b[:, :], part_i[:, 1, :]))
            for i in range(2):
                dve.sem_inc(oh_free[i], 1)
            with dve.Fori(0, EC // (2 * HG)) as b:
                for i in range(2):
                    dve.wait_ge(oh_free[i], b + 1)
                    dve.tensor_tensor(oh_lo[:, i], free_bcast(lo_b[:, bass.ds(b * 2 * HG + i * HG, HG)], 0, P),
                                      free_bcast(g["iota_b"][:, :], HG, 0), ALU.is_equal).then_inc(onehots_ready[i], 1)
                    dve.tensor_tensor(oh_hi[:, i], free_bcast(hi_b[:, bass.ds(b * 2 * HG + i * HG, HG)], 0, T),
                                      free_bcast(g["iota_b"][:, 0:T], HG, 0), ALU.is_equal).then_inc(onehots_ready[i], 1)
            dve.wait_ge(hist_done, 1)
            st.mark(dve.tensor_copy(g["deg"][:, :], hist[:, 0:T]))
            st.after(dve.tensor_copy(small[:, 3, :], node_i[:, :]))
            dve.sem_inc(deg_ready, 1)
            st.mark(dve.tensor_scalar(key[:, :], g["deg"][:, :], float(KEY_DEG), 4096.0, ALU.min, ALU.mult))
            st.after(dve.tensor_scalar(small[:, 0, :], small[:, 3, :], -1.0, 4095.0, ALU.mult, ALU.add))
            st.after(dve.tensor_tensor(key[:, :], key[:, :], small[:, 0, :], ALU.add))
            dve.sem_inc(key_ready, 1)
            dve.wait_ge(pref_done, 1)
            st.mark(dve.tensor_copy(niw[:, :, 0], small[:, 3, :]))
            st.mark(dve.tensor_copy(niw[:, :, 2], g["deg"][:, :]))
            st.mark(dve.memset(niw[:, :, 3], 0.0))
            st.after(dve.tensor_copy(small[:, 1, :], pref[:, 1, :]))
            st.after(dve.tensor_tensor_scan(small[:, 2, :], g["ones"][:, 0:T], small[:, 1, :], 0.0, ALU.mult, ALU.add))
            st.after(dve.tensor_tensor(small[:, 2, :], small[:, 2, :], small[:, 1, :], ALU.subtract))
            st.after(dve.tensor_tensor(niw[:, :, 1], small[:, 2, :], pref[:, 0, :], ALU.add))
            dve.wait_ge(key_copied, -(-T // 4))
            for t in range(half_v):
                st.after(dve.tensor_scalar(dump_v[:, :], keyrow[:, :], key[:, t:t + 1], 0.0, ALU.is_gt, ALU.add,
                                           accum_out=greater[:, t:t + 1]))
            dve.wait_ge(signs_done, T - half_v)
            st.after(dve.tensor_scalar(greater[:, half_v:T], sign_sum[:, half_v:T], -0.5, 0.5 * (NP - 1),
                                       ALU.mult, ALU.add))
            st.after(dve.tensor_copy(rank_i[:, :], greater[:, :]))
            dve.sem_inc(ranks_ready, 1)
            dve.wait_ge(ni_read, 16)
            st.mark(dve.memset(g["nid_i"][:, T:], 0))
            st.mark(dve.tensor_copy(g["nid_i"][:, 0:T], g["ni"][:, :, 0]))
            st.after(dve.tensor_copy(degs_c[:, :], g["ni"][:, :, 2]))
            dve.sem_inc(k_ready, 1)
            dve.wait_ge(k_turned, 1)
            st.after(dve.tensor_reduce(kcol[:, :], kt[0:T, :], AX.X, ALU.max))
            dve.sem_inc(k_ready, 1)
            dve.wait_ge(k_turned, 2)
            st.after(dve.tensor_copy(krow[:, :], pref[0:1, 0, :]))
            for i, size in enumerate((B, S)):
                st.after(dve.tensor_scalar(row_f[:, i, :], krow[:, :], 1.0, float(size - 1), ALU.max, ALU.add))
                st.after(dve.tensor_copy(krow_i[:, i, :], row_f[:, i, :]))
                st.after(dve.tensor_scalar(g["info"][:, i, :], krow_i[:, i, :], int(math.log2(size)), None,
                                           ALU.logical_shift_right))
                st.after(dve.tensor_copy(row_f[:, i, :], g["info"][:, i, :]))
                st.after(dve.tensor_tensor_scan(row_f[:, 2 + i, :], g["ones"][0:1, 0:T], row_f[:, i, :], 0.0,
                                                ALU.mult, ALU.add))
                st.after(dve.tensor_tensor(row_f[:, 2 + i, :], row_f[:, 2 + i, :], row_f[:, i, :], ALU.subtract))
                st.after(dve.tensor_copy(g["info"][:, 2 + i, :], row_f[:, 2 + i, :]))
            st.after(dve.tensor_scalar(krow[:, :], krow[:, :], 1.0, float(HB - 1), ALU.max, ALU.add))
            st.after(dve.tensor_copy(krow_i[:, 2, :], krow[:, :]))
            st.after(dve.tensor_scalar(g["info"][:, 5, :], krow_i[:, 2, :], int(math.log2(HB)), None,
                                       ALU.logical_shift_right))
            st.after(dve.tensor_reduce(krow[:, 0:1], row_f[:, 1, :], AX.X, ALU.max))
            st.after(dve.memset(g["info"][:, 4, :], 0))
            st.after(dve.tensor_copy(g["info"][:, 4, 0:1], krow[:, 0:1]))


def fill_slots(nc, g):
    with ExitStack() as ctx:
        s = Scope(nc, ctx)
        start_f = s.sb("start_f", [P, T])
        rem = s.sb("rem", [P, T])
        start_i = s.sb("start_i", [P, T], I32)
        srun = s.sb("srun", [P, T, S], I32)
        wrun = s.sb("wrun", [P, T, S])
        slot = s.sb("slot", [P, T, 3, S])
        place = s.sb("place", [P, S])
        gidx = s.sb("gidx", [P, T, SB, GB], I32)
        first_f = s.sb("first_f", [P, T, SB])
        blk = s.sb("blk", [P, SB])
        valid = s.sb("valid", [P, T, S])
        inval = s.sb("inval", [P, T, S])
        tmp = s.sb("tmp", [P, T, S])
        ubase = s.sb("ubase", [1, 6, T])
        u_i = s.sb("u_i", [1, T], I32)
        soft = s.sb("soft", [P, 4, T])
        expd = s.sb("expd", [P, T * S + T])
        msw = s.sb("msw", [P, T, 2])
        v_steps = s.sem("v2_steps")
        exp_in, exp_out = s.sem("exp_in"), s.sem("exp_out")
        ms_ready, ms_out = s.sem("ms_ready"), s.sem("ms_out")
        starts_ready, runs_in = s.sem("starts_ready"), s.sem("runs_in")
        slots_ready, slots_out = s.sem("slots_ready"), s.sem("slots_out")
        block = ctx.enter_context(nc.Block())
        NSTEP = 29

        @block.gpsimd
        def _(pool):
            rounds = pool.value_load(g["info"][0:1, 4, 0:1], min_val=1, max_val=U)
            with pool.Fori(0, rounds) as r:
                wait_count(pool, starts_ready, r + 1, g["pool_turns"])
                for t in range(T):
                    at = bass.IndirectOffsetOnAxis(ap=start_i[:, t:t + 1], axis=0)
                    pool.indirect_dma_start(srun[:, t, :], None, g["src"].unsqueeze(1), at).then_inc(runs_in, 16)
                    pool.indirect_dma_start(wrun[:, t, :], None, g["edge_weight"].unsqueeze(1), at).then_inc(runs_in, 16)
            pool.wait_ge(ms_ready, 2)
            for t in range(T):
                pool.indirect_dma_start(g["MS"], bass.IndirectOffsetOnAxis(ap=g["nid_i"][:, t:t + 1], axis=0),
                                        msw[:, t, :], None).then_inc(ms_out, 16)
            pool.wait_ge(ms_out, 16 * T)

        @block.scalar
        def _(act):
            rounds = act.value_load(g["info"][0:1, 4, 0:1], min_val=1, max_val=U)
            with act.Fori(0, rounds) as r:
                act.wait_ge(exp_in, r + 1)
                act.activation(expd[:, :], expd[:, :], ACT.Exp).then_inc(exp_out, 1)

        @block.vector
        def _(dve):
            st = Steps(dve, v_steps)
            rounds = dve.value_load(g["info"][0:1, 4, 0:1], min_val=1, max_val=U)
            st.mark(dve.tensor_copy(start_f[:, :], g["ni"][:, :, 1]))
            st.mark(dve.tensor_copy(rem[:, :], g["ni"][:, :, 2]))
            st.mark(dve.tensor_copy(ubase[:, 0:2, :], g["info"][:, 1:4:2, :]))
            st.mark(dve.memset(ubase[:, 2, :], 0.0))
            st.mark(dve.tensor_scalar(ubase[:, 5, :], g["iota_f"][0:1, 0:T], float(U), None, ALU.add))
            st.mark(dve.tensor_scalar(blk[:, :], g["iota_f"][:, 0:SB], float(B), None, ALU.mult))
            st.after(dve.tensor_scalar(place[:, :], g["iota_f"][:, 0:S], 1.0, None, ALU.add))
            st.mark(dve.memset(soft[:, 0, :], -BIG))
            st.after(dve.memset(soft[:, 1, :], 0.0))
            st.after(dve.tensor_scalar(start_i[:, :], start_f[:, :], float(E), None, ALU.min))
            dve.sem_inc(starts_ready, 1)
            first = st.n
            dve.sem_inc(slots_out, 1)
            with dve.Fori(0, rounds) as r:
                st = Steps(dve, v_steps, r * NSTEP + first)
                dve.wait_ge(slots_out, r * (2 * T * 16) + 1)
                st.after(dve.tensor_tensor(ubase[:, 3, :], ubase[:, 2, :], ubase[:, 0, :], ALU.is_lt))
                st.after(dve.tensor_scalar(ubase[:, 4, :], ubase[:, 3, :], -1.0, 1.0, ALU.mult, ALU.add))
                st.after(dve.tensor_tensor(ubase[:, 4, :], ubase[:, 4, :], ubase[:, 5, :], ALU.mult))
                st.after(dve.tensor_tensor(ubase[:, 3, :], ubase[:, 3, :], ubase[:, 1, :], ALU.mult))
                st.after(dve.tensor_tensor(u_i[:, :], ubase[:, 3, :], ubase[:, 4, :], ALU.add))
                st.mark(dve.tensor_tensor(valid[:, :, :], free_bcast(rem[:, :], 0, S),
                                          free_bcast(g["iota_f"][:, 0:S], T, 0), ALU.is_gt))
                st.mark(dve.tensor_copy(slot[:, :, 2, :], free_bcast(place[:, :], T, 0)))
                dve.wait_ge(runs_in, (r + 1) * (2 * T * 16))
                st.after(dve.tensor_copy(tmp[:, :, :], srun[:, :, :]))
                st.mark(dve.tensor_scalar(inval[:, :, :], valid[:, :, :], -1.0, None, ALU.add))
                st.after(dve.tensor_tensor(tmp[:, :, :], tmp[:, :, :], valid[:, :, :], ALU.mult))
                st.after(dve.tensor_tensor(slot[:, :, 0, :], tmp[:, :, :], inval[:, :, :], ALU.add))
                by_block = "p t (b k) -> p t b k"
                st.after(dve.scalar_tensor_tensor(out=gidx[:, :, :, 1:GB], in0=inval[:, :, :].rearrange(by_block, k=B),
                                                  scalar=-float(NO_ROW + 1),
                                                  in1=slot[:, :, 0, :].rearrange(by_block, k=B), op0=ALU.mult,
                                                  op1=ALU.add))
                st.after(dve.tensor_tensor(first_f[:, :, :], free_bcast(start_f[:, :], 0, SB), free_bcast(blk[:, :], T, 0),
                                           ALU.add))
                st.after(dve.tensor_scalar(gidx[:, :, :, 0], first_f[:, :, :], float(E), None, ALU.min))
                st.after(dve.tensor_tensor(tmp[:, :, :], wrun[:, :, :], valid[:, :, :], ALU.mult))
                st.after(dve.scalar_tensor_tensor(out=slot[:, :, 1, :], in0=inval[:, :, :], scalar=BIG,
                                                  in1=tmp[:, :, :], op0=ALU.mult, op1=ALU.add))
                dve.sem_inc(slots_ready, 1)
                st.after(dve.tensor_scalar(start_f[:, :], start_f[:, :], float(S), None, ALU.add))
                st.after(dve.tensor_scalar(start_i[:, :], start_f[:, :], float(E), None, ALU.min))
                dve.sem_inc(starts_ready, 1)
                st.mark(dve.tensor_scalar(rem[:, :], rem[:, :], -float(S), None, ALU.add))
                st.mark(dve.tensor_scalar(place[:, :], place[:, :], float(S), None, ALU.add))
                st.mark(dve.tensor_scalar(ubase[:, 1:3, :], ubase[:, 1:3, :], 1.0, None, ALU.add))
                weights = slot[:, :, 1, :]
                sums = expd[:, 0:T * S].rearrange("p (t k) -> p t k", k=S)
                st.after(dve.tensor_reduce(soft[:, 2, :], weights, AX.X, ALU.max))
                st.after(dve.tensor_tensor(soft[:, 2, :], soft[:, 2, :], soft[:, 0, :], ALU.max))
                st.mark(dve.tensor_tensor(expd[:, T * S:], soft[:, 0, :], soft[:, 2, :], ALU.subtract))
                st.after(dve.tensor_tensor(sums, weights, free_bcast(soft[:, 2, :], 0, S), ALU.subtract))
                dve.sem_inc(exp_in, 1)
                dve.wait_ge(exp_out, r + 1)
                st.mark(dve.tensor_copy(soft[:, 0, :], soft[:, 2, :]))
                st.mark(dve.tensor_reduce(soft[:, 3, :], sums, AX.X, ALU.add))
                st.after(dve.tensor_tensor(soft[:, 1, :], soft[:, 1, :], expd[:, T * S:], ALU.mult))
                st.after(dve.tensor_tensor(soft[:, 1, :], soft[:, 1, :], soft[:, 3, :], ALU.add))
                assert st.n == NSTEP, st.n
            dve.tensor_copy(msw[:, :, 0], soft[:, 0, :]).then_inc(ms_ready, 1)
            dve.tensor_copy(msw[:, :, 1], soft[:, 1, :]).then_inc(ms_ready, 1)

        @block.sync
        def _(sp):
            rounds = sp.value_load(g["info"][0:1, 4, 0:1], min_val=1, max_val=U)
            with sp.Fori(0, rounds) as r:
                wait_count(sp, slots_ready, r + 1, g["sp_turns"])
                for t in range(T):
                    u = sp.value_load(u_i[0:1, t:t + 1], min_val=0, max_val=U + T - 1)
                    sp.dma_start(g["SLOT"][:, bass.ds(u * (3 * S), 3 * S)],
                                 slot[:, t].rearrange("p c k -> p (c k)")).then_inc(slots_out, 16)
                    sp.dma_start(g["GIDX"][:, bass.ds(u * GS, GS)],
                                 gidx[:, t].rearrange("p b k -> p (b k)")).then_inc(slots_out, 16)
            wait_count(sp, slots_out, rounds * (2 * T * 16) + 1, g["sp_turns"])
            sp.wait_ge(g["pair_fill"], 16 * T)


def scatter_pairs(nc, g):
    with ExitStack() as ctx:
        s = Scope(nc, ctx)
        a = s.sb("sa", [P, 3, S])
        b = s.sb("sbb", [P, 3, S])
        differs = s.sb("differs", [P, S, S], BF16)
        zero_b = s.sb("sz", [P, P], BF16)
        places = s.sb("places", [P, 1])
        counted, counted_later = bank(g, 0)[:, 0:S], bank(g, 1)[:, 0:S]
        ex = s.sb("ex", [P, S * S + S])
        acc = s.sb("acc", [P, 2, S])
        new = s.sb("new", [P, 2, S])
        edges = s.sb("edges", [P, S])
        fin = s.sb("fin", [P, 4, S])
        dcol = s.sb("dcol", [P, 1])
        lns = s.sb("lns", [P, S])
        pair = s.sb("pair", [P, 2, S, 2])
        pair_at = s.sb("pair_at", [P, 2, S], I32)
        opened = s.sb("opened", [P, 2, 2])
        cmax = s.sb("cmax", [P, S])
        a_in, b_in, a_free, b_free = s.sem("a_in"), s.sem("b_in"), s.sem("a_free"), s.sem("b_free")
        tile_steps, sup_steps, pair_steps = s.sem("tile_steps"), s.sem("sup_steps"), s.sem("pair_steps")
        ex_in, ex_out, ln_in, ln_out = s.sem("ex_in"), s.sem("ex_out"), s.sem("ln_in"), s.sem("ln_out")
        entries_ready, entries_written = s.sem("entries_ready"), s.sem("entries_written")
        differs_ready, differs_free = s.sem("differs_ready"), s.sem("differs_free")
        counts_ready, counts_free, zero_ready = s.sem("counts_ready"), s.sem("counts_free"), s.sem("zero_ready")
        first_out, rest_out = s.sem("first_out"), s.sem("rest_out")
        block = ctx.enter_context(nc.Block())
        T_STEPS, U_STEPS, Q_STEPS = 1, 13, 11

        def sizes(eng, t):
            return (eng.value_load(g["info"][0:1, 1, bass.ds(t, 1)], min_val=1, max_val=U),
                    eng.value_load(g["info"][0:1, 3, bass.ds(t, 1)], min_val=0, max_val=U))

        @block.sync
        def _(sp):
            pairs = sp.alloc_register("sp_pairs")
            sp.reg_mov(pairs, 0)
            with sp.Fori(0, T) as t:
                rounds, base = sizes(sp, t)
                with sp.Fori(0, rounds) as r:
                    wait_count(sp, a_free, base + r + 1, g["sp_turns"])
                    sp.dma_start(a[:, :, :].rearrange("p c k -> p (c k)"),
                                 g["SLOT"][:, bass.ds(nc.s_assert_within(base + r, 0, U, skip_runtime_bounds_check_because="the tables are sized for it") * (3 * S), 3 * S)]).then_inc(a_in, 16)
                    with sp.Fori(0, rounds) as q:
                        n = sp.snap(pairs, min_val=0, max_val=1 << 23)
                        wait_count(sp, b_free, n + 1, g["sp_turns"])
                        sp.dma_start(b[:, :, :].rearrange("p c k -> p (c k)"),
                                     g["SLOT"][:, bass.ds(nc.s_assert_within(base + q, 0, U, skip_runtime_bounds_check_because="the tables are sized for it") * (3 * S), 3 * S)]).then_inc(b_in, 16)
                        sp.reg_add(pairs, pairs, 1)

        @block.vector
        def _(dve):
            pairs = dve.alloc_register("v_pairs")
            dve.reg_mov(pairs, 0)
            dve.sem_inc(a_free, 1)
            dve.sem_inc(b_free, 1)
            dve.sem_inc(entries_written, 1)
            dve.sem_inc(differs_free, 1)
            dve.sem_inc(counts_free, 1)
            dve.memset(zero_b[:, :], 0.0).then_inc(zero_ready, 1)
            dve.memset(cmax[:, :], 0.0).then_inc(tile_steps, 1)
            with dve.Fori(0, T) as t:
                rounds, base = sizes(dve, t)
                st = Steps(dve, tile_steps, t * T_STEPS + 1)
                st.after(dve.tensor_copy(dcol[:, :], g["ni"][:, bass.ds(t, 1), 0]))
                assert st.n == T_STEPS
                dve.sem_inc(g["v_turns"], 1)
                with dve.Fori(0, rounds) as r:
                    st = Steps(dve, sup_steps, (base + r) * U_STEPS)
                    st.mark(dve.memset(acc[:, 0, :], -BIG))
                    st.after(dve.memset(acc[:, 1, :], 0.0))
                    wait_count(dve, a_in, (base + r) * 16 + 16, g["v_turns"])
                    with dve.Fori(0, rounds) as q:
                        n = dve.snap(pairs, min_val=0, max_val=1 << 23)
                        sq = Steps(dve, pair_steps, n * Q_STEPS)
                        t_ex = ex[:, 0:S * S].rearrange("p (j k) -> p j k", k=S)
                        wait_count(dve, b_in, n * 16 + 16, g["v_turns"])
                        dve.wait_ge(differs_free, n + 1)
                        sq.after(dve.tensor_tensor(differs[:, :, :], free_bcast(a[:, 0, :], 0, S),
                                                   free_bcast(b[:, 0, :], S, 0), ALU.not_equal))
                        dve.sem_inc(differs_ready, 1)
                        sq.mark(dve.tensor_copy(places[:, :], b[:, 2, S - 1:S]))
                        sq.after(dve.scalar_tensor_tensor(out=t_ex, in0=differs[:, :, :], scalar=-BIG,
                                                          in1=free_bcast(b[:, 1, :], S, 0), op0=ALU.mult, op1=ALU.add))
                        dve.sem_inc(b_free, 1)
                        sq.after(dve.tensor_reduce(new[:, 0, :], t_ex, AX.X, ALU.max))
                        sq.after(dve.tensor_tensor(new[:, 0, :], acc[:, 0, :], new[:, 0, :], ALU.max))
                        sq.mark(dve.tensor_tensor(t_ex, t_ex, free_bcast(new[:, 0, :], 0, S), ALU.subtract))
                        sq.after(dve.tensor_tensor(ex[:, S * S:], acc[:, 0, :], new[:, 0, :], ALU.subtract))
                        dve.sem_inc(ex_in, 1)
                        sq.mark(dve.tensor_copy(acc[:, 0, :], new[:, 0, :]))
                        dve.wait_ge(ex_out, n + 1)
                        sq.mark(dve.tensor_reduce(new[:, 1, :], t_ex, AX.X, ALU.add))
                        sq.after(dve.tensor_tensor(acc[:, 1, :], acc[:, 1, :], ex[:, S * S:], ALU.mult))
                        sq.after(dve.tensor_tensor(acc[:, 1, :], acc[:, 1, :], new[:, 1, :], ALU.add))
                        assert sq.n == Q_STEPS, sq.n
                        dve.reg_add(pairs, pairs, 1)
                    dve.sem_inc(ln_in, 1)
                    st.mark(dve.tensor_scalar(fin[:, 1, :], a[:, 0, :], 0.0, None, ALU.is_ge))
                    st.mark(dve.tensor_scalar(fin[:, 2, :], a[:, 0, :], float(NP), dcol[:, 0:1], ALU.mult, ALU.add))
                    dve.wait_ge(counts_ready, base + r + 1)
                    st.mark(dve.tensor_scalar(edges[:, :], counted, -1.0, places[:, 0:1], ALU.mult, ALU.add))
                    st.after(dve.tensor_tensor(fin[:, 0, :], counted_later, a[:, 2, :], ALU.add))
                    dve.sem_inc(a_free, 1)
                    dve.sem_inc(counts_free, 1)
                    st.mark(dve.tensor_tensor(cmax[:, :], cmax[:, :], edges[:, :], ALU.max))
                    st.after(dve.tensor_scalar(fin[:, 0, :], fin[:, 0, :], places[:, 0:1], None, ALU.is_equal))
                    st.after(dve.tensor_tensor(fin[:, 0, :], fin[:, 0, :], fin[:, 1, :], ALU.mult))
                    st.after(dve.scalar_tensor_tensor(out=fin[:, 2, :], in0=fin[:, 2, :], scalar=-float(OFF),
                                                      in1=fin[:, 0, :], op0=ALU.add, op1=ALU.mult))
                    n = base + r
                    dve.wait_ge(entries_written, n + 1)
                    st.mark(dve.tensor_scalar(pair_at[:, bass.ds(n & 1, 1), :].squeeze(1), fin[:, 2, :], float(OFF),
                                              None, ALU.add))
                    st.mark(dve.tensor_copy(pair[:, bass.ds(n & 1, 1), :, 0].squeeze(1), edges[:, :]))
                    dve.wait_ge(ln_out, n + 1)
                    st.after(dve.tensor_tensor(pair[:, bass.ds(n & 1, 1), :, 1].squeeze(1), acc[:, 0, :], lns[:, :],
                                               ALU.add))
                    dve.sem_inc(entries_ready, 1)
                    assert st.n == U_STEPS, st.n
            st = Steps(dve, tile_steps, T * T_STEPS + 1)
            st.after(dve.tensor_reduce(g["cmax"][:, :], cmax[:, :], AX.X, ALU.max))

        @block.tensor
        def _(pe):
            pairs = pe.alloc_register("pe_pairs")
            pe.reg_mov(pairs, 0)

            def count(out, upto):
                for k in range(S):
                    if upto(k):
                        pe.matmul(out[:, 0:upto(k)], g["ident_b"][:, :], differs[:, 0:upto(k), k], start=False,
                                  stop=False, skip_group_check=True)

            pe.wait_ge(zero_ready, 1)
            with pe.Fori(0, T) as t:
                rounds, base = sizes(pe, t)
                with pe.Fori(0, rounds) as r:
                    wait_count(pe, counts_free, base + r + 1, g["pe_turns"])
                    for out in (counted, counted_later):
                        pe.matmul(out, zero_b[:, :], zero_b[:, 0:S], start=True, stop=False, skip_group_check=True)
                    with pe.Fori(0, rounds) as q:
                        n = pe.snap(pairs, min_val=0, max_val=1 << 23)
                        wait_count(pe, differs_ready, n + 1, g["pe_turns"])
                        count(counted, lambda k: S)
                        with pe.If(q > r):
                            count(counted_later, lambda k: S)
                        with pe.Else():
                            with pe.If(r > q):
                                pe.sem_inc(g["pe_turns"], 1)
                            with pe.Else():
                                count(counted_later, lambda k: k)
                            pe.sem_inc(g["pe_turns"], 1)
                        pe.matmul(counted, zero_b[:, :], zero_b[:, 0:S], start=False, stop=False,
                                  skip_group_check=True).then_inc(differs_free, 1)
                        pe.reg_add(pairs, pairs, 1)
                    for out in (counted, counted_later):
                        mm = pe.matmul(out, zero_b[:, :], zero_b[:, 0:S], start=False, stop=True, skip_group_check=True)
                    mm.then_inc(counts_ready, 1)

        @block.scalar
        def _(act):
            pairs = act.alloc_register("a_pairs")
            act.reg_mov(pairs, 0)
            with act.Fori(0, T) as t:
                rounds, base = sizes(act, t)
                with act.Fori(0, rounds) as r:
                    with act.Fori(0, rounds) as q:
                        n = act.snap(pairs, min_val=0, max_val=1 << 23)
                        act.wait_ge(ex_in, n + 1)
                        act.activation(ex[:, :], ex[:, :], ACT.Exp).then_inc(ex_out, 1)
                        act.reg_add(pairs, pairs, 1)
                    act.wait_ge(ln_in, base + r + 1)
                    act.activation(lns[:, :], acc[:, 1, :], ACT.Ln).then_inc(ln_out, 1)

        @block.gpsimd
        def _(pool):
            rest = pool.alloc_register("rest_count")
            pool.reg_mov(rest, 16)

            def scatter(n, k, halves, r):
                wait_count(pool, first_out, n * (HB * 16) + 16, g["pool_turns"])
                for j in range(2 * SB):
                    with pool.If(halves > r * (2 * SB) + j):
                        for c in range(HB * j, HB * j + HB):
                            at = bass.IndirectOffsetOnAxis(ap=pair_at[:, k, c:c + 1], axis=0)
                            pool.indirect_dma_start(g["PAIR"], at, pair[:, k, c, :], None, bounds_check=OFF - 1,
                                                    oob_is_err=False).then_inc(rest_out if j else first_out, 16)
                        if j:
                            pool.reg_add(rest, rest, HB * 16)
                    if j == 0:
                        wait_count(pool, rest_out, pool.snap(rest, min_val=16, max_val=1 << 30), g["pool_turns"])
                        pool.sem_inc(entries_written, 1)

            for i, sem in enumerate((first_out, rest_out)):
                at = bass.IndirectOffsetOnAxis(ap=g["nid_i"][:, 0:1], axis=0)
                pool.indirect_dma_start(opened[:, i, :], None, g["MS"], at).then_inc(sem, 16)
            with pool.Fori(0, T) as t:
                rounds, base = sizes(pool, t)
                halves = halves_of(pool, g, t)
                with pool.Fori(0, rounds) as r:
                    n = base + r
                    wait_count(pool, entries_ready, n + 1, g["pool_turns"])
                    with pool.If((n & 1) < 1):
                        scatter(n, 0, halves, r)
                    with pool.Else():
                        scatter(n, 1, halves, r)
            rounds, base = sizes(pool, T - 1)
            wait_count(pool, first_out, (base + rounds) * (HB * 16) + 16, g["pool_turns"])
            wait_count(pool, rest_out, pool.snap(rest, min_val=16, max_val=1 << 30), g["pool_turns"])


EXACT = 256
CH = 3
NCH = (T - 1) // CH
assert T == NCH * CH + 1


PIECES = 4


def read_pairs(nc, g):
    with ExitStack() as ctx:
        s = Scope(nc, ctx)
        width = NP // PIECES
        rows = [s.sb(f"rows{h}", [P, width, 2]) for h in range(PIECES)]
        minus_top = [s.sb(f"minus_top{h}", [P, 1]) for h in range(PIECES)]
        tops = s.sb("tops", [P, PIECES, T])
        sums = s.sb("sums", [P, PIECES, T])
        spread = s.sb("spread", [P, PIECES, T])
        dump = s.sb("dump", [P, width], BF16)
        rows_in = [s.sem(f"rows_in{h}") for h in range(PIECES)]
        rows_free = [s.sem(f"rows_free{h}") for h in range(PIECES)]
        top_ready = [s.sem(f"top_ready{h}") for h in range(PIECES)]
        part_ready = [s.sem(f"part_ready{h}") for h in range(PIECES)]
        v_steps = s.sem("v4_steps")
        spread_in, spread_out, most_turned = s.sem("spread_in"), s.sem("spread_out"), s.sem("most_turned")
        most = s.sb("most", [1, 1])
        block = ctx.enter_context(nc.Block())
        pairs = g["PAIR"].rearrange("(t p d) c -> t p (d c)", t=T, p=P)

        @block.sync
        def _(sp):
            with sp.Fori(0, T) as t:
                for h in range(PIECES):
                    wait_count(sp, rows_free[h], 2 * t + 2, g["sp_turns"])
                    sp.dma_start(rows[h][:, :, :].rearrange("p d c -> p (d c)"),
                                 pairs[bass.ds(t, 1), :, 2 * width * h:2 * width * (h + 1)].squeeze(0),
                                 max_dma_last_dim=8192).then_inc(rows_in[h], 16)

        @block.scalar
        def _(act):
            for h in range(PIECES):
                act.sem_inc(rows_free[h], 1)
            with act.Fori(0, T) as t:
                for h in range(PIECES):
                    act.wait_ge(rows_in[h], 16 * t + 16)
                    act.copy(g["A"][:, bass.ds(t, 1), width * h:width * (h + 1)].squeeze(1), rows[h][:, :, 0])
                    act.wait_ge(top_ready[h], t + 1)
                    act.activation(dump[:, :], rows[h][:, :, 1], ACT.Exp, bias=minus_top[h][:, 0:1],
                                   accum_out=sums[:, h, bass.ds(t, 1)]).then_inc(part_ready[h], 1)
                    act.wait_ge(part_ready[h], t + 2)
                    act.sem_inc(rows_free[h], 1)
            act.wait_ge(spread_in, 1)
            act.activation(spread[:, :, :], spread[:, :, :], ACT.Exp).then_inc(spread_out, 1)

        @block.tensor
        def _(pe):
            pe.transpose(bank(g, 0)[0:1, 0:P], g["cmax"][:, :], g["ident"][:, :]).then_inc(most_turned, 1)

        @block.vector
        def _(dve):
            for h in range(PIECES):
                dve.sem_inc(rows_free[h], 1)
                dve.sem_inc(part_ready[h], 1)
            with dve.Fori(0, T) as t:
                st = Steps(dve, v_steps, t * 2 * PIECES)
                for h in range(PIECES):
                    dve.wait_ge(rows_in[h], 16 * t + 16)
                    st.after(dve.tensor_reduce(tops[:, h, bass.ds(t, 1)], rows[h][:, :, 1], AX.X, ALU.max))
                    dve.sem_inc(rows_free[h], 1)
                    dve.wait_ge(part_ready[h], t + 1)
                    st.after(dve.tensor_scalar(minus_top[h][:, :], tops[:, h, bass.ds(t, 1)], -1.0, None, ALU.mult))
                    dve.sem_inc(top_ready[h], 1)
            st = Steps(dve, v_steps, T * 2 * PIECES)
            for h in range(PIECES):
                dve.wait_ge(part_ready[h], T + 1)
            dve.wait_ge(most_turned, 1)
            st.after(dve.tensor_reduce(most[:, :], bank(g, 0)[0:1, 0:P], AX.X, ALU.max))
            st.after(dve.tensor_copy(g["info"][0:1, 4, 1:2], most[:, :]))
            st.after(dve.tensor_reduce(g["mout"][:, :], tops[:, :, :].rearrange("p h t -> p t h"), AX.X, ALU.max))
            st.after(dve.tensor_tensor(spread[:, :, :], tops[:, :, :], free_bcast(g["mout"][:, :], PIECES, 0),
                                       ALU.subtract))
            dve.sem_inc(spread_in, 1)
            dve.wait_ge(spread_out, 1)
            st.after(dve.tensor_tensor(sums[:, :, :], sums[:, :, :], spread[:, :, :], ALU.mult))
            st.after(dve.tensor_reduce(g["sout"][:, :], sums[:, :, :].rearrange("p h t -> p t h"), AX.X, ALU.add))


def normalise(nc, g, first=False):
    with ExitStack() as ctx:
        s = Scope(nc, ctx)
        tmp = s.sb("ln_tmp", [P, T, D])
        st4 = s.sb("ln_st", [P, 4, 2 * T])
        v_steps, root_in, root_out = s.sem("ln_steps"), s.sem("root_in"), s.sem("root_out")
        block = ctx.enter_context(nc.Block())
        X, H = g["X"], g["H"]
        w = 2 * T if first else T

        @block.scalar
        def _(act):
            act.wait_ge(root_in, 1)
            act.activation(st4[:, 2, 0:w], st4[:, 1, 0:w], ACT.Sqrt).then_inc(root_out, 1)

        @block.vector
        def _(dve):
            st = Steps(dve, v_steps)
            st.after(dve.tensor_reduce(st4[:, 0, 0:T], X[:, :, :], AX.X, ALU.add))
            st.after(dve.tensor_scalar(st4[:, 0, 0:T], st4[:, 0, 0:T], 1.0 / D, None, ALU.mult))
            st.after(dve.tensor_tensor(H[:, :, :], X[:, :, :], free_bcast(st4[:, 0, 0:T], 0, D), ALU.subtract))
            st.after(dve.tensor_tensor(tmp[:, :, :], H[:, :, :], H[:, :, :], ALU.mult))
            st.after(dve.tensor_reduce(st4[:, 1, 0:T], tmp[:, :, :], AX.X, ALU.add))
            st.after(dve.tensor_scalar(st4[:, 1, 0:T], st4[:, 1, 0:T], 1.0 / D, 1e-5, ALU.mult, ALU.add))
            if first:
                st.after(dve.tensor_scalar(st4[:, 1, T:w], g["deg"][:, :], 1.0, None, ALU.add))
            dve.sem_inc(root_in, 1)
            dve.wait_ge(root_out, 1)
            st.after(dve.reciprocal(st4[:, 3, 0:w], st4[:, 2, 0:w]))
            st.after(dve.tensor_tensor(st4[:, 2, 0:w], st4[:, 3, 0:w], st4[:, 3, 0:w], ALU.mult))
            st.after(dve.tensor_tensor(st4[:, 2, 0:w], st4[:, 2, 0:w], st4[:, 1, 0:w], ALU.mult))
            st.after(dve.tensor_scalar(st4[:, 2, 0:w], st4[:, 2, 0:w], -0.5, 1.5, ALU.mult, ALU.add))
            st.after(dve.tensor_tensor(st4[:, 3, 0:w], st4[:, 3, 0:w], st4[:, 2, 0:w], ALU.mult))
            if first:
                st.after(dve.tensor_copy(g["dinv"][:, :], st4[:, 3, T:w]))
            st.after(dve.tensor_tensor(H[:, :, :], H[:, :, :], free_bcast(st4[:, 3, 0:T], 0, D), ALU.mult))
            st.after(dve.tensor_scalar(H[:, :, :], H[:, :, :], 0.0, None, ALU.max))


def aggregate(nc, g, weight, bias, own_degree=False, scale=1.0, relu=False, add_to_x=False):
    with ExitStack() as ctx:
        s = Scope(nc, ctx)
        tmp = s.sb("ag_tmp", [P, T, D])
        parts = s.sb("ag_parts", [P, T, 3, D], BF16)
        w2 = s.sb("ag_w", [P, D])
        brow = s.sb("ag_b", [P, D])
        o1 = s.sb("ag_o1", [P, CH * P])
        o2 = s.sb("ag_o2", [D, CH * P])
        sv = s.sb("ag_sv", [P, 4, T])
        dparts = s.sb("ag_dparts", [P, 3, T], BF16)
        diag = s.sb("ag_diag", [P, CH, 3, P], BF16)
        pj = bank(g, 4)
        lack = s.sb("ag_lack", [P, CH * P])
        counts = s.sb("ag_counts", [P, CH * P, 2])
        one_tile = s.sb("ag_one_tile", [P, D])
        counts_in, counts_free, lack_ready, lack_used = (
            s.sem(n) for n in ("counts_in", "ag_counts_free", "lack_ready", "lack_used"))
        w_in, v_steps = s.sem("w_in"), s.sem("ag_steps")
        parts_ready, diag_ready = s.sem("parts_ready"), s.sem("diag_ready")
        chunk_done, o1_ready, o2_ready = s.sem("chunk_done"), s.sem("o1_ready"), s.sem("o2_ready")
        pj_done, pj_free = s.sem("pj_done"), s.sem("pj_free")
        loop_steps = s.sem("ag_loop_steps")
        a_part = s.sem("a_part")
        block = ctx.enter_context(nc.Block())
        H = g["H"]
        pairs = g["PAIR"].rearrange("(t p d) c -> t p (d c)", t=T, p=P)
        nself = 3 if own_degree else 1

        def sums(c, third):
            return g["banks"][:, bass.ds((c & 1) + 2 * third, 1), :].squeeze(1)

        def most_edges(eng):
            return eng.value_load(g["info"][0:1, 4, 1:2], min_val=0, max_val=E)

        @block.sync
        def _(sp):
            def load_counts(c, tiles, t0):
                with sp.Fori(0, T) as t:
                    wait_count(sp, counts_free, c * T + t + 1, g["sp_turns"])
                    sp.dma_start(counts[:, 0:tiles * P, :].rearrange("p d c -> p (d c)"),
                                 pairs[bass.ds(t, 1), :, bass.ds(t0 * 2 * P, tiles * 2 * P)].squeeze(0))\
                        .then_inc(counts_in, 16)

            for i in range(2):
                sp.dma_start(w2[i * D:(i + 1) * D, :], weight).then_inc(w_in, 16)
            sp.dma_start(brow[:, :], bias.partition_broadcast(P)).then_inc(w_in, 16)
            with sp.If(most_edges(sp) > EXACT):
                with sp.Fori(0, NCH) as c:
                    load_counts(c, CH, c * CH)
                load_counts(NCH, 1, NCH * CH)
            with sp.Else():
                sp.sem_inc(g["sp_turns"], 1)

        @block.vector
        def _(dve):
            st = Steps(dve, v_steps)
            dv = free_bcast(g["dinv"][:, :], 0, D)
            st.after(dve.tensor_tensor(H[:, :, :], H[:, :, :], dv, ALU.mult))
            st.after(dve.tensor_copy(parts[:, :, 0, :], H[:, :, :]))
            st.after(dve.tensor_tensor(tmp[:, :, :], H[:, :, :], parts[:, :, 0, :], ALU.subtract))
            st.after(dve.tensor_copy(parts[:, :, 1, :], tmp[:, :, :]))
            st.after(dve.tensor_tensor(parts[:, :, 2, :], tmp[:, :, :], parts[:, :, 1, :], ALU.subtract))
            st.after(dve.tensor_scalar(sv[:, 0, :], g["dinv"][:, :], scale, None, ALU.mult))
            if own_degree:
                st.after(dve.tensor_scalar(sv[:, 1, :], g["deg"][:, :], 2.0, None, ALU.add))
                st.after(dve.tensor_copy(dparts[:, 0, :], sv[:, 1, :]))
                st.after(dve.tensor_tensor(sv[:, 2, :], sv[:, 1, :], dparts[:, 0, :], ALU.subtract))
                st.after(dve.tensor_copy(dparts[:, 1, :], sv[:, 2, :]))
                st.after(dve.tensor_tensor(dparts[:, 2, :], sv[:, 2, :], dparts[:, 1, :], ALU.subtract))
            else:
                st.after(dve.memset(dparts[:, 0, :], 1.0))
            dve.sem_inc(parts_ready, 1)
            st.after(dve.tensor_copy(tmp[:, :, :], H[:, :, :]))
            for sem in (pj_free, pj_done, counts_free, lack_used):
                dve.sem_inc(sem, 1)

            def diagonals(c, tiles, t0, steps):
                if not isinstance(c, int) or c:
                    dve.wait_ge(chunk_done, c)
                for j in range(tiles):
                    for i in range(nself):
                        steps.mark(dve.tensor_tensor(diag[:, j, i, :], g["ident_b"][:, :],
                                                     dparts[:, i, bass.ds(t0 + j, 1)].to_broadcast([P, P]),
                                                     ALU.mult))
                steps.wait()
                dve.sem_inc(diag_ready, 1)

            def find_lack(c, tiles, t0):
                dve.sem_inc(g["v_turns"], 1)
                with dve.If(many > EXACT):
                    with dve.Fori(0, T) as t:
                        wait_count(dve, counts_in, (c * T + t) * 16 + 16, g["v_turns"])
                        wait_count(dve, lack_used, c * T + t + 1, g["v_turns"])
                        dve.tensor_tensor(lack[:, 0:tiles * P], counts[:, 0:tiles * P, 0],
                                          g["A"][:, bass.ds(t, 1), bass.ds(t0 * P, tiles * P)].squeeze(1),
                                          ALU.subtract).then_inc(lack_ready, 1)
                        dve.tensor_copy(one_tile[:, :], tmp[:, bass.ds(t, 1), :].squeeze(1)).then_inc(lack_ready, 1)
                        wait_count(dve, lack_ready, (c * T + t) * 2 + 2, g["v_turns"])
                        dve.sem_inc(counts_free, 1)
                with dve.Else():
                    dve.sem_inc(g["v_turns"], 1)

            def finish(c, tiles, t0, steps):
                dve.wait_ge(chunk_done, c + 1)
                steps.after(dve.tensor_copy(o2[:, 0:tiles * P], sums(c, 1)[0:D, 0:tiles * P]))
                dve.sem_inc(o2_ready, 1)
                dve.wait_ge(pj_done, c + 2)
                steps.after(dve.tensor_tensor(H[:, bass.ds(t0, tiles), :],
                                              pj[:, 0:tiles * D].rearrange("p (t f) -> p t f", f=D),
                                              free_bcast(sv[:, 0, bass.ds(t0, tiles)], 0, D), ALU.mult))
                dve.sem_inc(pj_free, 1)

            n = CH * nself + 2
            many = most_edges(dve)
            diagonals(0, CH, 0, st)
            find_lack(0, CH, 0)
            with dve.Fori(0, NCH - 1) as c:
                loop = Steps(dve, loop_steps, c * n)
                diagonals(c + 1, CH, (c + 1) * CH, loop)
                find_lack(c + 1, CH, (c + 1) * CH)
                finish(c, CH, c * CH, loop)
            diagonals(NCH, 1, NCH * CH, st)
            find_lack(NCH, 1, NCH * CH)
            finish(NCH - 1, CH, (NCH - 1) * CH, st)
            finish(NCH, 1, NCH * CH, st)
            dve.wait_ge(w_in, 48)
            st.after(dve.tensor_tensor(H[:, :, :], H[:, :, :], free_bcast(brow[:, :], T, 0), ALU.add))
            if relu:
                st.after(dve.tensor_scalar(H[:, :, :], H[:, :, :], 0.0, None, ALU.max))
            if add_to_x:
                st.after(dve.tensor_tensor(g["X"][:, :, :], g["X"][:, :, :], H[:, :, :], ALU.add))

        @block.scalar
        def _(act):
            with act.Fori(0, NCH) as c:
                act.wait_ge(chunk_done, c + 1)
                act.wait_ge(pj_done, c + 1)
                act.copy(o1[:, :], sums(c, 0)[:, 0:CH * P]).then_inc(o1_ready, 1)
            act.wait_ge(chunk_done, NCH + 1)
            act.wait_ge(pj_done, NCH + 1)
            act.copy(o1[:, 0:P], sums(NCH, 0)[:, 0:P]).then_inc(o1_ready, 1)

        @block.tensor
        def _(pe):
            pe.wait_ge(parts_ready, 1)
            pe.wait_ge(w_in, 48)

            def add_up(c, tiles, t0):
                w = tiles * P
                c1, c2 = sums(c, 0), sums(c, 1)
                for src in range(T):
                    moving = g["A"][:, src, bass.ds(t0 * P, w)]
                    pe.matmul(c1[:, 0:w], parts[:, src, 0:2, :].rearrange("p a f -> p (a f)"), moving,
                              start=(src == 0), stop=False, skip_group_check=True)
                    pe.matmul(c2[0:D, 0:w], parts[:, src, 2, :], moving, start=(src == 0), stop=False,
                              skip_group_check=True)
                with pe.If(many > EXACT):
                    with pe.Fori(0, T) as t:
                        wait_count(pe, lack_ready, (c * T + t) * 2 + 2, g["pe_turns"])
                        pe.matmul(c2[0:D, 0:w], one_tile[:, :], lack[:, 0:w], start=False, stop=False,
                                  skip_group_check=True).then_inc(lack_used, 1)
                with pe.Else():
                    pe.sem_inc(g["pe_turns"], 1)
                wait_count(pe, diag_ready, c + 1, g["pe_turns"])
                for j in range(tiles):
                    for i in range(nself):
                        last = i == nself - 1
                        own = parts[:, bass.ds(t0 + j, 1), :, :].rearrange("p t a f -> p (t a f)")
                        pe.matmul(c1[:, j * P:(j + 1) * P], own[:, 0:2 * D], diag[:, j, i, :], start=False,
                                  stop=last, skip_group_check=True)
                        mm = pe.matmul(c2[0:D, j * P:(j + 1) * P], own[:, 2 * D:3 * D], diag[:, j, i, :],
                                       start=False, stop=last, skip_group_check=True)
                mm.then_inc(chunk_done, 1)

            def project(c, tiles):
                pe.wait_ge(o1_ready, c + 1)
                pe.wait_ge(o2_ready, c + 1)
                pe.wait_ge(pj_free, c + 1)
                for j in range(tiles):
                    pe.matmul(pj[:, j * D:(j + 1) * D], o1[:, j * P:(j + 1) * P], w2[:, :], start=True, stop=False)
                    mm = pe.matmul(pj[:, j * D:(j + 1) * D], o2[:, j * P:(j + 1) * P], w2[0:D, :], start=False,
                                   stop=True)
                mm.then_inc(pj_done, 1)

            many = most_edges(pe)
            add_up(0, CH, 0)
            with pe.Fori(0, NCH - 1) as c:
                add_up(c + 1, CH, (c + 1) * CH)
                project(c, CH)
            add_up(NCH, 1, NCH * CH)
            project(NCH - 1, CH)
            project(NCH, 1)


def bring_rows(nc, g, table, rows, width):
    with ExitStack() as ctx:
        s = Scope(nc, ctx)
        rows_in = s.sem("brought")
        block = ctx.enter_context(nc.Block())

        @block.gpsimd
        def _(pool):
            for t in range(T):
                at = bass.IndirectOffsetOnAxis(ap=g["rank_i"][:, t:t + 1], axis=0)
                pool.indirect_dma_start(rows[:, t, 0:width], None, table, at).then_inc(rows_in, 16)
            pool.wait_ge(rows_in, 16 * T)


GT = 4
assert T % GT


def attention_tables(nc, g, rows, k_dim, heads, chans, wl, bl, wr, br, att, left, right):
    hc = heads * chans
    chunks = [(k, min(P, k_dim - k)) for k in range(0, k_dim, P)]
    with ExitStack() as ctx:
        s = Scope(nc, ctx)
        w = s.sb("at_w", [P, len(chunks), 2, hc])
        b = s.sb("at_b", [P, 2, hc])
        a = s.sb("at_a", [P, 2, hc])
        xt = s.sb("at_xt", [P, GT, k_dim])
        xT = s.sb("at_xT", [P, len(chunks), GT, P])
        out = s.sb("at_out", [P, 2, GT, hc + heads])
        prod = s.sb("at_prod", [P, GT, hc])
        none = s.sb("at_none", [1, hc + heads])
        w_in, x_ready, x_turned, xT_ready = s.sem("aw_in"), s.sem("x_ready"), s.sem("x_turned"), s.sem("xT_ready")
        projected, rows_out, v_steps = s.sem("projected"), s.sem("rows_out"), s.sem("at_steps")
        rows_ready, mp_free = s.sem("rows_ready"), s.sem("mp_free")
        none_ready, none_out = s.sem("none_ready"), s.sem("none_out")
        block = ctx.enter_context(nc.Block())
        att_row = att.rearrange("h c -> (h c)")

        def turned(j):
            return bank(g, j).rearrange("p (t n) -> p t n", n=P)

        def product(i):
            return bank(g, 2 + i)[:, 0:2 * hc]

        def groups(eng, body):
            with eng.Fori(0, T // GT) as i:
                body(i, i * GT, GT)
            body(T // GT, T // GT * GT, T % GT)

        @block.sync
        def _(sp):
            for i, (wd, bd) in enumerate(((wl, bl), (wr, br))):
                for j, (k, n) in enumerate(chunks):
                    sp.dma_start(w[0:n, j, i, :], wd[k:k + n, :]).then_inc(w_in, 16)
                sp.dma_start(b[:, i, :], bd.partition_broadcast(P)).then_inc(w_in, 16)
                sp.dma_start(a[:, i, :], att_row.partition_broadcast(P)).then_inc(w_in, 16)
            sp.wait_ge(none_ready, 1)
            for table in (left, right):
                sp.dma_start(table[NO_ROW:NO_ROW + 1, :], none[:, :]).then_inc(none_out, 16)
            sp.wait_ge(none_out, 32)

            def body(i, t0, tiles):
                wait_count(sp, rows_ready, i + 1, g["sp_turns"])
                for k, table in enumerate((left, right)):
                    sp.dma_start(table[bass.ds(t0 * P, tiles * P), :].rearrange("(t p) w -> p t w", p=P),
                                 out[:, k, 0:tiles, :]).then_inc(rows_out, 16)
            groups(sp, body)
            sp.wait_ge(rows_out, 32 * (T // GT + 1) + 1)
        n_w = 16 * 2 * (len(chunks) + 2)

        @block.scalar
        def _(act):
            def body(i, t0, tiles):
                act.copy(xt[:, 0:tiles, :], rows[:, bass.ds(t0, tiles), 0:k_dim]).then_inc(x_ready, 1)
                act.wait_ge(x_turned, i + 1)
                for j, (k, n) in enumerate(chunks):
                    act.copy(xT[0:n, j, 0:tiles, :], turned(j)[0:n, 0:tiles, :]).then_inc(xT_ready, 1)
            groups(act, body)

        @block.tensor
        def _(pe):
            pe.wait_ge(w_in, n_w)

            def body(i, t0, tiles):
                wait_count(pe, x_ready, i + 1, g["pe_turns"])
                for t in range(tiles):
                    for j, (k, n) in enumerate(chunks):
                        mm = pe.transpose(turned(j)[0:n, t, :], xt[:, t, k:k + n], g["ident"][:, :])
                mm.then_inc(x_turned, 1)
                pe.wait_ge(xT_ready, (i + 1) * len(chunks))
                pe.wait_ge(mp_free, i + 1)
                for t in range(tiles):
                    for j, (k, n) in enumerate(chunks):
                        mm = pe.matmul(product(t), xT[0:n, j, t, :], w[0:n, j].rearrange("p i c -> p (i c)"),
                                       start=(j == 0), stop=(j == len(chunks) - 1))
                mm.then_inc(projected, 1)
            groups(pe, body)

        @block.vector
        def _(dve):
            dve.wait_ge(w_in, n_w)
            st = Steps(dve, v_steps)
            st.mark(dve.memset(none[:, 0:hc], 0.0))
            st.mark(dve.memset(none[:, hc:], -BIG))
            st.after(dve.tensor_scalar(a[:, :, :], a[:, :, :], 0.2, None, ALU.mult))
            dve.sem_inc(none_ready, 1)
            first = st.n
            dve.sem_inc(rows_out, 1)
            dve.sem_inc(mp_free, 1)

            def body(i, t0, tiles):
                st = Steps(dve, v_steps, first + i * 6)
                dve.wait_ge(projected, i + 1)
                dve.wait_ge(rows_out, 32 * i + 1)
                for k in range(2):
                    sums = g["banks"][:, 2:2 + tiles, k * hc:(k + 1) * hc]
                    st.mark(dve.tensor_tensor(out[:, k, 0:tiles, 0:hc], sums, free_bcast(b[:, k, :], tiles, 0), ALU.add))
                st.wait()
                dve.sem_inc(mp_free, 1)
                for k in range(2):
                    st.after(dve.tensor_tensor(prod[:, 0:tiles, :], out[:, k, 0:tiles, 0:hc],
                                               free_bcast(a[:, k, :], tiles, 0), ALU.mult))
                    st.after(dve.tensor_reduce(out[:, k, 0:tiles, hc:],
                                               prod[:, 0:tiles, :].rearrange("p t (h c) -> p t h c", c=chans), AX.X,
                                               ALU.add))
                dve.sem_inc(rows_ready, 1)
            groups(dve, body)


def block_column(nc, base, j):
    return nc.s_assert_within(base * GS + j * GB, 0, (U + T - 1) * GS,
                              skip_runtime_bounds_check_because="the tables are sized for it")


def attend(nc, g, heads, chans, att, bias, left, right, result):
    hc, wd = heads * chans, heads * (chans + 1)
    gs = 3 if 4 * wd > 512 else 4
    groups = [(k, min(gs, B - k)) for k in range(0, B, gs)]
    nb = len(groups)
    assert gs * wd <= 512 and 2 * nb + 1 <= 8
    with ExitStack() as ctx:
        s = Scope(nc, ctx)
        G = s.sb("gathered", [P, RING, B, wd])
        gi = s.sb("gat_idx", [P, GB], I32)
        nidc = s.sb("nidc", [P, 1], I32)
        own = s.sb("own", [P, 2, 2, wd])
        res = s.sb("res", [P, hc])
        z = g["H"][:, :, :].rearrange("p t f -> p (t f)")[:, 0:B * hc].rearrange("p (k w) -> p k w", w=hc)
        zo = s.sb("zo", [P, wd])
        wgt = s.sb("wgt", [P, B + 1, heads, chans + 1])
        arow = s.sb("arow", [P, hc])
        brow = s.sb("gbrow", [P, hc])
        num = s.sb("num", [P, heads, chans + 1])
        sm = s.sb("sm", [P, 5, heads])
        lg = s.sb("lg", [P, B, heads])
        ex = s.sb("gat_ex", [P, B + 1, heads])
        own_in, res_ready, res_out = s.sem("own_in"), s.sem("res_ready"), s.sem("res_out")
        consts_in, tile_done = s.sem("gc_in"), s.sem("tile_done")
        nid_ready, g_free = s.sem("nid_ready"), s.sem("g_free")
        idx_in, g_in = [[s.sem(f"{n}{q}") for q in range(Q)] for n in ("idx_in", "g_in")]
        tile_steps, block_steps, sum_steps, c_steps = (s.sem(n) for n in ("gt_steps", "gb_steps", "gd_steps", "gc_steps"))
        blank_ready = s.sem("blank_ready")
        z_ready, z_free = s.sem("z_ready"), s.sem("z_free")
        wgt_ready, sum_ready = s.sem("wgt_ready"), s.sem("sum_ready")
        ex_ready, ex_done = s.sem("gex_ready"), s.sem("gex_done")
        block = ctx.enter_context(nc.Block())
        runs = [(0, nb, gs)] if B % gs == 0 else [(0, nb - 1, gs), (nb - 1, 1, B % gs)]
        T_STEPS, B_STEPS, D_STEPS = 9, nb + len(runs) + 8, 2
        PART = BQ * 16

        @block.sync
        def _(sp):
            sp.dma_start(arow[:, :], att.rearrange("h c -> (h c)").partition_broadcast(P)).then_inc(consts_in, 16)
            sp.dma_start(brow[:, :], bias.partition_broadcast(P)).then_inc(consts_in, 16)
            whole = sp.alloc_register(f"sp_whole_{s.id}")
            sp.reg_mov(whole, 0)

            def load_part(q, base, j, n):
                wait_count(sp, g_in[q], n * PART + 16, g["sp_turns"])
                a, w = (1 + q * BQ, BQ) if q else (0, 1 + BQ)
                sp.dma_start(gi[:, a:a + w], g["GIDX"][:, bass.ds(block_column(nc, base, j) + a, w)])\
                    .then_inc(idx_in[q], 16)

            with sp.Fori(0, T) as t:
                halves = halves_of(sp, g, t)
                blocks, before = sizes_of(sp, g, t)
                base = sp.value_load(g["info"][0:1, 3, bass.ds(t, 1)], min_val=0, max_val=U)
                with sp.Fori(0, blocks) as j:
                    for q in range(Q // 2):
                        load_part(q, base, j, before + j)
                    with sp.If(halves > 2 * j + 1):
                        n = sp.snap(whole, min_val=0, max_val=SB * U)
                        for q in range(Q // 2, Q):
                            load_part(q, base, j, n)
                        sp.reg_add(whole, whole, 1)
                    with sp.Else():
                        sp.sem_inc(g["sp_turns"], 1)

        @block.gpsimd
        def _(pool):
            def own_rows(k):
                for i, table in enumerate((left, right)):
                    at = bass.IndirectOffsetOnAxis(ap=nidc[:, :], axis=0)
                    pool.indirect_dma_start(own[:, k, i, :], None, table, at).then_inc(own_in, 16)

            whole = pool.alloc_register(f"pool_whole_{s.id}")
            pool.reg_mov(whole, 0)

            def gather_part(q, n, k):
                wait_count(pool, idx_in[q], n * 16 + 16, g["pool_turns"])
                for c in range(q * BQ, (q + 1) * BQ):
                    at = bass.IndirectOffsetOnAxis(ap=gi[:, 1 + c:2 + c], axis=0)
                    pool.indirect_dma_start(G[:, k, c, :], None, left, at).then_inc(g_in[q], 16)

            def gather(n, k, both):
                for q in range(Q // 2):
                    gather_part(q, n, k)
                with pool.If(both):
                    m = pool.snap(whole, min_val=0, max_val=SB * U)
                    for q in range(Q // 2, Q):
                        gather_part(q, m, k)
                    pool.reg_add(whole, whole, 1)
                with pool.Else():
                    pool.memset(G[:, k, HB:B, 0:hc], 0.0).then_inc(blank_ready, 1)
                    pool.memset(G[:, k, HB:B, hc:wd], -BIG).then_inc(blank_ready, 1)
                pool.sem_inc(g["pool_turns"], 1)
            for q in range(Q):
                at = bass.IndirectOffsetOnAxis(ap=g["nid_i"][:, 0:1], axis=0)
                pool.indirect_dma_start(G[:, RING - 1, q, :], None, left, at).then_inc(g_in[q], 16)
            pool.tensor_copy(nidc[:, :], g["nid_i"][:, 0:1]).then_inc(nid_ready, 1)
            pool.wait_ge(nid_ready, 1)
            own_rows(0)
            with pool.Fori(0, T) as t:
                blocks, before = sizes_of(pool, g, t)
                halves = halves_of(pool, g, t)
                with pool.Fori(0, blocks) as j:
                    n = before + j
                    wait_count(pool, g_free, n + 1, g["pool_turns"])
                    with pool.If((n & 2) < 1):
                        with pool.If((n & 1) < 1):
                            gather(n, 0, halves > 2 * j + 1)
                        with pool.Else():
                            gather(n, 1, halves > 2 * j + 1)
                        pool.sem_inc(g["pool_turns"], 1)
                    with pool.Else():
                        with pool.If((n & 1) < 1):
                            gather(n, 2, halves > 2 * j + 1)
                        with pool.Else():
                            gather(n, 3, halves > 2 * j + 1)
                        pool.sem_inc(g["pool_turns"], 1)
                wait_count(pool, own_in, t * 32 + 32, g["pool_turns"])
                pool.tensor_copy(nidc[:, :], g["nid_i"][:, bass.ds(t + 1, 1)]).then_inc(nid_ready, 1)
                wait_count(pool, tile_done, t + 1, g["pool_turns"])
                wait_count(pool, nid_ready, t + 2, g["pool_turns"])
                with pool.If((t & 1) < 1):
                    own_rows(1)
                with pool.Else():
                    own_rows(0)
            pool.wait_ge(own_in, 32 * (T + 1))

        @block.tensor
        def _(pe):
            whole = pe.alloc_register(f"pe_whole_{s.id}")
            short = pe.alloc_register(f"pe_short_{s.id}")
            pe.reg_mov(whole, 0)
            pe.reg_mov(short, 0)

            def add_pairs(t, n, both):
                for q in range(Q // 2):
                    wait_count(pe, g_in[q], n * PART + PART + 16, g["pe_turns"])
                with pe.If(both):
                    m = pe.snap(whole, min_val=0, max_val=SB * U)
                    for q in range(Q // 2, Q):
                        wait_count(pe, g_in[q], m * PART + PART + 16, g["pe_turns"])
                    pe.reg_add(whole, whole, 1)
                with pe.Else():
                    m = pe.snap(short, min_val=0, max_val=SB * U)
                    wait_count(pe, blank_ready, m * 2 + 2, g["pe_turns"])
                    pe.reg_add(short, short, 1)
                wait_count(pe, z_free, n + 1, g["pe_turns"])
                for i, (k, w) in enumerate(groups):
                    out = g["banks"][:, bass.ds((n & 1) * nb + i, 1), 0:w * wd].squeeze(1)
                    pe.matmul(out, g["ident"][:, :], G[:, bass.ds(n & (RING - 1), 1), k:k + w, :]
                              .rearrange("p a k w -> p (a k w)"), start=True, stop=False)
                    row = own[:, bass.ds(t & 1, 1), 1, :].to_broadcast([P, w, wd])
                    pe.matmul(out, g["ident"][:, :], row, start=False, stop=True).then_inc(z_ready, 1)

            def sum_slots(n):
                wait_count(pe, wgt_ready, n + 1, g["pe_turns"])
                for k in range(B):
                    mm = pe.matmul(bank(g, 7)[:, 0:wd], g["ident"][:, :], wgt[:, k].rearrange("p h c -> p (h c)"),
                                   start=(k == 0), stop=(k == B - 1))
                mm.then_inc(sum_ready, 1)

            pe.wait_ge(own_in, 32)
            add_pairs(0, 0, halves_of(pe, g, 0) > 1)
            with pe.Fori(0, T) as t:
                blocks, before = sizes_of(pe, g, t)
                halves = halves_of(pe, g, t)
                with pe.Fori(0, blocks - 1) as j:
                    add_pairs(t, before + j + 1, halves > 2 * j + 3)
                    sum_slots(before + j)
                with pe.If(t < T - 1):
                    wait_count(pe, own_in, t * 32 + 64, g["pe_turns"])
                    following = nc.s_assert_within(t + 1, 0, T - 1, skip_runtime_bounds_check_because="t < T - 1 here")
                    add_pairs(t + 1, before + blocks, halves_of(pe, g, following) > 1)
                    pe.sem_inc(g["pe_turns"], 1)
                with pe.Else():
                    pe.sem_inc(g["pe_turns"], 1)
                sum_slots(before + blocks - 1)

        @block.vector
        def _(dve):
            for _ in range(RING):
                dve.sem_inc(g_free, 1)
            dve.sem_inc(tile_done, 1)
            for _ in range(D_STEPS):
                dve.sem_inc(sum_steps, 1)
            dve.sem_inc(sum_ready, 1)
            dve.sem_inc(res_out, 1)
            for _ in range(2):
                dve.sem_inc(z_free, 1)
            dve.wait_ge(consts_in, 32)
            st = Steps(dve, c_steps)
            st.after(dve.tensor_scalar(arow[:, :], arow[:, :], 0.8, None, ALU.mult))
            m, mn, bm, rd, kept_scale = (sm[:, i, :] for i in range(5))
            st.after(dve.memset(wgt[:, B, :, chans], 1.0))
            num_rows = num[:, :, 0:chans]

            def zsum(n, i, w):
                return g["banks"][:, bass.ds((n & 1) * nb + i, w), :]

            def add_block(done, scale):
                sd = Steps(dve, sum_steps, done * D_STEPS)
                sd.after(dve.tensor_tensor(num[:, :, :], num[:, :, :], free_bcast(scale, 0, chans + 1), ALU.mult))
                dve.wait_ge(sum_ready, done + 1)
                sd.after(dve.tensor_tensor(num[:, :, :], num[:, :, :],
                                           bank(g, 7)[:, 0:wd].rearrange("p (h c) -> p h c", h=heads), ALU.add))
                assert sd.n == D_STEPS

            def weigh(n, done=None):
                sb = Steps(dve, block_steps, n * B_STEPS)
                for i, (k, w) in enumerate(groups):
                    dve.wait_ge(z_ready, n * nb + i + 1)
                    zs = zsum(n, i, 1)[:, :, 0:w * wd].rearrange("p i (k w) -> p (i k) w", k=w)
                    sb.mark(dve.scalar_tensor_tensor(out=z[:, k:k + w, :], in0=zs[:, :, 0:hc], scalar=0.0,
                                                     in1=free_bcast(arow[:, :], w, 0), op0=ALU.max, op1=ALU.mult))
                sb.wait()
                sb.after(dve.tensor_reduce(lg[:, :, :], z[:, :, :].rearrange("p k (h c) -> p k h c", c=chans), AX.X,
                                           ALU.add))
                for i, w, slots in runs:
                    k0, k1 = i * gs, i * gs + w * slots
                    zs = zsum(n, i, w)[:, :, 0:slots * wd].rearrange("p i (k w) -> p i k w", k=slots)
                    lk = lg[:, k0:k1, :].rearrange("p (i k) h -> p i k h", i=w)
                    sb.mark(dve.tensor_tensor(lk, lk, zs[:, :, :, hc:wd], ALU.add))
                sb.wait()
                dve.sem_inc(z_free, 1)
                sb.after(dve.tensor_reduce(bm, lg[:, :, :].rearrange("p k h -> p h k"), AX.X, ALU.max))
                sb.mark(dve.tensor_copy(kept_scale, wgt[:, B, :, chans]))
                sb.after(dve.tensor_tensor(mn, m, bm, ALU.max))
                sb.mark(dve.tensor_tensor(ex[:, 0:B, :], lg[:, :, :], free_bcast(mn, B, 0), ALU.subtract))
                sb.after(dve.tensor_tensor(ex[:, B, :], m, mn, ALU.subtract))
                dve.sem_inc(ex_ready, 1)
                sb.mark(dve.tensor_copy(m, mn))
                if done is not None:
                    add_block(done, kept_scale)
                dve.wait_ge(ex_done, n + 1)
                Gn = G[:, bass.ds(n & (RING - 1), 1), :, 0:hc].rearrange("p a k (h c) -> p (a k) h c", h=heads)
                sb.after(dve.tensor_tensor(wgt[:, 0:B, :, 0:chans], Gn, free_bcast(wgt[:, 0:B, :, chans], 0, chans),
                                           ALU.mult))
                dve.sem_inc(g_free, 1)
                dve.sem_inc(wgt_ready, 1)
                assert sb.n == B_STEPS, sb.n

            tile_blocks, blocks_done = (dve.alloc_register(f"{n}_{s.id}") for n in ("tile_blocks", "blocks_done"))
            dve.reg_mov(tile_blocks, dve.value_load(g["info"][0:1, 0, 0:1], min_val=1, max_val=SB * U))
            dve.reg_mov(blocks_done, 0)
            with dve.Fori(0, T) as t:
                st = Steps(dve, tile_steps, t * T_STEPS)
                blocks = dve.snap(tile_blocks, min_val=1, max_val=SB * U)
                before = dve.snap(blocks_done, min_val=0, max_val=SB * U)
                dve.wait_ge(own_in, t * 32 + 32)
                own_l, own_r = (own[:, bass.ds(t & 1, 1), i, :].rearrange("p a w -> p (a w)") for i in range(2))
                st.mark(dve.tensor_tensor(zo[:, :], own_l, own_r, ALU.add))
                st.mark(dve.tensor_copy(num_rows, own_l[:, 0:hc].rearrange("p (h c) -> p h c", c=chans)))
                st.after(dve.memset(num[:, :, chans], 1.0))
                st.after(dve.scalar_tensor_tensor(out=z[:, 0, :], in0=zo[:, 0:hc], scalar=0.0, in1=arow[:, :],
                                                  op0=ALU.max, op1=ALU.mult))
                st.after(dve.tensor_reduce(m, z[:, 0, :].rearrange("p (h c) -> p h c", c=chans), AX.X, ALU.add))
                st.after(dve.tensor_tensor(m, m, zo[:, hc:], ALU.add))
                weigh(before)
                dve.sem_inc(g["v_turns"], 1)
                with dve.Fori(0, blocks - 1) as j:
                    weigh(before + j + 1, before + j + 1)
                dve.sem_inc(g["v_turns"], 1)
                with dve.If(t < T - 1):
                    following = nc.s_assert_within(t + 1, 0, T - 1, skip_runtime_bounds_check_because="t < T - 1 here")
                    dve.reg_mov(tile_blocks, dve.value_load(g["info"][0:1, 0, bass.ds(following, 1)], min_val=1,
                                                            max_val=SB * U))
                with dve.Else():
                    dve.sem_inc(g["v_turns"], 1)
                dve.reg_add(blocks_done, blocks_done, blocks)
                add_block(before + blocks, wgt[:, B, :, chans])
                dve.sem_inc(tile_done, 1)
                st.after(dve.reciprocal(rd, num[:, :, chans]))
                dve.wait_ge(res_out, t * 16 + 1)
                st.after(dve.tensor_tensor(res[:, :].rearrange("p (h c) -> p h c", c=chans), num_rows,
                                           free_bcast(rd, 0, chans), ALU.mult))
                st.after(dve.tensor_tensor(res[:, :], res[:, :], brow[:, :], ALU.add))
                dve.sem_inc(res_ready, 1)
                assert st.n == T_STEPS, st.n

        @block.scalar
        def _(act):
            with act.Fori(0, T) as t:
                blocks, before = sizes_of(act, g, t)
                with act.Fori(0, blocks) as j:
                    act.wait_ge(ex_ready, before + j + 1)
                    act.wait_ge(sum_ready, before + j + 1)
                    act.activation(wgt[:, :, :, chans], ex[:, :, :], ACT.Exp).then_inc(ex_done, 1)
                wait_count(act, res_ready, t + 1, g["act_turns"])
                act.dma_start(result[bass.ds(t * P, P), :], res[:, :]).then_inc(res_out, 16)
            act.wait_ge(res_out, 16 * T + 1)


def add_rows(nc, g, rows):
    with ExitStack() as ctx:
        s = Scope(nc, ctx)
        added = s.sem("added")
        block = ctx.enter_context(nc.Block())

        @block.vector
        def _(dve):
            dve.tensor_tensor(g["X"][:, :, :], g["X"][:, :, :], rows[:, :, :], ALU.add).then_inc(added, 1)


def pair_softmax(nc, g):
    with ExitStack() as outer:
        so = Scope(nc, outer)
        rin = so.sb("rin", [P, T])
        outT = so.sb("outT", [D, NP])
        with ExitStack() as ctx:
            s = Scope(nc, ctx)
            rows = [s.sb(f"prow{b}", [P, NP, 2]) for b in range(2)]
            wt = [s.sb(f"pwt{b}", [P, NP]) for b in range(2)]
            hs = [s.sb(f"phs{b}", [P, D]) for b in range(2)]
            minrow = s.sb("minrow", [P, NP])
            ms = s.sb("ms", [P, T, 2])
            hmin = s.sb("hmin", [P, T])
            hout = s.sb("hout", [P, T])
            bias_c = [s.sb(f"bias_c{b}", [P, 1]) for b in range(2)]
            st4 = s.sb("ps_st", [P, 3, 2 * T])
            zero_b = s.sb("pz", [P, 512], BF16)
            pt = [bank(g, c) for c in range(7)]
            turn = bank(g, 7)
            ms_in, root_in, root_out, v_steps = s.sem("ms_in"), s.sem("pr_in"), s.sem("pr_out"), s.sem("ps_steps")
            turned, copied, ready = s.sem("turned"), s.sem("copied"), s.sem("ready")
            rows_in, wt_ready, wt_exp, wt_free = [[s.sem(f"{n}{i}") for i in range(2)] for n in
                                                  ("prow_in", "wt_ready", "wt_exp", "wt_free")]
            tile_steps = s.sem("pt_steps")
            all_done = s.sem("all_done")
            block = ctx.enter_context(nc.Block())
            pairs = g["PAIR"].rearrange("(t p d) c -> t p (d c)", t=T, p=P)
            widths = [512] * (NP // 512) + [NP % 512]

            def tiles(eng, tile):
                with eng.Fori(0, T // 2) as i:
                    tile(2 * i, 0, i)
                    tile(2 * i + 1, 1, i)
                tile(T - 1, 0, T // 2)

            @block.sync
            def _(sp):
                sp.dma_start(ms[:, :, :], g["MS"].rearrange("(t p) c -> p t c", p=P)).then_inc(ms_in, 16)

                def tile(t, b, i):
                    wait_count(sp, wt_ready[b], i + 1, g["sp_turns"])
                    sp.dma_start(rows[b][:, :, :].rearrange("p d c -> p (d c)"), pairs[bass.ds(t, 1)].squeeze(0),
                                 max_dma_last_dim=8192).then_inc(rows_in[b], 16)
                tiles(sp, tile)

            @block.vector
            def _(dve):
                st = Steps(dve, v_steps)
                for b in range(2):
                    dve.sem_inc(wt_ready[b], 1)
                dve.wait_ge(ms_in, 16)
                st.after(dve.tensor_scalar(hmin[:, :], ms[:, :, 0], -0.1 * BIG, 0.5, ALU.max, ALU.mult))
                dve.sem_inc(ready, 1)
                st.mark(dve.memset(zero_b[:, :], 0.0))
                st.mark(dve.tensor_scalar(hout[:, :], g["mout"][:, :], -0.5, None, ALU.mult))
                st.mark(dve.tensor_copy(st4[:, 0, 0:T], ms[:, :, 1]))
                st.after(dve.tensor_copy(st4[:, 0, T:], g["sout"][:, :]))
                dve.sem_inc(root_in, 1)
                dve.wait_ge(root_out, 1)
                st.after(dve.reciprocal(st4[:, 2, :], st4[:, 1, :]))
                st.after(dve.tensor_tensor(st4[:, 1, :], st4[:, 2, :], st4[:, 2, :], ALU.mult))
                st.after(dve.tensor_tensor(st4[:, 1, :], st4[:, 1, :], st4[:, 0, :], ALU.mult))
                st.after(dve.tensor_scalar(st4[:, 1, :], st4[:, 1, :], -0.5, 1.5, ALU.mult, ALU.add))
                st.after(dve.tensor_tensor(st4[:, 2, :], st4[:, 2, :], st4[:, 1, :], ALU.mult))
                st.mark(dve.tensor_copy(rin[:, :], st4[:, 2, 0:T]))
                st.after(dve.tensor_tensor(g["H"][:, :, :], g["H"][:, :, :], free_bcast(st4[:, 2, T:], 0, D), ALU.mult))
                dve.sem_inc(ready, 1)
                dve.wait_ge(copied, -(-T // 4))

                def tile(t, b, i):
                    st = Steps(dve, tile_steps, t * 3)
                    dve.wait_ge(rows_in[b], i * 16 + 16)
                    dve.wait_ge(wt_free[b], i + 1)
                    st.mark(dve.tensor_copy(hs[b][:, :], g["H"][:, bass.ds(t, 1), :].squeeze(1)))
                    st.mark(dve.tensor_copy(bias_c[b][:, :], hout[:, bass.ds(t, 1)]))
                    st.after(dve.tensor_tensor(wt[b][:, :], rows[b][:, :, 1], minrow[:, :], ALU.subtract))
                    dve.sem_inc(wt_ready[b], 1)
                tiles(dve, tile)
                dve.wait_ge(all_done, 1)
                off = 0
                for c, w in enumerate(widths):
                    dve.tensor_copy(outT[:, off:off + w], pt[c][0:D, 0:w]).then_inc(v_steps, 1)
                    off += w

            @block.scalar
            def _(act):
                act.wait_ge(root_in, 1)
                act.activation(st4[:, 1, :], st4[:, 0, :], ACT.Sqrt).then_inc(root_out, 1)
                for j in range(-(-T // 4)):
                    act.wait_ge(turned, j + 1)
                    w = min(4, T - 4 * j) * P
                    act.copy(minrow[:, 4 * j * P:4 * j * P + w], turn[:, 0:w]).then_inc(copied, 1)

                def tile(t, b, i):
                    act.wait_ge(wt_ready[b], i + 2)
                    act.activation(wt[b][:, :], wt[b][:, :], ACT.Exp, bias=bias_c[b][:, 0:1]).then_inc(wt_exp[b], 1)
                tiles(act, tile)

            @block.tensor
            def _(pe):
                pe.wait_ge(ready, 1)
                for t in range(T):
                    if t and t % 4 == 0:
                        pe.wait_ge(copied, t // 4)
                    mm = pe.transpose(turn[:, (t % 4) * P:(t % 4 + 1) * P], hmin[:, t:t + 1].to_broadcast([P, P]),
                                      g["ident"][:, :])
                    if t % 4 == 3 or t == T - 1:
                        mm.then_inc(turned, 1)
                pe.wait_ge(ready, 2)
                for b in range(2):
                    pe.sem_inc(wt_free[b], 1)
                for c, w in enumerate(widths):
                    pe.matmul(pt[c][0:D, 0:w], zero_b[:, 0:D], zero_b[:, 0:w], start=True, stop=False,
                              skip_group_check=True)

                def tile(t, b, i):
                    pe.wait_ge(wt_exp[b], i + 1)
                    off = 0
                    for c, w in enumerate(widths):
                        mm = pe.matmul(pt[c][0:D, 0:w], hs[b][:, :], wt[b][:, off:off + w], start=False, stop=False,
                                       skip_group_check=True)
                        off += w
                    mm.then_inc(wt_free[b], 1)
                tiles(pe, tile)
                for c, w in enumerate(widths):
                    mm = pe.matmul(pt[c][0:D, 0:w], zero_b[:, 0:D], zero_b[:, 0:w], start=False, stop=True,
                                   skip_group_check=True)
                mm.then_inc(all_done, 1)

        with ExitStack() as ctx:
            s = Scope(nc, ctx)
            back = [bank(g, i).rearrange("p (t f) -> p t f", f=D) for i in range(4)]
            tmp = s.sb("ps_tmp", [P, T, D])
            turned, v_steps = s.sem("turned_back"), s.sem("psb_steps")
            block = ctx.enter_context(nc.Block())

            @block.tensor
            def _(pe):
                for t in range(T):
                    pe.transpose(back[t // 8][:, t % 8, :], outT[:, t * P:(t + 1) * P],
                                 g["ident"][0:D, 0:D]).then_inc(turned, 1)

            @block.vector
            def _(dve):
                st = Steps(dve, v_steps)
                for j in range(4):
                    a, b = 8 * j, min(8 * j + 8, T)
                    dve.wait_ge(turned, b)
                    st.after(dve.tensor_tensor(tmp[:, a:b, :], back[j][:, 0:b - a, :],
                                               free_bcast(rin[:, a:b], 0, D), ALU.mult))
                st.after(dve.tensor_tensor(g["X"][:, :, :], g["X"][:, :, :], tmp[:, :, :], ALU.add))


def store_rows(nc, g, table):
    with ExitStack() as ctx:
        s = Scope(nc, ctx)
        none = s.sb("f_none", [1, D])
        out, none_ready = s.sem("stored"), s.sem("f_none_ready")
        block = ctx.enter_context(nc.Block())

        @block.vector
        def _(dve):
            dve.memset(none[:, :], -BIG).then_inc(none_ready, 1)

        @block.sync
        def _(sp):
            sp.dma_start(table[0:NP, :].rearrange("(t p) f -> p t f", p=P), g["H"][:, :, :]).then_inc(out, 16)
            sp.wait_ge(none_ready, 1)
            sp.dma_start(table[NO_ROW:NO_ROW + 1, :], none[:, :]).then_inc(out, 16)
            sp.wait_ge(out, 32)


def edge_sums(nc, g, table, result):
    with ExitStack() as ctx:
        s = Scope(nc, ctx)
        G = s.sb("e_rows", [P, RING, B, D])
        AT = s.sb("e_attr", [P, RING, 2, B * D])
        gi = s.sb("e_idx", [P, GB], I32)
        z = s.sb("e_z", [P, B, D])
        acc = s.sb("e_acc", [P, D])
        part = s.sb("e_part", [P, D])
        res = s.sb("e_res", [P, D])
        res_ready, res_out = s.sem("er_ready"), s.sem("er_out")
        g_free = s.sem("e_g_free")
        attr_in = s.sem("attr_in")
        blank_ready = s.sem("e_blank_ready")
        idx_in, g_in = [[s.sem(f"{n}{q}") for q in range(Q)] for n in ("e_idx_in", "e_g_in")]
        tile_steps, block_steps = s.sem("et_steps"), s.sem("eb_steps")
        block = ctx.enter_context(nc.Block())
        T_STEPS, B_STEPS = 2, 4
        PART = BQ * 16

        @block.sync
        def _(sp):
            whole = sp.alloc_register(f"sp_whole_{s.id}")
            sp.reg_mov(whole, 0)
            runs = sp.alloc_register(f"sp_runs_{s.id}")
            sp.reg_mov(runs, 0)

            def load_part(q, base, j, n):
                wait_count(sp, g_in[q], n * PART + 16, g["sp_turns"])
                a, w = (1 + q * BQ, BQ) if q else (0, 1 + BQ)
                sp.dma_start(gi[:, a:a + w], g["GIDX"][:, bass.ds(block_column(nc, base, j) + a, w)])\
                    .then_inc(idx_in[q], 16)

            with sp.Fori(0, T) as t:
                halves = halves_of(sp, g, t)
                blocks, before = sizes_of(sp, g, t)
                base = sp.value_load(g["info"][0:1, 3, bass.ds(t, 1)], min_val=0, max_val=U)
                with sp.Fori(0, blocks) as j:
                    wait_count(sp, attr_in, sp.snap(runs, min_val=0, max_val=SB * U) * 16 + 16, g["sp_turns"])
                    for q in range(Q // 2):
                        load_part(q, base, j, before + j)
                    with sp.If((j & 1) < 1):
                        sp.reg_add(runs, runs, 1)
                    with sp.Else():
                        sp.sem_inc(g["sp_turns"], 1)
                    with sp.If(halves > 2 * j + 1):
                        n = sp.snap(whole, min_val=0, max_val=SB * U)
                        for q in range(Q // 2, Q):
                            load_part(q, base, j, n)
                        sp.reg_add(whole, whole, 1)
                    with sp.Else():
                        sp.sem_inc(g["sp_turns"], 1)

        @block.gpsimd
        def _(pool):
            whole = pool.alloc_register(f"pool_whole_{s.id}")
            pool.reg_mov(whole, 0)

            def gather_part(q, n, k):
                wait_count(pool, idx_in[q], n * 16 + 16, g["pool_turns"])
                for c in range(q * BQ, (q + 1) * BQ):
                    at = bass.IndirectOffsetOnAxis(ap=gi[:, 1 + c:2 + c], axis=0)
                    pool.indirect_dma_start(G[:, k, c, :], None, table, at).then_inc(g_in[q], 16)

            def gather_run(k):
                at = bass.IndirectOffsetOnAxis(ap=gi[:, 0:1], axis=0)
                pool.indirect_dma_start(AT[:, k].rearrange("p b w -> p (b w)"), None, g["edge_attr_64"], at)\
                    .then_inc(attr_in, 16)

            def gather(n, k, both):
                for q in range(Q // 2):
                    gather_part(q, n, k)
                with pool.If(both):
                    m = pool.snap(whole, min_val=0, max_val=SB * U)
                    for q in range(Q // 2, Q):
                        gather_part(q, m, k)
                    pool.reg_add(whole, whole, 1)
                with pool.Else():
                    pool.memset(G[:, k, HB:B, :], -BIG).then_inc(blank_ready, 1)
                pool.sem_inc(g["pool_turns"], 1)

            for q in range(Q):
                at = bass.IndirectOffsetOnAxis(ap=g["nid_i"][:, 0:1], axis=0)
                pool.indirect_dma_start(G[:, RING - 1, q, :], None, table, at).then_inc(g_in[q], 16)
            at = bass.IndirectOffsetOnAxis(ap=g["nid_i"][:, 0:1], axis=0)
            pool.indirect_dma_start(AT[:, RING - 1, 0, 0:D], None, table, at).then_inc(attr_in, 16)
            runs = pool.alloc_register(f"pool_runs_{s.id}")
            pool.reg_mov(runs, 0)
            with pool.Fori(0, T) as t:
                blocks, before = sizes_of(pool, g, t)
                halves = halves_of(pool, g, t)
                with pool.Fori(0, blocks) as j:
                    n = before + j
                    wait_count(pool, g_free, n + 1, g["pool_turns"])
                    with pool.If((j & 1) < 1):
                        u = pool.snap(runs, min_val=0, max_val=SB * U)
                        wait_count(pool, idx_in[0], n * 16 + 16, g["pool_turns"])
                        wait_count(pool, attr_in, u * 16 + 16, g["pool_turns"])
                        with pool.If((u & 2) < 1):
                            with pool.If((u & 1) < 1):
                                gather_run(0)
                            with pool.Else():
                                gather_run(1)
                            pool.sem_inc(g["pool_turns"], 1)
                        with pool.Else():
                            with pool.If((u & 1) < 1):
                                gather_run(2)
                            with pool.Else():
                                gather_run(3)
                            pool.sem_inc(g["pool_turns"], 1)
                        pool.reg_add(runs, runs, 1)
                    with pool.Else():
                        pool.sem_inc(g["pool_turns"], 1)
                    with pool.If((n & 2) < 1):
                        with pool.If((n & 1) < 1):
                            gather(n, 0, halves > 2 * j + 1)
                        with pool.Else():
                            gather(n, 1, halves > 2 * j + 1)
                        pool.sem_inc(g["pool_turns"], 1)
                    with pool.Else():
                        with pool.If((n & 1) < 1):
                            gather(n, 2, halves > 2 * j + 1)
                        with pool.Else():
                            gather(n, 3, halves > 2 * j + 1)
                        pool.sem_inc(g["pool_turns"], 1)

        @block.vector
        def _(dve):
            whole = dve.alloc_register(f"v_whole_{s.id}")
            short = dve.alloc_register(f"v_short_{s.id}")
            dve.reg_mov(whole, 0)
            dve.reg_mov(short, 0)
            runs = dve.alloc_register(f"v_runs_{s.id}")
            dve.reg_mov(runs, 0)
            for _ in range(RING):
                dve.sem_inc(g_free, 1)
            dve.sem_inc(res_out, 1)
            with dve.Fori(0, T) as t:
                st = Steps(dve, tile_steps, t * T_STEPS)
                st.after(dve.memset(acc[:, :], 0.0))
                blocks, before = sizes_of(dve, g, t)
                halves = halves_of(dve, g, t)
                with dve.Fori(0, blocks) as j:
                    n = before + j
                    sb = Steps(dve, block_steps, n * B_STEPS)
                    Gn = G[:, bass.ds(n & (RING - 1), 1)].rearrange("p a k w -> p (a k) w")
                    with dve.If((j & 1) < 1):
                        dve.reg_add(runs, runs, 1)
                    with dve.Else():
                        dve.sem_inc(g["v_turns"], 1)
                    u = dve.snap(runs, min_val=0, max_val=SB * U)
                    wait_count(dve, attr_in, u * 16 + 16, g["v_turns"])
                    An = AT[:, bass.ds((u + RING - 1) & (RING - 1), 1), bass.ds(j & 1, 1), :]\
                        .rearrange("p a b (k w) -> p (a b k) w", w=D)
                    for q in range(Q // 2):
                        wait_count(dve, g_in[q], (n + 1) * PART + 16, g["v_turns"])
                    with dve.If(halves > 2 * j + 1):
                        m = dve.snap(whole, min_val=0, max_val=SB * U)
                        for q in range(Q // 2, Q):
                            wait_count(dve, g_in[q], (m + 1) * PART + 16, g["v_turns"])
                        dve.reg_add(whole, whole, 1)
                    with dve.Else():
                        m = dve.snap(short, min_val=0, max_val=SB * U)
                        wait_count(dve, blank_ready, m + 1, g["v_turns"])
                        dve.reg_add(short, short, 1)
                    sb.after(dve.tensor_tensor(z[:, :, :], Gn, An, ALU.add))
                    dve.sem_inc(g_free, 1)
                    sb.after(dve.tensor_scalar(z[:, :, :], z[:, :, :], 0.0, None, ALU.max))
                    sb.after(dve.tensor_reduce(part[:, :], z[:, :, :].rearrange("p k w -> p w k"), AX.X, ALU.add))
                    sb.after(dve.tensor_tensor(acc[:, :], acc[:, :], part[:, :], ALU.add))
                    assert sb.n == B_STEPS, sb.n
                dve.wait_ge(res_out, t * 16 + 1)
                st.after(dve.tensor_copy(res[:, :], acc[:, :]))
                dve.sem_inc(res_ready, 1)
                assert st.n == T_STEPS, st.n

        @block.scalar
        def _(act):
            with act.Fori(0, T) as t:
                wait_count(act, res_ready, t + 1, g["act_turns"])
                act.dma_start(result[bass.ds(t * P, P), :], res[:, :]).then_inc(res_out, 16)
            act.wait_ge(res_out, 16 * T + 1)


def output_layer(nc, g, rows):
    with ExitStack() as ctx:
        s = Scope(nc, ctx)
        w = s.sb("ow", [D, D])
        brow = s.sb("obrow", [P, D])
        eps = s.sb("oeps", [P, 1])
        xt = s.sb("oxt", [P, GT, D])
        xT = s.sb("oxT", [D, GT, P])
        y = s.sb("oy", [P, GT, D])
        turned = bank(g, 0).rearrange("p (t n) -> p t n", n=P)
        product = bank(g, 1)[:, 0:GT * D].rearrange("p (t f) -> p t f", f=D)
        w_in, comb_ready, x_ready, x_turned = s.sem("ow_in"), s.sem("comb_ready"), s.sem("ox_ready"), s.sem("ox_turned")
        xT_ready, projected, mp_free, v_steps = s.sem("oxT_ready"), s.sem("oprojected"), s.sem("omp_free"), s.sem("o_steps")
        out_done, x_done = s.sem("out_done"), s.sem("x_done")
        block = ctx.enter_context(nc.Block())
        full = N // P

        def groups(eng, body):
            with eng.Fori(0, T // GT) as i:
                body(i, i * GT, GT)
            body(T // GT, T // GT * GT, T % GT)

        @block.sync
        def _(sp):
            sp.dma_start(w[:, :], g["L3_gnn_W_T"]).then_inc(w_in, 16)
            sp.dma_start(brow[:, :], g["L3_gnn_b"].partition_broadcast(P)).then_inc(w_in, 16)
            sp.dma_start(eps[:, :], g["L3_gnn_eps"].partition_broadcast(P)).then_inc(w_in, 16)
            sp.wait_ge(x_done, 1)
            sp.dma_start(g["out"][0:full * P, :].rearrange("(t p) f -> p t f", p=P),
                         g["X"][:, 0:full, :]).then_inc(out_done, 16)
            sp.dma_start(g["out"][full * P:N, :], g["X"][0:N - full * P, full, :]).then_inc(out_done, 16)
            sp.wait_ge(out_done, 32)

        @block.scalar
        def _(act):
            act.wait_ge(comb_ready, 1)

            def body(i, t0, tiles):
                act.copy(xt[:, 0:tiles, :], g["H"][:, bass.ds(t0, tiles), :]).then_inc(x_ready, 1)
                act.wait_ge(x_turned, i + 1)
                act.copy(xT[:, 0:tiles, :], turned[0:D, 0:tiles, :]).then_inc(xT_ready, 1)
            groups(act, body)

        @block.tensor
        def _(pe):
            pe.wait_ge(w_in, 48)

            def body(i, t0, tiles):
                wait_count(pe, x_ready, i + 1, g["pe_turns"])
                for t in range(tiles):
                    mm = pe.transpose(turned[0:D, t, :], xt[:, t, :], g["ident"][:, :])
                mm.then_inc(x_turned, 1)
                pe.wait_ge(mp_free, i + 1)
                pe.wait_ge(xT_ready, i + 1)
                for t in range(tiles):
                    mm = pe.matmul(product[:, t, :], xT[:, t, :], w[:, :], start=True, stop=True)
                mm.then_inc(projected, 1)
            groups(pe, body)

        @block.vector
        def _(dve):
            st = Steps(dve, v_steps)
            dve.wait_ge(w_in, 48)
            st.after(dve.tensor_scalar(eps[:, :], eps[:, :], 1.0, None, ALU.add))
            H = g["H"][:, :, :].rearrange("p t f -> p (t f)")
            st.after(dve.scalar_tensor_tensor(out=H, in0=H, scalar=eps[:, 0:1],
                                              in1=rows[:, :, :].rearrange("p t f -> p (t f)"), op0=ALU.mult,
                                              op1=ALU.add))
            dve.sem_inc(comb_ready, 1)
            dve.sem_inc(mp_free, 1)
            first = st.n

            def body(i, t0, tiles):
                st = Steps(dve, v_steps, first + 3 * i)
                dve.wait_ge(projected, i + 1)
                st.after(dve.tensor_tensor(y[:, 0:tiles, :], product[:, 0:tiles, :], free_bcast(brow[:, :], tiles, 0),
                                           ALU.add))
                dve.sem_inc(mp_free, 1)
                st.after(dve.tensor_scalar(y[:, 0:tiles, :], y[:, 0:tiles, :], 0.0, None, ALU.max))
                xs = g["X"][:, bass.ds(t0, tiles), :]
                st.after(dve.tensor_tensor(xs, xs, y[:, 0:tiles, :], ALU.add))
            groups(dve, body)
            dve.sem_inc(x_done, 1)


def build(nc, io):
    with ExitStack() as ctx:
        g = persistent(nc, ctx, io)
        s = Scope(nc, ctx)
        with nc.sbuf_tensor("fill", [P, NP, 2], F32) as fill:
            prepare(nc, g, fill)
            fill_slots(nc, g)
        scatter_pairs(nc, g)
        with ExitStack() as dense:
            g["A"] = dense.enter_context(nc.sbuf_tensor("A", [P, T, NP], BF16))
            read_pairs(nc, g)
            normalise(nc, g, first=True)
            aggregate(nc, g, g["L0_gnn_W_ssg"], g["L0_gnn_b_ssg"], own_degree=True, scale=0.5)
            tabs = [s.dram(f"TAB{i}", [NP + 1, w]) for i, w in enumerate((HC + H1, HC + H1, D + 1, D + 1))]
            heads1, heads2 = s.dram("HEADS1", [NP, HC]), s.dram("HEADS2", [NP, D])
            attention_tables(nc, g, g["H"], D, H1, C1, *[g[f"L0_gnn_{n}"] for n in ("W1l", "b1l", "W1r", "b1r", "att1")],
                             tabs[0], tabs[1])
            attend(nc, g, H1, C1, g["L0_gnn_att1"], g["L0_gnn_bias1"], tabs[0], tabs[1], heads1)
            with ExitStack() as c2:
                rows = c2.enter_context(nc.sbuf_tensor("heads_rows", [P, T, HC], F32))
                bring_rows(nc, g, heads1, rows, HC)
                attention_tables(nc, g, rows, HC, 1, D, *[g[f"L0_gnn_{n}"] for n in ("W2l", "b2l", "W2r", "b2r", "att2")],
                                 tabs[2], tabs[3])
            attend(nc, g, 1, D, g["L0_gnn_att2"], g["L0_gnn_bias2"], tabs[2], tabs[3], heads2)
            bring_rows(nc, g, heads2, g["H"], D)
            add_rows(nc, g, g["H"])
            normalise(nc, g)
            aggregate(nc, g, g["L1_gnn_W1"], g["L1_gnn_b1"], relu=True)
            aggregate(nc, g, g["L1_gnn_W2"], g["L1_gnn_b2"], relu=True)
            aggregate(nc, g, g["L1_gnn_W3"], g["L1_gnn_b3"], add_to_x=True)
        normalise(nc, g)
        pair_softmax(nc, g)
        normalise(nc, g)
        features, sums = s.dram("FEATURES", [NP + 1, D]), s.dram("SUMS", [NP, D])
        store_rows(nc, g, features)
        edge_sums(nc, g, features, sums)
        with ExitStack() as c3:
            rows = c3.enter_context(nc.sbuf_tensor("sum_rows", [P, T, D], F32))
            bring_rows(nc, g, sums, rows, D)
            output_layer(nc, g, rows)


def kernel(**inputs):
    import numpy as np
    import concourse.bacc as bacc
    from concourse.bass_utils import run_bass_kernel_spmd

    def padded(name, rows, value=0):
        a = np.asarray(inputs[name])
        out = np.full((rows,) + a.shape[1:], value, a.dtype)
        out[:a.shape[0]] = a
        return out

    arrays = {"x": padded("x", NP), "src": padded("src", ER), "dst": padded("dst", ER, NO_NODE),
              "edge_weight": padded("edge_weight", ER), "edge_attr_64": padded("edge_attr_64", ER)}
    for name in inputs:
        if name.startswith("L"):
            arrays[name] = np.ascontiguousarray(np.asarray(inputs[name]))
    arrays["L3_gnn_eps"] = arrays["L3_gnn_eps"].reshape(1)
    arrays["L3_gnn_W_T"] = np.ascontiguousarray(arrays.pop("L3_gnn_W").T)
    nc = bacc.Bacc("TRN2", target_bir_lowering=False, num_devices=1)
    io = {k: nc.dram_tensor(f"in_{k}", a.shape, mybir.dt.from_np(a.dtype), kind="ExternalInput").ap()
          for k, a in arrays.items()}
    io["out"] = nc.dram_tensor("out_x", (N, D), F32, kind="ExternalOutput").ap()
    build(nc, io)
    r = run_bass_kernel_spmd(nc, [{f"in_{k}": a for k, a in arrays.items()}], core_ids=[0])
    return r.results[0]["out_x"]
```
